# Optimizing a Trainium2 kernel written in Bass

```python
import numpy as np
import jax
import jax.numpy as jnp

def _softmax(x, axis=-1):
    return jax.nn.softmax(x, axis=axis)

def _gelu(x):
    return jax.nn.gelu(x, approximate=True)

def _silu(x):
    return jax.nn.silu(x)

def _sigmoid(x):
    return jax.nn.sigmoid(x)

def _layernorm(x, axis=-1, eps=1e-05):
    m = jnp.mean(x, axis=axis, keepdims=True)
    v = jnp.var(x, axis=axis, keepdims=True)
    return (x - m) / jnp.sqrt(v + eps)

def _scatter_add(tgt, idx, src, axis=0):
    return tgt.at[idx].add(src)

def _segment_sum(src, seg, n):
    return jax.ops.segment_sum(src, seg, n)
kernel_name = 'mk_vit_tower_d1_tok_img768_r4_c86105'

def setup_inputs(seed: int=0):
    np.random.seed(seed)
    _w = jnp.asarray

    def _rec_inputs():
        import jax
        import jax.numpy as jnp
        _rk = jax.random.key(seed)
        x = -0.000596345 + 1.00056 * jax.random.normal(jax.random.fold_in(_rk, 1), (16, 3, 64, 64), jnp.float32)
        return x
    x = _rec_inputs()

    def _L0_tok_setup():
        import jax, jax.numpy as jnp
        import numpy as np
        B = 16
        IMG = 64
        CH = 3
        EMBED = 64
        GP = 16
        PRE = [1, 2, 4]
        N_LEVELS = 3
        FUSED = EMBED * N_LEVELS

        def hilbert_flat_indices(n):
            t = np.arange(n * n, dtype=np.int64)
            x = np.zeros(n * n, dtype=np.int64)
            y = np.zeros(n * n, dtype=np.int64)
            s = 1
            while s < n:
                rx = 1 & t // 2
                ry = 1 & (t ^ rx)
                swap = ry == 0
                flip = swap & (rx == 1)
                x = np.where(flip, s - 1 - x, x)
                y = np.where(flip, s - 1 - y, y)
                x2 = np.where(swap, y, x)
                y2 = np.where(swap, x, y)
                x, y = (x2, y2)
                x = x + s * rx
                y = y + s * ry
                t = t // 4
                s *= 2
            return y * n + x

        def _level(x, idx, W, b, p, gp):
            Bsz, C, H, _ = x.shape
            h = H // p
            t = x.reshape(Bsz, C, h, p, h, p).transpose(0, 2, 4, 3, 5, 1).reshape(Bsz, h * h, p * p * C)
            t = t[:, idx]
            t = t.reshape(Bsz, h * h // gp, gp * p * p * C)
            return t @ W.T + b

        def _interp_linear(x, n_out):
            L = x.shape[1]
            pos = (jnp.arange(n_out, dtype=jnp.float32) + 0.5) * (L / n_out) - 0.5
            pos = jnp.clip(pos, 0.0, L - 1)
            i0 = jnp.floor(pos).astype(jnp.int32)
            i1 = jnp.minimum(i0 + 1, L - 1)
            w = (pos - i0).astype(x.dtype)
            return x[:, i0] * (1.0 - w)[None, :, None] + x[:, i1] * w[None, :, None]
        key = jax.random.key(seed)
        ks = jax.random.split(key, 9)
        inp = {'x': jax.random.normal(ks[0], (B, CH, IMG, IMG), jnp.float32)}
        for i, p in enumerate(PRE):
            din = CH * p * p * GP
            inp[f'W{i}'] = jax.random.normal(ks[1 + 2 * i], (EMBED, din), jnp.float32) * din ** (-0.5)
            inp[f'b{i}'] = jax.random.normal(ks[2 + 2 * i], (EMBED,), jnp.float32) * 0.02
        inp['Wf'] = jax.random.normal(ks[7], (FUSED, FUSED), jnp.float32) * FUSED ** (-0.5)
        inp['bf'] = jax.random.normal(ks[8], (FUSED,), jnp.float32) * 0.02
        for i, p in enumerate(PRE):
            inp[f'idx{i}'] = jnp.asarray(hilbert_flat_indices(IMG // p), jnp.int32)
        return inp
    _L0_tok_all = _L0_tok_setup()
    _L0_tok_in = {k: v for k, v in _L0_tok_all.items() if k in ('W0', 'b0', 'W1', 'b1', 'W2', 'b2', 'Wf', 'bf', 'idx0', 'idx1', 'idx2')}
    del _L0_tok_all

    def _L0_attn_setup():
        import jax, jax.numpy as jnp
        import numpy as np
        EPS = 1e-05
        NUM_HEADS = 12

        def rmsnorm(x, g):
            var = jnp.mean(x * x, axis=-1, keepdims=True)
            return x * jax.lax.rsqrt(var + EPS) * g

        def activation_quant(x):
            scale = 127.0 / jnp.clip(jnp.max(jnp.abs(x), axis=-1, keepdims=True), EPS, None)
            return jnp.clip(jnp.round(x * scale), -128, 127) / scale

        def weight_quant(w):
            scale = 1.0 / jnp.clip(jnp.mean(jnp.abs(w)), EPS, None)
            return jnp.clip(jnp.round(w * scale), -1, 1) / scale

        def bitlinear(x, w, g):
            xn = rmsnorm(x, g)
            xq = xn + jax.lax.stop_gradient(activation_quant(xn) - xn)
            wq = w + jax.lax.stop_gradient(weight_quant(w) - w)
            return jnp.einsum('bnc,oc->bno', xq, wq)
        key = jax.random.key(seed)
        k1, k2, k3 = jax.random.split(key, 3)
        B, N, C = (2, 512, 192)
        return {'x': jax.random.normal(k1, (B, N, C), dtype=jnp.float32), 'w_qkv': jax.random.normal(k2, (3 * C, C), dtype=jnp.float32) * 0.02, 'g_qkv': jnp.ones((C,), dtype=jnp.float32), 'w_proj': jax.random.normal(k3, (C, C), dtype=jnp.float32) * 0.02, 'g_proj': jnp.ones((C,), dtype=jnp.float32)}
    _L0_attn_all = _L0_attn_setup()
    _L0_attn_in = {k: v for k, v in _L0_attn_all.items() if k in ('w_qkv', 'g_qkv', 'w_proj', 'g_proj')}
    del _L0_attn_all

    def _L0_ffn_setup():
        import jax, jax.numpy as jnp
        import numpy as np
        GT0 = [[0, 1, 0, 0, 1, 0], [0, 1, 0, 0, 0, 1], [0, 0, 1, 0, 1, 0], [0, 0, 1, 0, 0, 1], [0, 0, 0, 1, 1, 0], [0, 0, 0, 1, 0, 1]]
        NCLS = 6
        K = 1

        def _expert_pairs():
            pairs = []
            for i in range(NCLS):
                p = [(j - 1, k - 1) for j in range(1, 6) for k in range(1, 6) if j != k and GT0[i][j] == 1 and (GT0[i][k] == 1)]
                pairs.append(p)
            return pairs
        PAIRS = _expert_pairs()
        B, P, D, H = (64, 64, 192, 768)

        def _gelu(t):
            return jax.nn.gelu(t, approximate=False)
        key = jax.random.key(seed)
        ks = jax.random.split(key, 8)
        s = 0.02
        x = jax.random.normal(ks[0], (B, NCLS + P, D), dtype=jnp.float32)
        mids = jax.random.randint(ks[1], (B,), 0, 6)
        moe0_W1 = jax.random.normal(ks[2], (D, H), dtype=jnp.float32) * s
        moe0_b1 = jnp.zeros((H,), jnp.float32)
        moe0_W2 = jax.random.normal(ks[3], (H, D), dtype=jnp.float32) * s
        moe0_b2 = jnp.zeros((D,), jnp.float32)
        A1_W = jax.random.normal(ks[4], (5, D, H), dtype=jnp.float32) * s
        A1_b = jnp.zeros((5, H), jnp.float32)
        A2_W = jax.random.normal(ks[5], (5, H, D), dtype=jnp.float32) * s
        A2_b = jnp.zeros((5, D), jnp.float32)
        G_W = jax.random.normal(ks[6], (NCLS, D, 2), dtype=jnp.float32) * s
        return {'x': x, 'moe0_W1': moe0_W1, 'moe0_b1': moe0_b1, 'moe0_W2': moe0_W2, 'moe0_b2': moe0_b2, 'A1_W': A1_W, 'A1_b': A1_b, 'A2_W': A2_W, 'A2_b': A2_b, 'G_W': G_W, 'mids': mids}
    _L0_ffn_all = _L0_ffn_setup()
    _L0_ffn_in = {k: v for k, v in _L0_ffn_all.items() if k in ('moe0_W1', 'moe0_b1', 'moe0_W2', 'moe0_b2', 'A1_W', 'A1_b', 'A2_W', 'A2_b', 'G_W', 'mids')}
    del _L0_ffn_all
    return {'x': x, 'L0_tok_W0': _L0_tok_in['W0'], 'L0_tok_b0': _L0_tok_in['b0'], 'L0_tok_W1': _L0_tok_in['W1'], 'L0_tok_b1': _L0_tok_in['b1'], 'L0_tok_W2': _L0_tok_in['W2'], 'L0_tok_b2': _L0_tok_in['b2'], 'L0_tok_Wf': _L0_tok_in['Wf'], 'L0_tok_bf': _L0_tok_in['bf'], 'L0_tok_idx0': _L0_tok_in['idx0'], 'L0_tok_idx1': _L0_tok_in['idx1'], 'L0_tok_idx2': _L0_tok_in['idx2'], 'L0_attn_w_qkv': _L0_attn_in['w_qkv'], 'L0_attn_g_qkv': _L0_attn_in['g_qkv'], 'L0_attn_w_proj': _L0_attn_in['w_proj'], 'L0_attn_g_proj': _L0_attn_in['g_proj'], 'L0_ffn_moe0_W1': _L0_ffn_in['moe0_W1'], 'L0_ffn_moe0_b1': _L0_ffn_in['moe0_b1'], 'L0_ffn_moe0_W2': _L0_ffn_in['moe0_W2'], 'L0_ffn_moe0_b2': _L0_ffn_in['moe0_b2'], 'L0_ffn_A1_W': _L0_ffn_in['A1_W'], 'L0_ffn_A1_b': _L0_ffn_in['A1_b'], 'L0_ffn_A2_W': _L0_ffn_in['A2_W'], 'L0_ffn_A2_b': _L0_ffn_in['A2_b'], 'L0_ffn_G_W': _L0_ffn_in['G_W'], 'L0_ffn_mids': _L0_ffn_in['mids']}

def reference(x, L0_tok_W0, L0_tok_b0, L0_tok_W1, L0_tok_b1, L0_tok_W2, L0_tok_b2, L0_tok_Wf, L0_tok_bf, L0_tok_idx0, L0_tok_idx1, L0_tok_idx2, L0_attn_w_qkv, L0_attn_g_qkv, L0_attn_w_proj, L0_attn_g_proj, L0_ffn_moe0_W1, L0_ffn_moe0_b1, L0_ffn_moe0_W2, L0_ffn_moe0_b2, L0_ffn_A1_W, L0_ffn_A1_b, L0_ffn_A2_W, L0_ffn_A2_b, L0_ffn_G_W, L0_ffn_mids):
    import jax
    import jax.numpy as jnp

    def _L0_tok_ref(x, W0, b0, W1, b1, W2, b2, Wf, bf, idx0, idx1, idx2):
        import jax, jax.numpy as jnp
        import numpy as np
        B = 16
        IMG = 64
        CH = 3
        EMBED = 64
        GP = 16
        PRE = [1, 2, 4]
        N_LEVELS = 3
        FUSED = EMBED * N_LEVELS

        def hilbert_flat_indices(n):
            t = np.arange(n * n, dtype=np.int64)
            x = np.zeros(n * n, dtype=np.int64)
            y = np.zeros(n * n, dtype=np.int64)
            s = 1
            while s < n:
                rx = 1 & t // 2
                ry = 1 & (t ^ rx)
                swap = ry == 0
                flip = swap & (rx == 1)
                x = np.where(flip, s - 1 - x, x)
                y = np.where(flip, s - 1 - y, y)
                x2 = np.where(swap, y, x)
                y2 = np.where(swap, x, y)
                x, y = (x2, y2)
                x = x + s * rx
                y = y + s * ry
                t = t // 4
                s *= 2
            return y * n + x

        def _level(x, idx, W, b, p, gp):
            Bsz, C, H, _ = x.shape
            h = H // p
            t = x.reshape(Bsz, C, h, p, h, p).transpose(0, 2, 4, 3, 5, 1).reshape(Bsz, h * h, p * p * C)
            t = t[:, idx]
            t = t.reshape(Bsz, h * h // gp, gp * p * p * C)
            return t @ W.T + b

        def _interp_linear(x, n_out):
            L = x.shape[1]
            pos = (jnp.arange(n_out, dtype=jnp.float32) + 0.5) * (L / n_out) - 0.5
            pos = jnp.clip(pos, 0.0, L - 1)
            i0 = jnp.floor(pos).astype(jnp.int32)
            i1 = jnp.minimum(i0 + 1, L - 1)
            w = (pos - i0).astype(x.dtype)
            return x[:, i0] * (1.0 - w)[None, :, None] + x[:, i1] * w[None, :, None]
        Ws = [(idx0, W0, b0, PRE[0]), (idx1, W1, b1, PRE[1]), (idx2, W2, b2, PRE[2])]
        outs = [_level(x, idx, W, b, p, GP) for idx, W, b, p in Ws]
        n_tokens = outs[0].shape[1]
        outs = [outs[0]] + [_interp_linear(o, n_tokens) for o in outs[1:]]
        y = jnp.concatenate(outs, axis=-1)
        return y @ Wf.T + bf

    def _L0_attn_ref(x, w_qkv, g_qkv, w_proj, g_proj):
        import jax, jax.numpy as jnp
        import numpy as np
        EPS = 1e-05
        NUM_HEADS = 12

        def rmsnorm(x, g):
            var = jnp.mean(x * x, axis=-1, keepdims=True)
            return x * jax.lax.rsqrt(var + EPS) * g

        def activation_quant(x):
            scale = 127.0 / jnp.clip(jnp.max(jnp.abs(x), axis=-1, keepdims=True), EPS, None)
            return jnp.clip(jnp.round(x * scale), -128, 127) / scale

        def weight_quant(w):
            scale = 1.0 / jnp.clip(jnp.mean(jnp.abs(w)), EPS, None)
            return jnp.clip(jnp.round(w * scale), -1, 1) / scale

        def bitlinear(x, w, g):
            xn = rmsnorm(x, g)
            xq = xn + jax.lax.stop_gradient(activation_quant(xn) - xn)
            wq = w + jax.lax.stop_gradient(weight_quant(w) - w)
            return jnp.einsum('bnc,oc->bno', xq, wq)
        B, N, C = x.shape
        H = NUM_HEADS
        D = C // H
        scale = D ** (-0.5)
        qkv = bitlinear(x, w_qkv, g_qkv)
        qkv = qkv.reshape(B, N, 3, H, D)
        q = qkv[:, :, 0].transpose(0, 2, 1, 3)
        k = qkv[:, :, 1].transpose(0, 2, 1, 3)
        v = qkv[:, :, 2].transpose(0, 2, 1, 3)
        attn = jnp.einsum('bhnd,bhmd->bhnm', q, k) * scale
        attn = jax.nn.softmax(attn, axis=-1)
        out = jnp.einsum('bhnm,bhmd->bhnd', attn, v)
        out = out.transpose(0, 2, 1, 3).reshape(B, N, C)
        return bitlinear(out, w_proj, g_proj)

    def _L0_ffn_ref(x, moe0_W1, moe0_b1, moe0_W2, moe0_b2, A1_W, A1_b, A2_W, A2_b, G_W, mids):
        import jax, jax.numpy as jnp
        import numpy as np
        GT0 = [[0, 1, 0, 0, 1, 0], [0, 1, 0, 0, 0, 1], [0, 0, 1, 0, 1, 0], [0, 0, 1, 0, 0, 1], [0, 0, 0, 1, 1, 0], [0, 0, 0, 1, 0, 1]]
        NCLS = 6
        K = 1

        def _expert_pairs():
            pairs = []
            for i in range(NCLS):
                p = [(j - 1, k - 1) for j in range(1, 6) for k in range(1, 6) if j != k and GT0[i][j] == 1 and (GT0[i][k] == 1)]
                pairs.append(p)
            return pairs
        PAIRS = _expert_pairs()
        B, P, D, H = (64, 64, 192, 768)

        def _gelu(t):
            return jax.nn.gelu(t, approximate=False)
        cls_tokens = x[:, :NCLS]
        patch_tokens = x[:, NCLS:]
        patch_out = _gelu(patch_tokens @ moe0_W1 + moe0_b1) @ moe0_W2 + moe0_b2
        cls_outs = []
        for i in range(NCLS):
            tok = cls_tokens[:, i]
            eouts = [_gelu(tok @ A1_W[a] + A1_b[a]) @ A2_W[c] + A2_b[c] for a, c in PAIRS[i]]
            out = jnp.stack(eouts, axis=-1)
            gate = jax.nn.softmax(tok @ G_W[i], axis=-1)
            thr = jnp.sort(gate, axis=-1)[..., -(K + 1)]
            mask = (gate > thr[..., None]).astype(gate.dtype)
            g = gate * mask
            g = g / jnp.clip(jnp.sum(g, axis=-1, keepdims=True), 1e-06)
            cls_outs.append(jnp.sum(out * g[:, None, :], axis=-1))
        cls_out = jnp.stack(cls_outs, axis=1)
        return jnp.concatenate([cls_out, patch_out], axis=1)
    h = _L0_tok_ref(x, L0_tok_W0, L0_tok_b0, L0_tok_W1, L0_tok_b1, L0_tok_W2, L0_tok_b2, L0_tok_Wf, L0_tok_bf, L0_tok_idx0, L0_tok_idx1, L0_tok_idx2)
    h = h + _L0_attn_ref(_layernorm(h, axis=-1), L0_attn_w_qkv, L0_attn_g_qkv, L0_attn_w_proj, L0_attn_g_proj)
    h = h + _L0_ffn_ref(_layernorm(h, axis=-1), L0_ffn_moe0_W1, L0_ffn_moe0_b1, L0_ffn_moe0_W2, L0_ffn_moe0_b2, L0_ffn_A1_W, L0_ffn_A1_b, L0_ffn_A2_W, L0_ffn_A2_b, L0_ffn_G_W, L0_ffn_mids)
    return h

_drawn_inputs = setup_inputs


def setup_inputs(seed=0):
    import zlib

    import numpy as np

    out = dict(_drawn_inputs(seed))
    spreads = {'L0_attn_g_qkv': (1.0, 0.2),
     'L0_attn_g_proj': (1.0, 0.2),
     'L0_ffn_moe0_b1': (0.0, 0.27),
     'L0_ffn_moe0_b2': (0.0, 0.1),
     'L0_ffn_A1_b': (0.0, 0.8),
     'L0_ffn_A2_b': (0.0, 0.475)}
    factors = {'L0_tok_b0': 3.038,
     'L0_tok_b1': 3.251,
     'L0_tok_b2': 2.796,
     'L0_ffn_A1_W': 4.219,
     'L0_ffn_A2_W': 3.909,
     'L0_ffn_G_W': 3.404}
    for name, (base, spread) in spreads.items():
        noise = np.random.default_rng([zlib.crc32(name.encode()), seed]).standard_normal(out[name].shape)
        drawn = base * np.exp(spread * noise) if base else spread * noise
        out[name] = jnp.asarray(drawn.astype(out[name].dtype))
    for name, factor in factors.items():
        out[name] = (out[name] * factor).astype(out[name].dtype)
    return out
```

```python
import concourse.bass as bass
from concourse import mybir
from contextlib import ExitStack

F32 = mybir.dt.float32
BF16 = mybir.dt.bfloat16
I32 = mybir.dt.int32
ALU = mybir.AluOpType
ACT = mybir.ActivationFunctionType
AX = mybir.AxisListType

B = 16
N = 256
C = 192
H, D = 12, 16
NC = N // 128
KC = C // 96
G = H // 4
U = H // 2
HID = 768
NF = HID // 128
NCLS, NEXP = 6, 5
GP = 16
T1, T2 = 64, 16
P0, P1, P2 = 3, 12, 48
ZR = T1 + T2
PARTS = 6
EPS = 1e-5
MAGIC = 1.5 * 2.0 ** 23
QMAX = 127.0


def vit_tower(nc, x0, x1, x2, idx0, idx1, idx2, w0, w1, w2, b012, wf, bf, wqkv, gqkv, wproj, gproj,
              mw1, mb1, mw2, mb2, aw1, ab1, aw2, ab2, gw, out):
    ctx = ExitStack()
    with ctx:
        def sb(name, shape, dt=F32):
            return ctx.enter_context(nc.sbuf_tensor(name, shape, dt))

        def sem(name):
            return ctx.enter_context(nc.semaphore(name))

        def sems(name, n):
            return [sem(f"{name}{i}") for i in range(n)]

        ident = sb("ident", [128, 128])
        identb = sb("identb", [128, 128], BF16)
        ones = sb("ones", [128, 128])
        neg_half = sb("neg_half", [128, 2])
        idx0_sb = sb("idx0_sb", [128, NC * GP], I32)
        idx1_sb = sb("idx1_sb", [128, 8], I32)
        idx2_sb = sb("idx2_sb", [128, 2], I32)
        gath0 = sb("gath0", [128, NC, GP, B * P0])
        b012_sb = sb("b012_sb", [64, 3])
        bf_sb = sb("bf_sb", [1, C])
        zall = sb("zall", [128, B, C])
        tok_in = sb("tok_in", [128, NC, 128])
        pos = sb("pos", [128, 2, NC])
        tok_inT = sb("tok_inT", [128, N])
        h_all = sb("h_all", [128, B, NC, C])
        flat0 = h_all[:, :, :, :].rearrange("p b c n -> p (b c n)")
        fused = flat0[0:96, 0:11 * C].rearrange("p (k n) -> p k n", n=C)
        pat2, pat1 = (flat0[:, n:n + B * 96].rearrange("p (b n) -> p b n", b=B) for n in (11 * C, 11 * C + B * 96))
        wq = sb("wq", [96, KC, 3 * C], BF16)
        wp = sb("wp", [96, KC, C], BF16)
        wabs = sb("wabs", [96, 2])
        wscale = sb("wscale", [128, 4])
        wsq = sb("wsq", [128, 2])
        gq_sb = sb("gq_sb", [128, C])
        gp_sb = sb("gp_sb", [128, C])
        mb2_sb = sb("mb2_sb", [128, C])
        mw1_sb = sb("mw1_sb", [96, KC, HID])
        mb1_sb = sb("mb1_sb", [128, NF])
        mw2_sb = sb("mw2_sb", [128, NF, C])

        u_q = sb("u_q", [128, NC, C])
        r_q = sb("r_q", [128, NC, C])
        i_q = sb("i_q", [128, NC, C], BF16)
        iT_q = sb("iT_q", [96, KC, N], BF16)
        st_q = sb("st_q", [128, NC, 6])
        mv_q = sb("mv_q", [128, NC, 2])
        sc_q = sb("sc_q", [128, 8, NC])
        part1 = sb("part1", [128, 2, NC, H * D], BF16)
        part2 = sb("part2", [128, 2, NC, H * D], BF16)
        rest = sb("rest", [128, 2, NC, H * D])
        stack = sb("stack", [128, 2, NC, H, PARTS * D], BF16)
        qk = [sb(f"qk{i}", [98, 2, H, N], BF16) for i in range(2)]
        vals = sb("vals", [128, NC, H, 32])
        negmax = sb("negmax", [128, H, NC])
        shift = sb("shift", [128, NC, 2, H], BF16)
        shiftT = sb("shiftT", [2 * H, N], BF16)
        probs = sb("probs", [128, 4, 2, NC, N])
        oT = sb("oT", [128, G, N])
        recip = sb("recip", [128, NC, H])
        o = sb("o", [128, NC, H, D])
        u_p = sb("u_p", [128, NC, C])
        r_p = sb("r_p", [128, NC, C])
        i_p = sb("i_p", [128, NC, C], BF16)
        iT_p = sb("iT_p", [96, KC, N], BF16)
        st_p = sb("st_p", [128, NC, 6])
        mv_p = sb("mv_p", [128, NC, 2])
        sc_p = sb("sc_p", [128, 8, NC])
        st_n = sb("st_n", [128, NC, 6])
        mv_n = sb("mv_n", [128, NC, 2])
        sc_n = sb("sc_n", [128, 2, NC])
        xn = sb("xn", [128, NC, C])
        xnT = [sb(f"xnT{i}", [96, KC, N]) for i in range(2)]
        hb = [sb(f"hb{i}", [128, NC, C]) for i in range(2)]
        hid = sb("hid", [128, NF, N])
        o_sb = sb("o_sb", [128, NC, C])

        clsT = sb("clsT", [96, KC, NCLS, B])
        aw1_sb = sb("aw1_sb", [96, NEXP, KC, HID])
        ab1_sb = sb("ab1_sb", [128, NEXP, NF])
        aw2_sb = sb("aw2_sb", [128, NEXP, NF, C])
        ab2_sb = sb("ab2_sb", [NEXP, C])
        flat1 = aw1_sb[:, :, :, :].rearrange("p e k n -> p (e k n)")
        flat2 = aw2_sb[:, :, :, :].rearrange("p e f n -> p (e f n)")
        n_x, n_w = B * 128, KC * 4 * C
        x1T = flat1[:, 0:n_x].rearrange("p (j b n) -> p j b n", j=2, b=B)
        x2T = flat1[:, n_x:2 * n_x].rearrange("p (j b n) -> p j b n", j=8, b=B)
        w_raw, w_rnd = (flat1[:, 2 * n_x + n_w * i:2 * n_x + n_w * (i + 1)].rearrange("p (k n) -> p k n", k=KC)
                        for i in range(2))
        n_g, n_z = B * P2 * 2, B // 2 * C
        gath1 = flat2[:, 0:n_g].rearrange("p (t n) -> p t n", t=8)
        gath2 = flat2[:, n_g:2 * n_g].rearrange("p (t n) -> p t n", t=2)
        z1 = flat2[:, 2 * n_g:2 * n_g + n_z].rearrange("p (a n) -> p a n", n=C)
        z2 = flat2[:, 2 * n_g + n_z:2 * n_g + n_z + B // 8 * C].rearrange("p (a n) -> p a n", n=C)
        gw_sb = sb("gw_sb", [96, KC, 2 * NCLS])
        sel = sb("sel", [NEXP, 2, NCLS, B])
        own = sb("own", [NCLS * B, 2, NCLS])
        flat3 = probs[:, :, :, :, :].rearrange("p s a c n -> p (s a c n)")
        w0_sb, w1_sb, w2_sb = flat3[0:64, 0:48], flat3[0:64, 48:240], flat3[0:64, 240:1008]
        wf_sb = flat3[0:64, 1008:1008 + 3 * C].rearrange("p (k n) -> p k n", k=3)
        b012_wide = flat3[0:64, 1600:1600 + 3 * 128].rearrange("p (k n) -> p k n", k=3)
        hat = flat3[:, 2000:2000 + NC * ZR].rearrange("p (c t) -> p c t", c=NC)
        zbias = flat3[:, 2200:2200 + C]
        n_e, n_p = NEXP * NF * NCLS * B, 2 * NF * 3 * B
        hexp = flat3[:, 0:n_e].rearrange("p (c f t) -> p c f t", c=NEXP, f=NF)
        hcls = flat3[0:NCLS * B, n_e + n_p:n_e + n_p + C]
        ocls = flat3[0:NCLS * B, n_e + n_p + C:n_e + n_p + 2 * C]
        hpre = flat3[:, n_e:n_e + n_p].rearrange("p (a f s b) -> p a f s b", a=2, f=NF, s=3)
        logit = sb("logit", [NCLS * B, 2, NCLS])
        gate = sb("gate", [NCLS * B, 16])

        PS = ctx.enter_context(nc.psum_tensor("PS", [128, 8, 512], F32))
        PSb = PS[:, :, :].bitcast(BF16)

        s_idx = sem("s_idx")
        s_pat = sem("s_pat")
        s_tw = sem("s_tw")
        s_aw = sem("s_aw")
        s_fw = sem("s_fw")
        s_ew = sem("s_ew")
        s_g0, s_g12 = sem("s_g0"), sem("s_g12")
        s_zero = sem("s_zero")
        s_id = sem("s_id")
        s_pool = sem("s_pool")
        s_vc = sem("s_vc")
        s_wsum = sem("s_wsum")
        s_bw = sem("s_bw")
        s_fps, s_fsb = sem("s_fps"), sem("s_fsb")
        s_t12 = sem("s_t12")
        s_z, s_zc = sem("s_z"), sem("s_zc")
        s_zall = sem("s_zall")
        s_wt = sem("s_wt")
        s_const = sem("s_const")
        s_carrier = sem("s_carrier")
        scores, maxed = sems("scores", U), sems("maxed", U)
        shift_hi, shift_done, shift_t, shift_c = sem("shift_hi"), sem("shift_done"), sem("shift_t"), sem("shift_c")
        shift_rows = sems("shift_rows", 2)
        scoresT, expd = sems("scoresT", U), sems("expd", U)
        pv, oT_done = sems("pv", G), sems("oT_done", G)
        f1, gelud, f2, out_done, stored = sems("f1", NF), sems("gelud", NF), sems("f2", NC), sems("out_done", NC), sems("stored", NC)
        tok_ready, tok_t, tok_c, h_ps, h_sb = sem("tok_ready"), sem("tok_t"), sem("tok_c"), sem("h_ps"), sem("h_sb")
        q_steps = sems("q_step", 10)
        q_pow, q_int, q_t, q_tc = sem("q_pow"), sem("q_int"), sem("q_t"), sem("q_tc")
        qk_ps, v_ps, v_sb = sems("qk_ps", NC), sem("v_ps"), sem("v_sb")
        p1_done, rest_done, p2_done, p3_done, dup_done = sems("p1_done", NC), sems("rest_done", NC), sem("p2_done"), sem("p3_done"), sem("dup_done")
        stk_t, stk_c = sems("stk_t", U), sems("stk_c", U)
        o_t, o_rec, o_sbd = sem("o_t"), sem("o_rec"), sem("o_sbd")
        p_steps = sems("p_step", 10)
        p_pow, p_int, p_t, p_tc, p_ps = sem("p_pow"), sem("p_int"), sem("p_t"), sem("p_tc"), sem("p_ps")
        n_steps, xn_done = sems("n_step", 5), sem("xn_done")
        n_pow, n_t, n_tc, hb_done, cls_done = sem("n_pow"), sem("n_t"), sem("n_tc"), sem("hb_done"), sem("cls_done")
        e_hcls, e_l, e_lc, e_gate = sem("e_hcls"), sem("e_l"), sem("e_lc"), sem("e_gate")
        e_h, e_b, e_g, e_fin, e_out = sem("e_h"), sem("e_b"), sem("e_g"), sem("e_fin"), sem("e_out")

        block = ctx.enter_context(nc.Block())

        class At:

            def __init__(self, eng, t, loop=None):
                self.t, self.eng, self.loop = t, eng, loop
                self.seen = {}

            def __call__(self, off):
                if self.loop is None:
                    return min(self.t + off, B)
                k = self.t + off
                if k not in self.seen:
                    self.seen[k] = self.eng.snap(self.loop + k)
                return self.seen[k]

        def wait(eng, s, count, by=1):
            if isinstance(count, int):
                if count > 0:
                    eng.wait_ge(s, by * count)
            else:
                eng.wait_ge(s, count * by if by != 1 else count)

        def wait_alone(eng, s, count, by=1):
            wait(eng, s, count, by)
            eng.sem_inc(s_carrier)

        LOOP, LAST = 4, B + 1

        def steps(eng, body):
            for t in range(-1, LOOP):
                body(At(eng, t), t, t % 2)
            with eng.Fori(LOOP, B - 2, 2) as i:
                seen = {}
                for p in range(2):
                    at = At(eng, p, i)
                    at.seen = seen
                    body(at, LOOP, p)
            for t in range(B - 2, LAST + 1):
                body(At(eng, t), t, t % 2)

        def has(t):
            return 0 <= t < B, t + 1 < B, 1 <= t <= B, t >= 2

        @block.sync
        def _(sp):
            sp.dma_start(idx2_sb[:, :], idx2).then_inc(s_idx, 16)
            sp.dma_start(idx1_sb[:, :], idx1).then_inc(s_idx, 16)
            sp.dma_start(idx0_sb[:, :], idx0).then_inc(s_idx, 16)
            for dst, src in ((w0_sb, w0), (w1_sb, w1), (w2_sb, w2), (wf_sb, wf),
                             (b012_sb[:, :], b012), (bf_sb[:, :], bf)):
                sp.dma_start(dst, src).then_inc(s_tw, 16)
            sp.dma_start(w_raw[:, :, 0:3 * C], wqkv).then_inc(s_aw, 16)
            sp.dma_start(w_raw[:, :, 3 * C:4 * C], wproj).then_inc(s_aw, 16)
            sp.dma_start(gq_sb[:, :], gqkv.broadcast_to([128, C])).then_inc(s_aw, 16)
            sp.dma_start(gp_sb[:, :], gproj.broadcast_to([128, C])).then_inc(s_aw, 16)
            sp.dma_start(mb2_sb[:, :], mb2.broadcast_to([128, C])).then_inc(s_aw, 16)
            sp.wait_ge(s_fsb, 1)
            for b in range(B):
                sp.dma_start(zall[ZR:128, b, :], fused[0:48, 0, :]).then_inc(s_zall, 16)
            sp.dma_start(mw1_sb[:, :, :], mw1).then_inc(s_fw, 16)
            sp.dma_start(mb1_sb[:, :], mb1).then_inc(s_fw, 16)
            sp.dma_start(mw2_sb[:, :, :], mw2).then_inc(s_fw, 16)
            sp.wait_ge(s_zc, 8)
            zpair = zall[0:T1, :, :].rearrange("p (a e) n -> p a e n", e=2)
            for e in range(2):
                sp.dma_start(zpair[:, :, e, :], z1[T1 * e:T1 * (e + 1), :, :]).then_inc(s_zall, 16)
            sp.wait_ge(s_zc, 10)
            zoct = zall[T1:ZR, :, :].rearrange("p (a e) n -> p a e n", e=8)
            for e in range(8):
                sp.dma_start(zoct[:, :, e, :], z2[T2 * e:T2 * (e + 1), :, :]).then_inc(s_zall, 16)
            sp.wait_ge(s_wt, 8)
            sp.wait_ge(s_z, 10)
            sp.wait_ge(s_zall, 16 * (B + 10))
            sp.dma_start(aw1_sb[:, :, :, :], aw1).then_inc(s_ew, 16)
            sp.dma_start(aw2_sb[:, :, :, :], aw2).then_inc(s_ew, 16)
            sp.dma_start(ab1_sb[:, :, :], ab1).then_inc(s_ew, 16)
            sp.dma_start(ab2_sb[:, :], ab2).then_inc(s_ew, 16)
            sp.dma_start(gw_sb[:, :, :], gw).then_inc(s_ew, 16)

            def body(at, t, par):
                attn, front, back, ffn = has(t)
                if attn:
                    wait_alone(sp, shift_c, at(1))
                    wait_alone(sp, scoresT[U - 1], at(-1))
                    for r in range(2):
                        sp.dma_start(qk[par][96 + r:97 + r, 0, :, :], shiftT[H * r:H * (r + 1), :])\
                          .then_inc(shift_rows[r], 16)
                if ffn:
                    img = at(-2)
                    wait_alone(sp, out_done[0], at(-1))
                    sp.dma_start(out[bass.ds(img, 1), NCLS:128, :].rearrange("a p n -> p a n"), o_sb[NCLS:128, 0:1, :])\
                      .then_inc(stored[0], 16)
                    wait_alone(sp, out_done[1], at(-1))
                    sp.dma_start(out[bass.ds(img, 1), 128:N, :].rearrange("a p n -> p a n"), o_sb[:, 1:2, :])\
                      .then_inc(stored[1], 16)

            steps(sp, body)
            sp.wait_ge(n_steps[1], B)
            sp.wait_ge(pv[G - 1], B)
            for i in range(NCLS):
                sp.dma_start(hcls[B * i:B * (i + 1), :], h_all[i:i + 1, :, 0, :]).then_inc(e_hcls, 16)
            sp.wait_ge(e_fin, 2)
            for i in range(NCLS):
                sp.dma_start(out[:, i, :], ocls[B * i:B * (i + 1), :]).then_inc(e_out, 16)
            sp.wait_ge(stored[0], 16 * B)
            sp.wait_ge(stored[1], 16 * B)
            sp.wait_ge(e_out, 16 * NCLS)

        @block.gpsimd
        def _(pool):
            pool.wait_ge(s_idx, 48)
            for t in range(2):
                pool.indirect_dma_start(gath2[:, t, :], None, x2, bass.IndirectOffsetOnAxis(idx2_sb[:, t:t + 1], 0))\
                    .then_inc(s_g12, 16)
            for t in range(8):
                pool.indirect_dma_start(gath1[:, t, :], None, x1, bass.IndirectOffsetOnAxis(idx1_sb[:, t:t + 1], 0))\
                    .then_inc(s_g12, 16)
            pool.memset(ident[:, :], 0.0).then_inc(s_zero, 1)
            pool.memset(identb[:, :], 0.0).then_inc(s_zero, 1)
            pool.wait_ge(s_zero, 2)
            for m in (ident, identb):
                pool.affine_select(out=m[:, :], in_=m[:, :], compare_op=ALU.not_equal, fill=1.0, base=0,
                                   pattern=[[-1, 128]], channel_multiplier=1).then_inc(s_id, 1)
            for j in range(NC * GP):
                pool.indirect_dma_start(gath0[:, j // GP, j % GP, :], None, x0,
                                        bass.IndirectOffsetOnAxis(idx0_sb[:, j:j + 1], 0)).then_inc(s_g0, 16)
            pool.iota(hat[:, :, 0:T1], pattern=[[0, NC], [1, T1]], base=0, channel_multiplier=0,
                      allow_small_or_imprecise_dtypes=True).then_inc(s_pool, 1)
            pool.iota(hat[:, :, T1:ZR], pattern=[[0, NC], [1, T2]], base=0, channel_multiplier=0,
                      allow_small_or_imprecise_dtypes=True).then_inc(s_pool, 1)
            pool.iota(pos[:, :, :], pattern=[[0, 2], [128, NC]], base=0, channel_multiplier=1,
                      allow_small_or_imprecise_dtypes=True).then_inc(s_pool, 1)
            pool.memset(own[:, :, :], 1.0).then_inc(s_zero, 1)
            pool.wait_ge(s_zero, 3)
            pool.affine_select(out=own[:, :, :], in_=own[:, :, :], compare_op=ALU.is_ge, fill=0.0, base=0,
                               pattern=[[0, 2], [-B, NCLS]], channel_multiplier=1).then_inc(s_zero, 1)
            pool.wait_ge(s_zero, 4)
            pool.affine_select(out=own[:, :, :], in_=own[:, :, :], compare_op=ALU.is_ge, fill=0.0, base=B - 1,
                               pattern=[[0, 2], [B, NCLS]], channel_multiplier=-1).then_inc(s_const, 1)
            pool.memset(sel[:, :, :, :], 0.0).then_inc(s_zero, 1)
            pool.wait_ge(s_zero, 5)
            pool.affine_select(out=sel[:, 0, :, :].rearrange("p (l s) b -> p l s b", s=2),
                               in_=sel[:, 0, :, :].rearrange("p (l s) b -> p l s b", s=2),
                               compare_op=ALU.not_equal, fill=1.0, base=-3,
                               pattern=[[0, 3], [-1, 2], [0, B]], channel_multiplier=1).then_inc(s_const, 1)
            pool.affine_select(out=sel[:, 1, :, :].rearrange("p (l s) b -> p l s b", s=2),
                               in_=sel[:, 1, :, :].rearrange("p (l s) b -> p l s b", s=2),
                               compare_op=ALU.not_equal, fill=1.0, base=0,
                               pattern=[[-1, 3], [0, 2], [0, B]], channel_multiplier=1).then_inc(s_const, 1)
            pool.wait_ge(s_g0, 16 * NC * GP)

            def body(at, t, par):
                attn, front, back, ffn = has(t)
                if front:
                    wait(pool, tok_t, at(1))
                    if t == -1:
                        pool.wait_ge(s_vc, 6)
                    src = gath0[:, :, :, bass.ds(at(1) * P0, P0)]
                    pool.tensor_copy(tok_in[:, :, ZR:128].rearrange("p c (j k) -> p c j k", k=P0), src)\
                        .then_inc(tok_ready, 1)
                if back:
                    wait(pool, p_steps[1], at(0))
                    pool.tensor_tensor(sc_p[:, 1, :], sc_p[:, 0, :], neg_half[:, :], ALU.pow).then_inc(p_pow, 1)
                    wait(pool, p_steps[7], at(0))
                    wait_alone(pool, p_t, at(-1))
                    pool.tensor_scalar(i_p[:, :, :], r_p[:, :, :], -MAGIC, 1.0, ALU.add, ALU.mult).then_inc(p_int, 1)
                if front:
                    wait(pool, q_steps[1], at(2))
                    pool.tensor_tensor(sc_q[:, 1, :], sc_q[:, 0, :], neg_half[:, :], ALU.pow).then_inc(q_pow, 1)
                    wait(pool, q_steps[7], at(2))
                    wait_alone(pool, q_t, at(1))
                    pool.tensor_scalar(i_q[:, :, :], r_q[:, :, :], -MAGIC, 1.0, ALU.add, ALU.mult).then_inc(q_int, 1)
                if back:
                    wait(pool, n_steps[2], at(0))
                    pool.tensor_tensor(sc_n[:, 1, :], sc_n[:, 0, :], neg_half[:, :], ALU.pow).then_inc(n_pow, 1)
                    wait(pool, out_done[1], at(-2))
                    hrow = h_all[:, bass.ds(at(-1), 1), :, :].rearrange("p a c n -> p (a c) n")
                    pool.tensor_tensor(hb[1 - par][:, :, :], hrow,
                                       mb2_sb[:, :].unsqueeze(1).broadcast_to([128, NC, C]), ALU.add).then_inc(hb_done, 1)
                if front:
                    wait(pool, rest_done[1], at(2))
                    wait_alone(pool, dup_done, at(1))
                    pool.tensor_scalar(part2[:, :, :, :], rest[:, :, :, :], 1.0, 0.0, ALU.mult, ALU.add).then_inc(p2_done, 1)
                    wait(pool, p2_done, at(2))
                    wait(pool, stk_t[U - 1], at(1))
                    for side, slot in ((0, 5), (1, 2)):
                        last = pool.tensor_tensor(
                            stack[:, side, :, :, D * slot:D * (slot + 1)],
                            rest[:, side, :, :].rearrange("p c (h d) -> p c h d", d=D),
                            part2[:, side, :, :].rearrange("p c (h d) -> p c h d", d=D), ALU.subtract)
                    last.then_inc(p3_done, 1)
                if back:
                    wait(pool, n_tc, at(0))
                    pool.tensor_copy(clsT[:, :, :, bass.ds(at(-1), 1)].rearrange("p k i a -> p k (i a)"),
                                     xnT[1 - par][:, :, 0:NCLS]).then_inc(cls_done, 1)

            steps(pool, body)
            pool.wait_ge(pv[G - 1], B)
            pool.memset(hexp[:, :, :, :], 0.0).then_inc(s_const, 1)

        @block.scalar
        def _(act):
            def body(at, t, par):
                attn, front, back, ffn = has(t)

                def gelu(f):
                    if ffn:
                        wait(act, f1[f], at(-1))
                        if f == 0:
                            wait(act, f2[1], at(-2))
                        nc.scalar.activation(hid[:, f, :], PS[:, 4 + f % 2, 0:N], ACT.Gelu, bias=mb1_sb[:, f:f + 1])\
                            .then_inc(gelud[f], 1)

                def exp(u):
                    if attn:
                        wait(act, scoresT[u], at(1))
                        if u == 0:
                            wait(act, pv[G - 1], at(0))
                        if u >= 4:
                            wait(act, pv[0], at(1))
                        nc.scalar.activation(probs[:, u % 4, :, :, :].rearrange("p a c n -> p (a c n)"),
                                             PS[:, 2 * (u % 2):2 * (u % 2) + 2, :].rearrange("p a n -> p (a n)"),
                                             ACT.Exp, scale=float(D) ** -0.5).then_inc(expd[u], 1)

                def out_t(g):
                    if attn:
                        wait(act, pv[g], at(1))
                        if g == 0:
                            wait(act, o_t, at(0))
                        nc.scalar.copy(oT[:, g, :], PS[:, 6, 0:N]).then_inc(oT_done[g], 1)

                for f in range(4):
                    gelu(f)
                if front:
                    wait(act, tok_t, at(2))
                    wait(act, h_ps, at(1))
                    nc.scalar.copy(tok_inT[:, :], PS[:, 7, 0:N]).then_inc(tok_c, 1)
                for f in range(4, NF):
                    gelu(f)
                if back:
                    wait(act, p_t, at(0))
                    wait(act, p_ps, at(-1))
                    nc.scalar.copy(iT_p[:, :, :].rearrange("p k n -> p (k n)"), PSb[0:96, 7, 0:2 * N]).then_inc(p_tc, 1)
                if attn:
                    wait(act, shift_t, at(1))
                    wait(act, shift_rows[0], at(0), 16)
                    wait(act, shift_rows[1], at(0), 16)
                    nc.scalar.copy(shiftT[:, :], PSb[0:2 * H, 7, 0:N]).then_inc(shift_c, 1)
                for u in range(3):
                    exp(u)
                if front:
                    wait(act, q_t, at(2))
                    wait(act, v_ps, at(1))
                    nc.scalar.copy(iT_q[:, :, :].rearrange("p k n -> p (k n)"), PSb[0:96, 7, 0:2 * N]).then_inc(q_tc, 1)
                exp(3)
                out_t(0)
                if back:
                    wait(act, n_t, at(0))
                    wait(act, f1[NF - 1], at(-2))
                    wait(act, cls_done, at(-2))
                    nc.scalar.copy(xnT[1 - par][:, :, :].rearrange("p k n -> p (k n)"), PS[0:96, 7, :]).then_inc(n_tc, 1)
                exp(4)
                if front:
                    for c in range(NC):
                        wait(act, qk_ps[c], at(2))
                        if c == 0:
                            wait(act, dup_done, at(1))
                            wait(act, q_steps[6], at(2))
                        nc.scalar.activation(part1[:, :, c, :], PS[:, 4 + c, 0:2 * C].rearrange("p (s n) -> p s n", s=2),
                                             ACT.Copy, scale=sc_q[:, 6, c:c + 1]).then_inc(p1_done[c], 1)
                exp(5)
                out_t(1)
                out_t(2)
                if front:
                    for w in range(1, U, 2):
                        wait(act, stk_t[w], at(2))
                        nc.scalar.copy(qk[1 - par][0:96, :, 2 * w:2 * w + 2, :].rearrange("p s h n -> p s (h n)"),
                                       PSb[0:96, 4 + w % 2, :].rearrange("p (s n) -> p s n", s=2)).then_inc(stk_c[w], 1)

            for k in range(11):
                act.wait_ge(s_fps, k + 1)
                nrow = GP * P0 if k == 0 else 96
                nc.scalar.copy(fused[0:nrow, k, :], PS[0:nrow, k % 8, 0:C]).then_inc(s_fsb, 1)
            for k in range(8):
                act.wait_ge(s_t12, k + 1)
                dst = (x2T if k < 4 else x1T)[:, :, 4 * (k % 4):4 * (k % 4) + 4, :]
                src = PS[0:96, k, :].rearrange("p (b j n) -> p j b n", b=4, j=8 if k < 4 else 2)
                nc.scalar.copy(dst, src).then_inc(s_fsb, 1)
            act.wait_ge(s_fw, 48)
            steps(act, body)

            act.wait_ge(s_const, 4)
            for a in range(NEXP):
                act.wait_ge(e_b, a + 1)
                if a < 3:
                    view = hexp[:, 3:5, :, :].rearrange("p c f (l s b) -> p c s f l b", l=3, s=2)
                    for s in range(2):
                        last = nc.scalar.activation(view[:, s, s, :, a, :], hpre[:, a % 2, :, s, :], ACT.Gelu)
                else:
                    view = hexp[:, 0:3, :, :].rearrange("p c f (l s b) -> p c l s f b", l=3, s=2)
                    for l in range(3):
                        last = nc.scalar.activation(view[:, l, l, a - 3, :, :], hpre[:, a % 2, :, l, :], ACT.Gelu)
                last.then_inc(e_g, 1)
            act.wait_ge(e_gate, 2)
            nc.scalar.activation(gate[:, 3:5], gate[:, 3:5], ACT.Exp).then_inc(e_gate, 1)

        @block.vector
        def _(dve):
            V = nc.vector
            V.memset(ones[:, :], 1.0).then_inc(s_bw, 1)
            V.memset(neg_half[:, :], -0.5)
            for q in qk:
                V.memset(q[96:98, 1, :, :], 1.0)
            V.memset(vals[:, :, :, D:32], 0.0).then_inc(s_vc, 1)
            dve.wait_ge(s_vc, 1)
            V.memset(vals[:, :, :, D:D + 1], 1.0).then_inc(s_bw, 1)
            dve.wait_ge(s_tw, 96)
            dve.wait_ge(s_bw, 2)
            V.tensor_copy(b012_wide[:, :, :], b012_sb[:, :].unsqueeze(2).broadcast_to([64, 3, 128])).then_inc(s_bw, 1)
            dve.wait_ge(s_g12, 160)
            V.tensor_copy(pat2.rearrange("p b (t n) -> p b t n", t=2), gath2.rearrange("p t (b n) -> p b t n", b=B))\
             .then_inc(s_pat, 1)
            V.tensor_copy(pat1.rearrange("p b (t n) -> p b t n", t=8), gath1.rearrange("p t (b n) -> p b t n", b=B))\
             .then_inc(s_pat, 1)
            dve.wait_ge(s_aw, 80)
            for k, (a, b) in enumerate(((0, 3 * C), (3 * C, 4 * C))):
                last = V.tensor_reduce(wabs[:, k:k + 1], w_raw[:, :, a:b], AX.XY, ALU.add, apply_absolute_value=True)
            last.then_inc(s_wsum, 1)
            dve.wait_ge(s_wsum, 2)
            V.tensor_scalar(wscale[:, 0:1], PS[:, 7, 0:1], 1.0 / (3 * C * C), EPS, ALU.mult, ALU.max)
            V.tensor_scalar(wscale[:, 1:2], PS[:, 7, 1:2], 1.0 / (C * C), EPS, ALU.mult, ALU.max).then_inc(s_wt, 1)
            dve.wait_ge(s_wt, 1)
            V.reciprocal(wscale[:, 2:4], wscale[:, 0:2]).then_inc(s_wt, 1)
            V.tensor_scalar(wsq[:, :], wscale[:, 0:2], 1.0 / QMAX, None, ALU.mult).then_inc(s_wt, 1)
            dve.wait_ge(s_wt, 3)
            for k, (a, b) in enumerate(((0, 3 * C), (3 * C, 4 * C))):
                V.tensor_scalar(w_rnd[:, :, a:b], w_raw[:, :, a:b], wscale[0:96, 2 + k:3 + k], MAGIC, ALU.mult, ALU.add)\
                 .then_inc(s_wt, 1)
            dve.wait_ge(s_wt, 5)
            V.tensor_scalar(w_raw[:, :, :], w_rnd[:, :, :], -MAGIC, 1.0, ALU.add, ALU.min).then_inc(s_wt, 1)
            dve.wait_ge(s_wt, 6)
            V.tensor_scalar(wq[:, :, :], w_raw[:, :, 0:3 * C], -1.0, None, ALU.max).then_inc(s_wt, 1)
            V.tensor_scalar(wp[:, :, :], w_raw[:, :, 3 * C:4 * C], -1.0, None, ALU.max).then_inc(s_wt, 1)
            dve.wait_ge(s_fps, 12)
            V.tensor_copy(zbias[:, :], PS[:, 3, 0:C]).then_inc(s_vc, 1)
            dve.wait_ge(s_pool, 3)
            for lev, n_in in enumerate((T1, T2)):
                last = V.tensor_scalar(pos[:, lev, :], pos[:, lev, :], n_in / N, 0.5 * n_in / N - 0.5, ALU.mult, ALU.add)
            last.then_inc(s_vc, 1)
            dve.wait_ge(s_vc, 3)
            for lev, n_in in enumerate((T1, T2)):
                last = V.tensor_scalar(pos[:, lev, :], pos[:, lev, :], 0.0, float(n_in - 1), ALU.max, ALU.min)
            last.then_inc(s_vc, 1)
            dve.wait_ge(s_vc, 4)
            for lev, (a, b) in enumerate(((0, T1), (T1, ZR))):
                for c in range(NC):
                    last = V.tensor_scalar(hat[:, c, a:b], hat[:, c, a:b], pos[:, lev, c:c + 1], None, ALU.subtract)
            last.then_inc(s_bw, 1)
            dve.wait_ge(s_bw, 4)
            V.scalar_tensor_tensor(hat[:, :, :], hat[:, :, :], -1.0, hat[:, :, :], ALU.mult, ALU.max).then_inc(s_vc, 1)
            dve.wait_ge(s_vc, 5)
            V.tensor_scalar(hat[:, :, :], hat[:, :, :], -1.0, 1.0, ALU.mult, ALU.add).then_inc(s_bw, 1)
            dve.wait_ge(s_bw, 5)
            V.tensor_scalar(tok_in[:, :, 0:ZR], hat[:, :, :], 0.0, None, ALU.max).then_inc(s_vc, 1)
            for k in range(10):
                dve.wait_ge(s_z, k + 1)
                if k < 8:
                    V.tensor_tensor(z1[:, k, :], PS[:, k, 0:C], zbias[:, :], ALU.add).then_inc(s_zc, 1)
                else:
                    V.tensor_copy(z2[:, k - 8, :], PS[:, k - 8, 0:C]).then_inc(s_zc, 1)

            def quantise(k, stp, sc, u, r, w):
                V.tensor_tensor(sc[:, 3, :], sc[:, 2, :], sc[:, 1, :], ALU.mult).then_inc(stp[3], 1)
                wait(dve, stp[3], k)
                V.tensor_scalar(sc[:, 3, :], sc[:, 3, :], EPS, None, ALU.max).then_inc(stp[4], 1)
                wait(dve, stp[4], k)
                V.reciprocal(sc[:, 4, :], sc[:, 3, :]).then_inc(stp[5], 1)
                wait(dve, stp[5], k)
                V.tensor_scalar(sc[:, 6, :], sc[:, 3, :], w, None, ALU.mult)
                V.scalar_tensor_tensor(sc[:, 5, :], sc[:, 4, :], QMAX, sc[:, 1, :], ALU.mult, ALU.mult).then_inc(stp[6], 1)
                wait(dve, stp[6], k)
                for c in range(NC):
                    last = V.tensor_scalar(r[:, c, :], u[:, c, :], sc[:, 5, c:c + 1], MAGIC, ALU.mult, ALU.add)
                last.then_inc(stp[7], 1)

            def body(at, t, par):
                attn, front, back, ffn = has(t)

                def row_max(u):
                    if attn:
                        wait(dve, scores[u], at(1))
                        if u == 0:
                            wait(dve, shift_done, at(0))
                        V.tensor_reduce(negmax[:, 2 * u:2 * u + 2, :],
                                        PS[:, 2 * (u % 2):2 * (u % 2) + 2, :].rearrange("p a (c n) -> p a c n", c=NC),
                                        AX.X, ALU.max, negate=True).then_inc(maxed[u], 1)

                row_max(0)
                row_max(1)
                if back:
                    wait(dve, o_t, at(0))
                    ov = PS[:, 6:8, 0:128 * G].rearrange("p c (h e) -> p c h e", e=32)
                    V.reciprocal(recip[:, :, :], ov[:, :, :, D]).then_inc(o_rec, 1)
                    wait(dve, o_rec, at(0))
                    V.tensor_tensor(o[:, :, :, :], ov[:, :, :, 0:D],
                                    recip[:, :, :].unsqueeze(3).broadcast_to([128, NC, H, D]), ALU.mult).then_inc(o_sbd, 1)
                    wait_alone(dve, o_sbd, at(0))
                    of = o[:, :, :, :].rearrange("p c h d -> p c (h d)")
                    for c in range(NC):
                        last = V.bn_stats(st_p[:, c, :], of[:, c, :])
                    last.then_inc(p_steps[8], 1)
                    wait_alone(dve, p_steps[8], at(0))
                    for c in range(NC):
                        last = V.bn_aggr(mv_p[:, c, :], st_p[:, c, :])
                    last.then_inc(p_steps[9], 1)
                    wait(dve, p_steps[9], at(0))
                    V.tensor_tensor(sc_p[:, 7, :], mv_p[:, :, 0], mv_p[:, :, 0], ALU.mult).then_inc(p_steps[0], 1)
                    wait(dve, p_steps[0], at(0))
                    V.scalar_tensor_tensor(sc_p[:, 0, :], sc_p[:, 7, :], EPS, mv_p[:, :, 1], ALU.add, ALU.add)\
                        .then_inc(p_steps[1], 1)
                row_max(2)
                row_max(3)
                if back:
                    V.tensor_tensor(u_p[:, :, :], of, gp_sb[:, :].unsqueeze(1).broadcast_to([128, NC, C]), ALU.mult)\
                        .then_inc(p_steps[2], 1)
                    wait(dve, p_steps[2], at(0))
                    V.tensor_reduce(sc_p[:, 2, :], u_p[:, :, :], AX.X, ALU.max, apply_absolute_value=True).then_inc(n_steps[0], 1)
                    wait(dve, n_steps[0], at(0))
                    wait(dve, p_pow, at(0))
                    wait(dve, p_int, at(-1))
                    quantise(at(0), p_steps, sc_p, u_p, r_p, wsq[:, 1:2])
                row_max(4)
                row_max(5)
                if attn:
                    wait(dve, maxed[U - 1], at(1))
                    wait(dve, shift_t, at(0))
                    hi = shift[:, :, 0, :].rearrange("p c h -> p h c")
                    lo = shift[:, :, 1, :].rearrange("p c h -> p h c")
                    V.tensor_copy(hi, negmax[:, :, :]).then_inc(shift_hi, 1)
                    wait(dve, shift_hi, at(1))
                    V.tensor_tensor(lo, negmax[:, :, :], hi, ALU.subtract).then_inc(shift_done, 1)
                if front:
                    wait(dve, h_ps, at(2))
                    hn = h_all[:, bass.ds(at(1), 1), :, :].rearrange("p a c n -> p (a c) n")
                    V.tensor_copy(hn, PS[:, 7, 0:NC * C].rearrange("p (c n) -> p c n", c=NC)).then_inc(h_sb, 1)
                    wait_alone(dve, h_sb, at(2))
                    for c in range(NC):
                        last = V.bn_stats(st_q[:, c, :], hn[:, c, :])
                    last.then_inc(q_steps[8], 1)
                    wait_alone(dve, q_steps[8], at(2))
                    for c in range(NC):
                        last = V.bn_aggr(mv_q[:, c, :], st_q[:, c, :])
                    last.then_inc(q_steps[0], 1)
                    wait(dve, q_steps[0], at(2))
                    V.tensor_scalar(sc_q[:, 0, :], mv_q[:, :, 1], 1.0 + EPS, EPS * EPS, ALU.mult, ALU.add)\
                        .then_inc(q_steps[1], 1)
                    for c in range(NC):
                        last = V.scalar_tensor_tensor(u_q[:, c, :], hn[:, c, :], mv_q[:, c, 0:1], gq_sb[:, :],
                                                      ALU.subtract, ALU.mult)
                    last.then_inc(q_steps[2], 1)
                    wait(dve, q_steps[2], at(2))
                    V.tensor_reduce(sc_q[:, 2, :], u_q[:, :, :], AX.X, ALU.max, apply_absolute_value=True).then_inc(q_steps[9], 1)
                    wait(dve, q_steps[9], at(2))
                    wait(dve, q_pow, at(2))
                    wait(dve, q_int, at(1))
                    quantise(at(2), q_steps, sc_q, u_q, r_q, wsq[:, 0:1])

                def ffn_out(c):
                    if ffn:
                        wait(dve, f2[c], at(-1))
                        wait(dve, hb_done, at(-1))
                        wait(dve, stored[c], at(-2), 16)
                        V.tensor_tensor(o_sb[:, c, :], PS[:, 6, 0:C], hb[par][:, c, :], ALU.add).then_inc(out_done[c], 1)

                ffn_out(0)
                if back:
                    wait(dve, p_ps, at(0))
                    hr = h_all[:, bass.ds(at(-1), 1), :, :].rearrange("p a c n -> p (a c) n")
                    for c in range(NC):
                        last = V.scalar_tensor_tensor(hr[:, c, :], PS[:, 7, C * c:C * (c + 1)], sc_p[:, 6, c:c + 1],
                                                      hr[:, c, :], ALU.mult, ALU.add)
                    last.then_inc(n_steps[1], 1)
                    wait_alone(dve, n_steps[1], at(0))
                    for c in range(NC):
                        last = V.bn_stats(st_n[:, c, :], hr[:, c, :])
                    last.then_inc(n_steps[3], 1)
                    wait_alone(dve, n_steps[3], at(0))
                    for c in range(NC):
                        last = V.bn_aggr(mv_n[:, c, :], st_n[:, c, :])
                    last.then_inc(n_steps[4], 1)
                    wait(dve, n_steps[4], at(0))
                    V.tensor_scalar(sc_n[:, 0, :], mv_n[:, :, 1], EPS, None, ALU.add).then_inc(n_steps[2], 1)
                    wait(dve, n_pow, at(0))
                    wait(dve, n_t, at(-1))
                    for c in range(NC):
                        last = V.tensor_scalar(xn[:, c, :], hr[:, c, :], mv_n[:, c, 0:1], sc_n[:, 1, c:c + 1],
                                               ALU.subtract, ALU.mult)
                    last.then_inc(xn_done, 1)
                if front:
                    wait(dve, v_ps, at(2))
                    wait(dve, pv[G - 1], at(1))
                    for c in range(NC):
                        last = V.tensor_scalar(vals[:, c, :, 0:D],
                                               PS[:, 7, C * c:C * (c + 1)].rearrange("p (h d) -> p h d", d=D),
                                               sc_q[:, 6, c:c + 1], None, ALU.mult)
                    last.then_inc(v_sb, 1)
                    for c in range(NC):
                        wait(dve, p1_done[c], at(2))
                        if c == 0:
                            wait(dve, p3_done, at(1))
                        V.scalar_tensor_tensor(rest[:, :, c, :], PS[:, 4 + c, 0:2 * C].rearrange("p (s n) -> p s n", s=2),
                                               sc_q[:, 6, c:c + 1], part1[:, :, c, :], ALU.mult, ALU.subtract)\
                            .then_inc(rest_done[c], 1)
                    wait(dve, stk_t[U - 1], at(1))

                    def dup(side, part, first, last_, step):
                        src = part[:, side, :, :].rearrange("p c (h d) -> p (c h) d", d=D)
                        dst = stack[:, side, :, :, :].rearrange("p c h (s d) -> p (c h) s d", d=D)[:, :, first:last_:step, :]
                        n = len(range(first, last_, step))
                        return V.tensor_copy(dst, src.unsqueeze(2).broadcast_to([128, NC * H, n, D]))

                    dup(0, part1, 0, 3, 1)
                    dup(1, part1, 0, 1, 1)
                    dup(1, part1, 3, 6, 2)
                    wait(dve, p2_done, at(2))
                    dup(0, part2, 3, 5, 1)
                    dup(1, part2, 1, 5, 3).then_inc(dup_done, 1)
                ffn_out(1)
                if front:
                    for w in range(0, U, 2):
                        wait(dve, stk_t[w], at(2))
                        V.tensor_copy(qk[1 - par][0:96, :, 2 * w:2 * w + 2, :].rearrange("p s h n -> p s (h n)"),
                                      PSb[0:96, 4 + w % 2, :].rearrange("p (s n) -> p s n", s=2)).then_inc(stk_c[w], 1)

            steps(dve, body)

            dve.wait_ge(e_l, 1)
            dve.wait_ge(s_const, 3)
            V.tensor_tensor(logit[:, :, :], PS[0:NCLS * B, 7, 0:2 * NCLS].rearrange("p (i e) -> p e i", e=2), own[:, :, :],
                            ALU.mult).then_inc(e_lc, 1)
            dve.wait_ge(e_lc, 1)
            V.tensor_reduce(gate[:, 0:2], logit[:, :, :], AX.X, ALU.add).then_inc(e_lc, 1)
            dve.wait_ge(e_lc, 2)
            V.tensor_reduce(gate[:, 2:3], gate[:, 0:2], AX.X, ALU.max).then_inc(e_gate, 1)
            dve.wait_ge(e_gate, 1)
            V.tensor_scalar(gate[:, 3:5], gate[:, 0:2], gate[:, 2:3], None, ALU.subtract).then_inc(e_gate, 1)

            def expert_bias(a):
                dve.wait_ge(e_h, a + 1)
                if a >= 2:
                    dve.wait_ge(e_g, a - 1)
                pair = 2 * (a % 3)
                for half in range(2):
                    src = PS[:, pair + half, 0:3 * NCLS * B]
                    if a < 3:
                        src = src.rearrange("p (f l s b) -> p f l s b", f=3, l=3, s=2)[:, :, a, :, :]
                        n = 2
                    else:
                        src = src.rearrange("p (f l s b) -> p f l s b", f=3, l=3, s=2)[:, :, :, a - 3, :]
                        n = 3
                    bias = ab1_sb[:, a, 3 * half:3 * half + 3].unsqueeze(2).unsqueeze(3).broadcast_to([128, 3, n, B])
                    last = V.tensor_tensor(hpre[:, a % 2, 3 * half:3 * half + 3, 0:n, :], src, bias, ALU.add)
                last.then_inc(e_b, 1)

            dve.wait_ge(pv[G - 1], B)
            for a in range(NEXP):
                expert_bias(a)
            dve.wait_ge(e_gate, 3)
            V.tensor_reduce(gate[:, 5:6], gate[:, 3:5], AX.X, ALU.add).then_inc(e_gate, 1)
            dve.wait_ge(e_gate, 4)
            V.reciprocal(gate[:, 6:7], gate[:, 5:6]).then_inc(e_gate, 1)
            dve.wait_ge(e_gate, 5)
            V.tensor_scalar(gate[:, 7:9], gate[:, 3:5], gate[:, 6:7], None, ALU.mult).then_inc(e_gate, 1)
            dve.wait_ge(e_gate, 6)
            V.tensor_reduce(gate[:, 9:10], gate[:, 7:9], AX.X, ALU.min).then_inc(e_gate, 1)
            dve.wait_ge(e_gate, 7)
            V.scalar_tensor_tensor(gate[:, 10:12], gate[:, 7:9], gate[:, 9:10], gate[:, 7:9], ALU.is_gt, ALU.mult).then_inc(e_gate, 1)
            dve.wait_ge(e_gate, 8)
            V.tensor_reduce(gate[:, 12:13], gate[:, 10:12], AX.X, ALU.add).then_inc(e_gate, 1)
            dve.wait_ge(e_gate, 9)
            V.tensor_scalar(gate[:, 12:13], gate[:, 12:13], 1e-6, None, ALU.max).then_inc(e_gate, 1)
            dve.wait_ge(e_gate, 10)
            V.reciprocal(gate[:, 13:14], gate[:, 12:13]).then_inc(e_gate, 1)
            dve.wait_ge(e_gate, 11)
            V.tensor_scalar(gate[:, 14:16], gate[:, 10:12], gate[:, 13:14], None, ALU.mult).then_inc(e_gate, 1)
            dve.wait_ge(e_gate, 12)
            dve.wait_ge(e_hcls, 16 * NCLS)
            dve.wait_ge(e_h, NEXP + 1)
            V.scalar_tensor_tensor(ocls[:, :], PS[0:NCLS * B, 6, 0:C], gate[:, 14:15], hcls[:, :], ALU.mult, ALU.add)\
             .then_inc(e_fin, 1)
            dve.wait_ge(e_fin, 1)
            dve.wait_ge(e_h, NEXP + 2)
            V.scalar_tensor_tensor(ocls[:, :], PS[0:NCLS * B, 7, 0:C], gate[:, 15:16], ocls[:, :], ALU.mult, ALU.add)\
             .then_inc(e_fin, 1)

        @block.tensor
        def _(pe):
            T = nc.tensor

            def mm(o_, l, r, first=True, final=True):
                return T.matmul(o_, l, r, start=first, stop=final)

            pe.wait_ge(s_tw, 96)
            for k in range(11):
                if k >= 8:
                    pe.wait_ge(s_fsb, k - 7)
                if k == 0:
                    mm(PS[0:GP * P0, 0, 0:C], w0_sb[:, :], wf_sb[:, 0, :]).then_inc(s_fps, 1)
                elif k < 3:
                    mm(PS[0:96, k, 0:C], w1_sb[:, 96 * (k - 1):96 * k], wf_sb[:, 1, :]).then_inc(s_fps, 1)
                else:
                    mm(PS[0:96, k % 8, 0:C], w2_sb[:, 96 * (k - 3):96 * (k - 2)], wf_sb[:, 2, :]).then_inc(s_fps, 1)
            pe.wait_ge(s_bw, 3)
            pe.wait_ge(s_fsb, 4)
            for lev in range(3):
                mm(PS[:, 3, 0:C], b012_wide[:, lev, :], wf_sb[:, lev, :], lev == 0, False)
            mm(PS[:, 3, 0:C], ones[0:1, :], bf_sb[:, :], False, True).then_inc(s_fps, 1)
            pe.wait_ge(s_wsum, 1)
            pe.wait_ge(s_fsb, 8)
            mm(PS[:, 7, 0:2], ones[0:96, :], wabs[:, :]).then_inc(s_wsum, 1)
            pe.wait_ge(s_id, 2)
            pe.wait_ge(s_fsb, 11)
            pe.wait_ge(s_vc, 2)
            for k in range(8):
                src = pat2 if k < 4 else pat1
                if k % 4 == 0:
                    pe.wait_ge(s_pat, 1 + k // 4)
                if k == 7:
                    pe.wait_ge(s_wt, 1)
                for e in range(4):
                    b = 4 * (k % 4) + e
                    last = T.transpose(PS[0:96, k, 128 * e:128 * (e + 1)], src[:, b, :], ident[:, :])
                last.then_inc(s_t12, 1)
            for k in range(10):
                if k == 0:
                    pe.wait_ge(s_fsb, 19)
                if k >= 8:
                    pe.wait_ge(s_zc, k - 7)
                if k < 8:
                    for jh in range(2):
                        last = mm(PS[:, k, 0:C], x1T[:, jh, 2 * k:2 * k + 2, :].rearrange("p b n -> p (b n)"), fused[:, 1 + jh, :],
                                  jh == 0, jh == 1)
                else:
                    e = k - 8
                    for j8 in range(8):
                        last = mm(PS[:, e, 0:C], x2T[:, j8, 8 * e:8 * e + 8, :].rearrange("p b n -> p (b n)"), fused[:, 3 + j8, :],
                                  j8 == 0, j8 == 7)
                last.then_inc(s_z, 1)
            pe.wait_ge(s_zc, 10)
            pe.wait_ge(s_zall, 16 * (B + 10))
            pe.wait_ge(s_wt, 8)
            pe.wait_ge(s_fw, 48)

            def body(at, t, par):
                attn, front, back, ffn = has(t)

                def score(u):
                    if attn:
                        if u < 2:
                            wait(pe, expd[4 + u], at(0))
                        else:
                            wait(pe, maxed[u - 2], at(1))
                        wait(pe, stk_c[u], at(1))
                        for hh in range(2):
                            for c in range(NC):
                                last = mm(PS[:, 2 * (u % 2) + hh, N * c:N * (c + 1)],
                                          qk[par][0:96, 0, 2 * u + hh, 128 * c:128 * (c + 1)],
                                          qk[par][0:96, 1, 2 * u + hh, :])
                        last.then_inc(scores[u], 1)

                def score_t(u):
                    if attn:
                        if u < 2:
                            wait(pe, maxed[4 + u], at(1))
                        else:
                            wait(pe, expd[u - 2], at(1))
                        if u == 0:
                            for r in range(2):
                                wait(pe, shift_rows[r], at(1), 16)
                        for hh in range(2):
                            for c in range(NC):
                                last = mm(PS[:, 2 * (u % 2) + hh, N * c:N * (c + 1)],
                                          qk[par][:, 1, 2 * u + hh, 128 * c:128 * (c + 1)],
                                          qk[par][:, 0, 2 * u + hh, :])
                        last.then_inc(scoresT[u], 1)

                def weighted(g):
                    if attn:
                        wait(pe, expd[2 * g], at(1))
                        wait(pe, expd[2 * g + 1], at(1))
                        if g == 0:
                            wait(pe, v_sb, at(1))
                            wait(pe, out_done[0], at(-1))
                            wait(pe, o_sbd, at(0))
                        else:
                            wait(pe, oT_done[g - 1], at(1))
                        for c in range(NC):
                            for j in range(4):
                                last = mm(PS[32 * j:32 * (j + 1), 6, 0:N], vals[:, c, 4 * g + j, :],
                                          probs[:, (2 * g + j // 2) % 4, j % 2, c, :], c == 0, c == NC - 1)
                        last.then_inc(pv[g], 1)

                def hidden(f):
                    if ffn:
                        if f == 0:
                            wait(pe, n_tc, at(-1))
                        if f < 2:
                            wait(pe, stk_c[4 + f], at(1))
                        else:
                            wait(pe, gelud[f - 2], at(-1))
                        for k in range(KC):
                            last = mm(PS[:, 4 + f % 2, 0:N], mw1_sb[:, k, 128 * f:128 * (f + 1)], xnT[par][:, k, :],
                                      k == 0, k == KC - 1)
                        last.then_inc(f1[f], 1)

                def ffn_rows(c):
                    if ffn:
                        if c == 0:
                            for f in range(NF):
                                wait(pe, gelud[f], at(-1))
                            if back:
                                wait(pe, o_sbd, at(0))
                            else:
                                wait(pe, out_done[1], at(-2))
                        else:
                            wait(pe, oT_done[G - 1], at(1))
                            wait(pe, out_done[0], at(-1))
                        for f in range(NF):
                            last = mm(PS[:, 6, 0:C], hid[:, f, 128 * c:128 * (c + 1)], mw2_sb[:, f, :], f == 0, f == NF - 1)
                        last.then_inc(f2[c], 1)

                score(0)
                hidden(0)
                score(1)
                hidden(1)
                if back:
                    for g in range(G):
                        wait(pe, oT_done[g], at(0))
                    wait(pe, out_done[1], at(-2))
                    wait(pe, v_sb, at(1))
                    for c in range(NC):
                        for g in range(G):
                            last = T.transpose(PS[:, 6 + c, 128 * g:128 * (g + 1)], oT[:, g, 128 * c:128 * (c + 1)], ident[:, :])
                    last.then_inc(o_t, 1)
                score(2)
                hidden(2)
                score(3)
                hidden(3)
                if front:
                    wait(pe, tok_ready, at(2))
                    wait(pe, v_sb, at(1))
                    wait(pe, o_sbd, at(0))
                    for c in range(NC):
                        last = T.transpose(PS[:, 7, 128 * c:128 * (c + 1)], tok_in[:, c, :], ident[:, :])
                    last.then_inc(tok_t, 1)
                score(4)
                hidden(4)
                score(5)
                hidden(5)
                if front:
                    wait(pe, tok_c, at(2))
                    for c in range(NC):
                        last = mm(PS[:, 7, C * c:C * (c + 1)], tok_inT[:, 128 * c:128 * (c + 1)],
                                  zall[:, bass.ds(at(1), 1), :].rearrange("p a n -> p (a n)"))
                    last.then_inc(h_ps, 1)
                if back:
                    wait(pe, p_int, at(0))
                    wait(pe, o_sbd, at(0))
                    if front:
                        wait(pe, h_sb, at(2))
                    for k in range(KC):
                        for c in range(NC):
                            last = T.transpose(PSb[0:96, 7, N * k + 128 * c:N * k + 128 * (c + 1)],
                                               i_p[:, c, 96 * k:96 * (k + 1)], identb[:, :])
                    last.then_inc(p_t, 1)
                if attn:
                    wait(pe, shift_done, at(1))
                    if front:
                        wait(pe, h_sb, at(2))
                    if back:
                        wait(pe, p_tc, at(0))
                    else:
                        wait(pe, v_sb, at(1))
                    for c in range(NC):
                        last = T.transpose(PSb[0:2 * H, 7, 128 * c:128 * (c + 1)],
                                           shift[:, c, :, :].rearrange("p r h -> p (r h)"), identb[:, :])
                    last.then_inc(shift_t, 1)
                ffn_rows(0)
                if back:
                    wait(pe, p_tc, at(0))
                    if attn:
                        wait(pe, shift_c, at(1))
                    for c in range(NC):
                        for k in range(KC):
                            last = mm(PS[:, 7, C * c:C * (c + 1)], iT_p[:, k, 128 * c:128 * (c + 1)], wp[:, k, :],
                                      k == 0, k == KC - 1)
                    last.then_inc(p_ps, 1)
                score_t(0)
                score_t(1)
                score_t(2)
                if front:
                    wait(pe, q_int, at(2))
                    if attn:
                        wait(pe, shift_c, at(1))
                    if back:
                        wait(pe, n_steps[1], at(0))
                    for k in range(KC):
                        for c in range(NC):
                            last = T.transpose(PSb[0:96, 7, N * k + 128 * c:N * k + 128 * (c + 1)],
                                               i_q[:, c, 96 * k:96 * (k + 1)], identb[:, :])
                    last.then_inc(q_t, 1)
                score_t(3)
                weighted(0)
                if back:
                    wait(pe, xn_done, at(0))
                    if front:
                        wait(pe, q_tc, at(2))
                    for k in range(KC):
                        for c in range(NC):
                            last = T.transpose(PS[0:96, 7, N * k + 128 * c:N * k + 128 * (c + 1)],
                                               xn[:, c, 96 * k:96 * (k + 1)], ident[:, :])
                    last.then_inc(n_t, 1)
                score_t(4)
                if front:
                    wait(pe, q_tc, at(2))
                    if ffn:
                        for f in range(NF - 2, NF):
                            wait(pe, gelud[f], at(-1))
                    for c in range(NC):
                        if t != -1 and c == 0:
                            for w in range(U - 2, U):
                                wait(pe, stk_c[w], at(1))
                        for k in range(KC):
                            last = mm(PS[:, 4 + c, 0:2 * C], iT_q[:, k, 128 * c:128 * (c + 1)], wq[:, k, 0:2 * C],
                                      k == 0, k == KC - 1)
                        last.then_inc(qk_ps[c], 1)
                    if back:
                        wait(pe, n_tc, at(0))
                    for c in range(NC):
                        for k in range(KC):
                            last = mm(PS[:, 7, C * c:C * (c + 1)], iT_q[:, k, 128 * c:128 * (c + 1)], wq[:, k, 2 * C:3 * C],
                                      k == 0, k == KC - 1)
                    last.then_inc(v_ps, 1)
                score_t(5)
                weighted(1)
                weighted(2)
                ffn_rows(1)
                if front:
                    wait(pe, p3_done, at(2))
                    wait(pe, dup_done, at(2))
                    for w in range(U):
                        if w < 2:
                            wait(pe, rest_done[w], at(2))
                        else:
                            wait(pe, stk_c[w - 2], at(2))
                        for side in range(2):
                            for hh in range(2):
                                for c in range(NC):
                                    at_ = (4 * side + 2 * hh + c) * 128
                                    last = T.transpose(PSb[0:96, 4 + w % 2, at_:at_ + 128], stack[:, side, c, 2 * w + hh, :],
                                                       identb[:, :])
                        last.then_inc(stk_t[w], 1)

            steps(pe, body)

            pe.wait_ge(s_ew, 80)
            pe.wait_ge(cls_done, B)
            pe.wait_ge(n_tc, B)
            tok = clsT[:, :, :, :].rearrange("p k i b -> p k (i b)")
            for k in range(KC):
                last = mm(PS[0:NCLS * B, 7, 0:2 * NCLS], tok[:, k, :], gw_sb[:, k, :], k == 0, k == KC - 1)
            last.then_inc(e_l, 1)

            def second(e, bank, experts):
                for c in experts:
                    for f in range(NF):
                        mm(PS[0:NCLS * B, bank, 0:C], hexp[:, c, f, :], aw2_sb[:, c, f, :], c == experts[0] and f == 0, False)
                mm(PS[0:NCLS * B, bank, 0:C], sel[:, e, :, :].rearrange("p i b -> p (i b)"), ab2_sb[:, :], False, True)\
                    .then_inc(e_h, 1)

            for a in range(NEXP):
                if a >= 3:
                    pe.wait_ge(e_b, a - 2)
                if a == 2:
                    pe.wait_ge(gelud[NF - 1], B)
                for f in range(NF):
                    for k in range(KC):
                        last = mm(PS[:, 2 * (a % 3) + f // 3, NCLS * B * (f % 3):NCLS * B * (f % 3 + 1)],
                                  aw1_sb[:, a, k, 128 * f:128 * (f + 1)], tok[:, k, :], k == 0, k == KC - 1)
                last.then_inc(e_h, 1)
            pe.wait_ge(s_const, 3)
            pe.wait_ge(out_done[1], B)
            pe.wait_ge(e_g, 3)
            second(0, 6, (3, 4))
            pe.wait_ge(e_g, 5)
            pe.wait_ge(e_lc, 1)
            second(1, 7, (0, 1, 2))


def kernel(**inputs):
    import numpy as np
    import concourse.bacc as bacc
    from concourse.bass_utils import run_bass_kernel_spmd

    a = {k: np.asarray(v) for k, v in inputs.items()}

    def patches(p):
        n = 64 // p
        return a["x"].reshape(B, 3, n, p, n, p).transpose(2, 4, 0, 3, 5, 1).reshape(n * n, B * p * p * 3)

    def chunks(w, rows):
        w = w.reshape(w.shape[:-2] + (w.shape[-2] // rows, rows, w.shape[-1]))
        return np.moveaxis(w, -2, 0)

    ins = {
        "x0": patches(1), "x1": patches(2), "x2": patches(4),
        "idx0": a["L0_tok_idx0"].reshape(NC, 128, GP).transpose(1, 0, 2).reshape(128, NC * GP),
        "idx1": a["L0_tok_idx1"].reshape(T1, 2, 8).transpose(1, 0, 2).reshape(128, 8),
        "idx2": a["L0_tok_idx2"].reshape(T2, 8, 2).transpose(1, 0, 2).reshape(128, 2),
        "w0": a["L0_tok_W0"], "w1": a["L0_tok_W1"], "w2": a["L0_tok_W2"],
        "b012": np.stack([a["L0_tok_b0"], a["L0_tok_b1"], a["L0_tok_b2"]], axis=1),
        "wf": chunks(a["L0_tok_Wf"].T, 64), "bf": a["L0_tok_bf"].reshape(1, C),
        "wqkv": chunks(a["L0_attn_w_qkv"].T, 96), "gqkv": a["L0_attn_g_qkv"].reshape(1, C),
        "wproj": chunks(a["L0_attn_w_proj"].T, 96), "gproj": a["L0_attn_g_proj"].reshape(1, C),
        "mw1": chunks(a["L0_ffn_moe0_W1"], 96), "mb1": a["L0_ffn_moe0_b1"].reshape(NF, 128).T,
        "mw2": chunks(a["L0_ffn_moe0_W2"], 128), "mb2": a["L0_ffn_moe0_b2"].reshape(1, C),
        "aw1": chunks(a["L0_ffn_A1_W"], 96), "ab1": a["L0_ffn_A1_b"].reshape(NEXP, NF, 128).transpose(2, 0, 1),
        "aw2": chunks(a["L0_ffn_A2_W"], 128), "ab2": a["L0_ffn_A2_b"],
        "gw": chunks(a["L0_ffn_G_W"].transpose(1, 0, 2).reshape(C, 2 * NCLS), 96),
    }
    nc = bacc.Bacc("TRN2", target_bir_lowering=False, num_devices=1)
    arrays, args = {}, []
    for name, v in ins.items():
        v = np.ascontiguousarray(v)
        arrays[f"in_{name}"] = v
        args.append(nc.dram_tensor(f"in_{name}", v.shape, mybir.dt.from_np(v.dtype), kind="ExternalInput").ap())
    args.append(nc.dram_tensor("out_0", (B, N, C), F32, kind="ExternalOutput").ap())
    vit_tower(nc, *args)
    r = run_bass_kernel_spmd(nc, [arrays], core_ids=[0])
    return r.results[0]["out_0"]
```

```python
import concourse.bass as bass
from concourse import mybir
from contextlib import ExitStack

F32 = mybir.dt.float32
BF16 = mybir.dt.bfloat16
I32 = mybir.dt.int32
ALU = mybir.AluOpType
ACT = mybir.ActivationFunctionType
AX = mybir.AxisListType

B = 16
N = 256
C = 192
H, D = 12, 16
NC = N // 128
KC = C // 96
G = H // 4
U = H // 2
HID = 768
NF = HID // 128
NCLS, NEXP = 6, 5
GP = 16
T1, T2 = 64, 16
P0, P1, P2 = 3, 12, 48
ZR = T1 + T2
PARTS = 6
EPS = 1e-5
MAGIC = 1.5 * 2.0 ** 23
QMAX = 127.0


def vit_tower(nc, x0, x1, x2, idx0, idx1, idx2, w0, w1, w2, b012, wf, bf, wqkv, gqkv, wproj, gproj,
              mw1, mb1, mw2, mb2, aw1, ab1, aw2, ab2, gw, out):
    ctx = ExitStack()
    with ctx:
        def sb(name, shape, dt=F32):
            return ctx.enter_context(nc.sbuf_tensor(name, shape, dt))

        def sem(name):
            return ctx.enter_context(nc.semaphore(name))

        def sems(name, n):
            return [sem(f"{name}{i}") for i in range(n)]

        ident = sb("ident", [128, 128])
        identb = sb("identb", [128, 128], BF16)
        ones = sb("ones", [128, 128])
        neg_half = sb("neg_half", [128, 2])
        idx0_sb = sb("idx0_sb", [128, NC * GP], I32)
        idx1_sb = sb("idx1_sb", [128, 8], I32)
        idx2_sb = sb("idx2_sb", [128, 2], I32)
        gath0 = sb("gath0", [128, NC, GP, B * P0])
        b012_sb = sb("b012_sb", [64, 3])
        bf_sb = sb("bf_sb", [1, C])
        zall = sb("zall", [128, B, C])
        tok_in = sb("tok_in", [128, NC, 128])
        pos = sb("pos", [128, 2, NC])
        tok_inT = sb("tok_inT", [128, N])
        h_all = sb("h_all", [128, B, NC, C])
        flat0 = h_all[:, :, :, :].rearrange("p b c n -> p (b c n)")
        fused = flat0[0:96, 0:11 * C].rearrange("p (k n) -> p k n", n=C)
        pat2, pat1 = (flat0[:, n:n + B * 96].rearrange("p (b n) -> p b n", b=B) for n in (11 * C, 11 * C + B * 96))
        wq = sb("wq", [96, KC, 3 * C], BF16)
        wp = sb("wp", [96, KC, C], BF16)
        wabs = sb("wabs", [96, 2])
        wscale = sb("wscale", [128, 4])
        wsq = sb("wsq", [128, 2])
        gq_sb = sb("gq_sb", [128, C])
        gp_sb = sb("gp_sb", [128, C])
        mb2_sb = sb("mb2_sb", [128, C])
        mw1_sb = sb("mw1_sb", [96, KC, HID])
        mb1_sb = sb("mb1_sb", [128, NF])
        mw2_sb = sb("mw2_sb", [128, NF, C])

        u_q = sb("u_q", [128, NC, C])
        r_q = sb("r_q", [128, NC, C])
        i_q = sb("i_q", [128, NC, C], BF16)
        iT_q = sb("iT_q", [96, KC, N], BF16)
        st_q = sb("st_q", [128, NC, 6])
        mv_q = sb("mv_q", [128, NC, 2])
        sc_q = sb("sc_q", [128, 8, NC])
        part1 = sb("part1", [128, 2, NC, H * D], BF16)
        part2 = sb("part2", [128, 2, NC, H * D], BF16)
        rest = sb("rest", [128, 2, NC, H * D])
        stack = sb("stack", [128, 2, NC, H, PARTS * D], BF16)
        qk = [sb(f"qk{i}", [98, 2, H, N], BF16) for i in range(2)]
        vals = sb("vals", [128, NC, H, 32])
        negmax = sb("negmax", [128, H, NC])
        shift = sb("shift", [128, NC, 2, H], BF16)
        shiftT = sb("shiftT", [2 * H, N], BF16)
        probs = sb("probs", [128, 4, 2, NC, N])
        oT = sb("oT", [128, G, N])
        recip = sb("recip", [128, NC, H])
        o = sb("o", [128, NC, H, D])
        u_p = sb("u_p", [128, NC, C])
        r_p = sb("r_p", [128, NC, C])
        i_p = sb("i_p", [128, NC, C], BF16)
        iT_p = sb("iT_p", [96, KC, N], BF16)
        st_p = sb("st_p", [128, NC, 6])
        mv_p = sb("mv_p", [128, NC, 2])
        sc_p = sb("sc_p", [128, 8, NC])
        st_n = sb("st_n", [128, NC, 6])
        mv_n = sb("mv_n", [128, NC, 2])
        sc_n = sb("sc_n", [128, 2, NC])
        xn = sb("xn", [128, NC, C])
        xnT = [sb(f"xnT{i}", [96, KC, N]) for i in range(2)]
        hb = [sb(f"hb{i}", [128, NC, C]) for i in range(2)]
        hid = sb("hid", [128, NF, N])
        o_sb = sb("o_sb", [128, NC, C])

        clsT = sb("clsT", [96, KC, NCLS, B])
        aw1_sb = sb("aw1_sb", [96, NEXP, KC, HID])
        ab1_sb = sb("ab1_sb", [128, NEXP, NF])
        aw2_sb = sb("aw2_sb", [128, NEXP, NF, C])
        ab2_sb = sb("ab2_sb", [NEXP, C])
        flat1 = aw1_sb[:, :, :, :].rearrange("p e k n -> p (e k n)")
        flat2 = aw2_sb[:, :, :, :].rearrange("p e f n -> p (e f n)")
        n_x, n_w = B * 128, KC * 4 * C
        x1T = flat1[:, 0:n_x].rearrange("p (j b n) -> p j b n", j=2, b=B)
        x2T = flat1[:, n_x:2 * n_x].rearrange("p (j b n) -> p j b n", j=8, b=B)
        w_raw, w_rnd = (flat1[:, 2 * n_x + n_w * i:2 * n_x + n_w * (i + 1)].rearrange("p (k n) -> p k n", k=KC)
                        for i in range(2))
        n_g, n_z = B * P2 * 2, B // 2 * C
        gath1 = flat2[:, 0:n_g].rearrange("p (t n) -> p t n", t=8)
        gath2 = flat2[:, n_g:2 * n_g].rearrange("p (t n) -> p t n", t=2)
        z1 = flat2[:, 2 * n_g:2 * n_g + n_z].rearrange("p (a n) -> p a n", n=C)
        z2 = flat2[:, 2 * n_g + n_z:2 * n_g + n_z + B // 8 * C].rearrange("p (a n) -> p a n", n=C)
        gw_sb = sb("gw_sb", [96, KC, 2 * NCLS])
        sel = sb("sel", [NEXP, 2, NCLS, B])
        own = sb("own", [NCLS * B, 2, NCLS])
        flat3 = probs[:, :, :, :, :].rearrange("p s a c n -> p (s a c n)")
        w0_sb, w1_sb, w2_sb = flat3[0:64, 0:48], flat3[0:64, 48:240], flat3[0:64, 240:1008]
        wf_sb = flat3[0:64, 1008:1008 + 3 * C].rearrange("p (k n) -> p k n", k=3)
        b012_wide = flat3[0:64, 1600:1600 + 3 * 128].rearrange("p (k n) -> p k n", k=3)
        hat = flat3[:, 2000:2000 + NC * ZR].rearrange("p (c t) -> p c t", c=NC)
        zbias = flat3[:, 2200:2200 + C]
        n_e, n_p = NEXP * NF * NCLS * B, 2 * NF * 3 * B
        hexp = flat3[:, 0:n_e].rearrange("p (c f t) -> p c f t", c=NEXP, f=NF)
        hcls = flat3[0:NCLS * B, n_e + n_p:n_e + n_p + C]
        ocls = flat3[0:NCLS * B, n_e + n_p + C:n_e + n_p + 2 * C]
        hpre = flat3[:, n_e:n_e + n_p].rearrange("p (a f s b) -> p a f s b", a=2, f=NF, s=3)
        logit = sb("logit", [NCLS * B, 2, NCLS])
        gate = sb("gate", [NCLS * B, 16])

        PS = ctx.enter_context(nc.psum_tensor("PS", [128, 8, 512], F32))
        PSb = PS[:, :, :].bitcast(BF16)

        s_idx = sem("s_idx")
        s_pat = sem("s_pat")
        s_tw = sem("s_tw")
        s_aw = sem("s_aw")
        s_fw = sem("s_fw")
        s_ew = sem("s_ew")
        s_g0, s_g12 = sem("s_g0"), sem("s_g12")
        s_zero = sem("s_zero")
        s_id = sem("s_id")
        s_pool = sem("s_pool")
        s_vc = sem("s_vc")
        s_wsum = sem("s_wsum")
        s_bw = sem("s_bw")
        s_fps = sem("s_fps")
        s_fsb, s_zc = sem("s_fsb"), sem("s_zc")
        s_zall = sem("s_zall")
        s_wt = sem("s_wt")
        s_const = sem("s_const")
        W_STEPS, T_STEPS, Z_STEPS = 12, 20, 30
        s_carrier = sem("s_carrier")
        scores, maxed = sems("scores", U), sems("maxed", U)
        shift_hi, shift_done, shift_t, shift_c = sem("shift_hi"), sem("shift_done"), sem("shift_t"), sem("shift_c")
        shift_rows = sems("shift_rows", 2)
        scoresT, expd = sems("scoresT", U), sems("expd", U)
        pv, oT_done = sems("pv", G), sems("oT_done", G)
        f1, gelud, f2, out_done, stored = sems("f1", NF), sems("gelud", NF), sem("f2"), sems("out_done", NC), sems("stored", NC)
        tok_ready, tok_t, tok_c, h_ps, h_sb = sem("tok_ready"), sem("tok_t"), sem("tok_c"), sem("h_ps"), sem("h_sb")
        q_steps = sems("q_step", 10)
        q_pow, q_int, q_t, q_tc = sem("q_pow"), sem("q_int"), sem("q_t"), sem("q_tc")
        qk_ps, v_ps, v_sb = sems("qk_ps", NC), sem("v_ps"), sem("v_sb")
        p1_done, rest_done, p2_done, p3_done = (sems(n, 2) for n in ("p1_done", "rest_done", "p2_done", "p3_done"))
        dup_done = sem("dup_done")
        stk_t, stk_c = sems("stk_t", U), sems("stk_c", U)
        o_t, o_rec, o_sbd = sem("o_t"), sem("o_rec"), sem("o_sbd")
        p_steps = sems("p_step", 10)
        p_pow, p_int, p_t, p_tc, p_ps = sem("p_pow"), sem("p_int"), sem("p_t"), sem("p_tc"), sem("p_ps")
        n_steps, xn_done = sems("n_step", 5), sem("xn_done")
        n_pow, n_t, n_tc, hb_done, cls_done = sem("n_pow"), sem("n_t"), sem("n_tc"), sem("hb_done"), sem("cls_done")
        e_hcls, e_gate = sem("e_hcls"), sem("e_gate")
        e_h, e_b, e_g, e_fin, e_out = sem("e_h"), sem("e_b"), sem("e_g"), sem("e_fin"), sem("e_out")

        block = ctx.enter_context(nc.Block())

        class At:

            def __init__(self, eng, t, loop=None):
                self.t, self.eng, self.loop = t, eng, loop
                self.seen = {}

            def __call__(self, off):
                if self.loop is None:
                    return min(self.t + off, B)
                k = self.t + off
                if k not in self.seen:
                    self.seen[k] = self.eng.snap(self.loop + k)
                return self.seen[k]

        def wait(eng, s, count, by=1):
            if isinstance(count, int):
                if count > 0:
                    eng.wait_ge(s, by * count)
            else:
                eng.wait_ge(s, count * by if by != 1 else count)

        def wait_alone(eng, s, count, by=1):
            wait(eng, s, count, by)
            eng.sem_inc(s_carrier)

        LOOP, LAST = 4, B + 1

        def steps(eng, body):
            for t in range(-1, LOOP):
                body(At(eng, t), t, t % 2)
            with eng.Fori(LOOP, B - 2, 2) as i:
                seen = {}
                for p in range(2):
                    at = At(eng, p, i)
                    at.seen = seen
                    body(at, LOOP, p)
            for t in range(B - 2, LAST + 1):
                body(At(eng, t), t, t % 2)

        def has(t):
            return 0 <= t < B, t + 1 < B, 1 <= t <= B, t >= 2

        def third_part(eng, side):
            slot = (5, 2)[side]
            return eng.tensor_tensor(stack[:, side, :, :, D * slot:D * (slot + 1)],
                                     rest[:, side, :, :].rearrange("p c (h d) -> p c h d", d=D),
                                     part2[:, side, :, :].rearrange("p c (h d) -> p c h d", d=D), ALU.subtract)

        STACK_BANK = (5, 0, 1, 2, 3, 7)
        BY_ACT = (1, 4)
        QK_BANK = (5, 7)

        @block.sync
        def _(sp):
            sp.dma_start(idx2_sb[:, :], idx2).then_inc(s_idx, 16)
            sp.dma_start(idx1_sb[:, :], idx1).then_inc(s_idx, 16)
            sp.dma_start(idx0_sb[:, :], idx0).then_inc(s_idx, 16)
            for dst, src in ((w0_sb, w0), (w1_sb, w1), (w2_sb, w2), (wf_sb, wf),
                             (b012_sb[:, :], b012), (bf_sb[:, :], bf)):
                sp.dma_start(dst, src).then_inc(s_tw, 16)
            sp.dma_start(w_raw[:, :, 0:3 * C], wqkv).then_inc(s_aw, 16)
            sp.dma_start(w_raw[:, :, 3 * C:4 * C], wproj).then_inc(s_aw, 16)
            sp.dma_start(gq_sb[:, :], gqkv.broadcast_to([128, C])).then_inc(s_aw, 16)
            sp.dma_start(gp_sb[:, :], gproj.broadcast_to([128, C])).then_inc(s_aw, 16)
            sp.dma_start(mb2_sb[:, :], mb2.broadcast_to([128, C])).then_inc(s_aw, 16)
            sp.wait_ge(s_fsb, 1)
            for b in range(B):
                sp.dma_start(zall[ZR:128, b, :], fused[0:48, 0, :]).then_inc(s_zall, 16)
            sp.dma_start(mw1_sb[:, :, :], mw1).then_inc(s_fw, 16)
            sp.dma_start(mb1_sb[:, :], mb1).then_inc(s_fw, 16)
            sp.dma_start(mw2_sb[:, :, :], mw2).then_inc(s_fw, 16)
            sp.wait_ge(s_zc, 8)
            zpair = zall[0:T1, :, :].rearrange("p (a e) n -> p a e n", e=2)
            for e in range(2):
                sp.dma_start(zpair[:, :, e, :], z1[T1 * e:T1 * (e + 1), :, :]).then_inc(s_zall, 16)
            sp.wait_ge(s_zc, 10)
            zoct = zall[T1:ZR, :, :].rearrange("p (a e) n -> p a e n", e=8)
            for e in range(8):
                sp.dma_start(zoct[:, :, e, :], z2[T2 * e:T2 * (e + 1), :, :]).then_inc(s_zall, 16)
            sp.wait_ge(s_wt, 8)
            sp.wait_ge(s_fps, Z_STEPS)
            sp.wait_ge(s_zall, 16 * (B + 10))
            sp.dma_start(aw1_sb[:, :, :, :], aw1).then_inc(s_ew, 16)
            sp.dma_start(aw2_sb[:, :, :, :], aw2).then_inc(s_ew, 16)
            sp.dma_start(ab1_sb[:, :, :], ab1).then_inc(s_ew, 16)
            sp.dma_start(ab2_sb[:, :], ab2).then_inc(s_ew, 16)
            sp.dma_start(gw_sb[:, :, :], gw).then_inc(s_ew, 16)

            def body(at, t, par):
                attn, front, back, ffn = has(t)
                if attn:
                    wait_alone(sp, shift_c, at(1))
                    wait_alone(sp, scoresT[U - 1], at(-1))
                    for r in range(2):
                        sp.dma_start(qk[par][96 + r:97 + r, 0, :, :], shiftT[H * r:H * (r + 1), :])\
                          .then_inc(shift_rows[r], 16)
                if ffn:
                    img = at(-2)
                    wait_alone(sp, out_done[0], at(-1))
                    sp.dma_start(out[bass.ds(img, 1), NCLS:128, :].rearrange("a p n -> p a n"), o_sb[NCLS:128, 0:1, :])\
                      .then_inc(stored[0], 16)
                    wait_alone(sp, out_done[1], at(-1))
                    sp.dma_start(out[bass.ds(img, 1), 128:N, :].rearrange("a p n -> p a n"), o_sb[:, 1:2, :])\
                      .then_inc(stored[1], 16)

            steps(sp, body)
            sp.wait_ge(n_steps[1], B)
            sp.wait_ge(pv[G - 1], B)
            for i in range(NCLS):
                sp.dma_start(hcls[B * i:B * (i + 1), :], h_all[i:i + 1, :, 0, :]).then_inc(e_hcls, 16)
            sp.wait_ge(e_fin, 2)
            for i in range(NCLS):
                sp.dma_start(out[:, i, :], ocls[B * i:B * (i + 1), :]).then_inc(e_out, 16)
            sp.wait_ge(stored[0], 16 * B)
            sp.wait_ge(stored[1], 16 * B)
            sp.wait_ge(e_out, 16 * NCLS)

        @block.gpsimd
        def _(pool):
            pool.wait_ge(s_idx, 48)
            for t in range(2):
                pool.indirect_dma_start(gath2[:, t, :], None, x2, bass.IndirectOffsetOnAxis(idx2_sb[:, t:t + 1], 0))\
                    .then_inc(s_g12, 16)
            for t in range(8):
                pool.indirect_dma_start(gath1[:, t, :], None, x1, bass.IndirectOffsetOnAxis(idx1_sb[:, t:t + 1], 0))\
                    .then_inc(s_g12, 16)
            pool.memset(ident[:, :], 0.0).then_inc(s_zero, 1)
            pool.memset(identb[:, :], 0.0).then_inc(s_zero, 1)
            pool.wait_ge(s_zero, 2)
            for m in (ident, identb):
                pool.affine_select(out=m[:, :], in_=m[:, :], compare_op=ALU.not_equal, fill=1.0, base=0,
                                   pattern=[[-1, 128]], channel_multiplier=1).then_inc(s_id, 1)
            pool.iota(hat[:, :, 0:T1], pattern=[[0, NC], [1, T1]], base=0, channel_multiplier=0,
                      allow_small_or_imprecise_dtypes=True).then_inc(s_pool, 1)
            pool.iota(hat[:, :, T1:ZR], pattern=[[0, NC], [1, T2]], base=0, channel_multiplier=0,
                      allow_small_or_imprecise_dtypes=True).then_inc(s_pool, 1)
            pool.iota(pos[:, :, :], pattern=[[0, 2], [128, NC]], base=0, channel_multiplier=1,
                      allow_small_or_imprecise_dtypes=True).then_inc(s_pool, 1)
            for j in range(NC * GP):
                pool.indirect_dma_start(gath0[:, j // GP, j % GP, :], None, x0,
                                        bass.IndirectOffsetOnAxis(idx0_sb[:, j:j + 1], 0)).then_inc(s_g0, 16)
            pool.memset(own[:, :, :], 1.0).then_inc(s_zero, 1)
            pool.wait_ge(s_zero, 3)
            pool.affine_select(out=own[:, :, :], in_=own[:, :, :], compare_op=ALU.is_ge, fill=0.0, base=0,
                               pattern=[[0, 2], [-B, NCLS]], channel_multiplier=1).then_inc(s_zero, 1)
            pool.wait_ge(s_zero, 4)
            pool.affine_select(out=own[:, :, :], in_=own[:, :, :], compare_op=ALU.is_ge, fill=0.0, base=B - 1,
                               pattern=[[0, 2], [B, NCLS]], channel_multiplier=-1).then_inc(s_const, 1)
            pool.memset(sel[:, :, :, :], 0.0).then_inc(s_zero, 1)
            pool.wait_ge(s_zero, 5)
            pool.affine_select(out=sel[:, 0, :, :].rearrange("p (l s) b -> p l s b", s=2),
                               in_=sel[:, 0, :, :].rearrange("p (l s) b -> p l s b", s=2),
                               compare_op=ALU.not_equal, fill=1.0, base=-3,
                               pattern=[[0, 3], [-1, 2], [0, B]], channel_multiplier=1).then_inc(s_const, 1)
            pool.affine_select(out=sel[:, 1, :, :].rearrange("p (l s) b -> p l s b", s=2),
                               in_=sel[:, 1, :, :].rearrange("p (l s) b -> p l s b", s=2),
                               compare_op=ALU.not_equal, fill=1.0, base=0,
                               pattern=[[-1, 3], [0, 2], [0, B]], channel_multiplier=1).then_inc(s_const, 1)
            pool.wait_ge(s_g0, 16 * NC * GP)

            def body(at, t, par):
                attn, front, back, ffn = has(t)
                if front:
                    wait(pool, tok_t, at(1))
                    if t == -1:
                        pool.wait_ge(s_vc, 6)
                    src = gath0[:, :, :, bass.ds(at(1) * P0, P0)]
                    pool.tensor_copy(tok_in[:, :, ZR:128].rearrange("p c (j k) -> p c j k", k=P0), src)\
                        .then_inc(tok_ready, 1)
                if front:
                    wait(pool, q_steps[1], at(2))
                    pool.tensor_tensor(sc_q[:, 1, :], sc_q[:, 0, :], neg_half[:, :], ALU.pow).then_inc(q_pow, 1)
                if back:
                    wait(pool, p_steps[1], at(0))
                    pool.tensor_tensor(sc_p[:, 1, :], sc_p[:, 0, :], neg_half[:, :], ALU.pow).then_inc(p_pow, 1)
                if front:
                    wait(pool, q_steps[7], at(2))
                    wait_alone(pool, q_t, at(1))
                    pool.tensor_scalar(i_q[:, :, :], r_q[:, :, :], -MAGIC, 1.0, ALU.add, ALU.mult).then_inc(q_int, 1)
                if back:
                    wait(pool, p_steps[7], at(0))
                    wait_alone(pool, p_t, at(-1))
                    pool.tensor_scalar(i_p[:, :, :], r_p[:, :, :], -MAGIC, 1.0, ALU.add, ALU.mult).then_inc(p_int, 1)
                if front:
                    for c in range(NC):
                        wait(pool, rest_done[c], at(2))
                        if c == 0:
                            wait(pool, dup_done, at(1))
                        wait_alone(pool, stk_t[U - 1], at(1))
                        pool.tensor_scalar(part2[:, :, c, :], rest[:, :, c, :], 1.0, 0.0, ALU.mult, ALU.add)\
                            .then_inc(p2_done[c], 1)
                if back:
                    wait(pool, n_steps[2], at(0))
                    pool.tensor_tensor(sc_n[:, 1, :], sc_n[:, 0, :], neg_half[:, :], ALU.pow).then_inc(n_pow, 1)
                if front:
                    wait(pool, p2_done[0], at(2))
                    wait(pool, p2_done[1], at(2))
                    third_part(pool, 0).then_inc(p3_done[0], 1)
                if back:
                    wait(pool, out_done[1], at(-2))
                    hrow = h_all[:, bass.ds(at(-1), 1), :, :].rearrange("p a c n -> p (a c) n")
                    pool.tensor_tensor(hb[1 - par][:, :, :], hrow,
                                       mb2_sb[:, :].unsqueeze(1).broadcast_to([128, NC, C]), ALU.add).then_inc(hb_done, 1)
                    wait(pool, n_tc, at(0))
                    pool.tensor_copy(clsT[:, :, :, bass.ds(at(-1), 1)].rearrange("p k i a -> p k (i a)"),
                                     xnT[1 - par][:, :, 0:NCLS]).then_inc(cls_done, 1)

            steps(pool, body)
            pool.wait_ge(pv[G - 1], B)
            pool.memset(hexp[:, :, :, :], 0.0).then_inc(s_const, 1)

        @block.scalar
        def _(act):
            def body(at, t, par):
                attn, front, back, ffn = has(t)

                def gelu(f):
                    if ffn:
                        wait(act, f1[f], at(-1))
                        if f == 0:
                            wait(act, f2, at(-2))
                        nc.scalar.activation(hid[:, f, :], PS[:, 4 + f % 2, 0:N], ACT.Gelu, bias=mb1_sb[:, f:f + 1])\
                            .then_inc(gelud[f], 1)

                def exp(u):
                    if attn:
                        wait(act, scoresT[u], at(1))
                        if u == 0:
                            wait(act, pv[G - 1], at(0))
                        if u >= 4:
                            wait(act, pv[0], at(1))
                        nc.scalar.activation(probs[:, u % 4, :, :, :].rearrange("p a c n -> p (a c n)"),
                                             PS[:, 2 * (u % 2):2 * (u % 2) + 2, :].rearrange("p a n -> p (a n)"),
                                             ACT.Exp, scale=float(D) ** -0.5).then_inc(expd[u], 1)

                def out_t(g):
                    if attn:
                        wait(act, pv[g], at(1))
                        if g == 0:
                            wait(act, o_t, at(0))
                        nc.scalar.copy(oT[:, g, :], PS[:, 6, 0:N]).then_inc(oT_done[g], 1)

                for f in range(3):
                    gelu(f)
                if front:
                    wait(act, tok_t, at(2))
                    wait(act, h_ps, at(1))
                    nc.scalar.copy(tok_inT[:, :], PS[:, 7, 0:N]).then_inc(tok_c, 1)
                gelu(3)
                gelu(4)
                if front:
                    wait_alone(act, h_ps, at(2))
                    nc.scalar.copy(h_all[:, bass.ds(at(1), 1), :, :].rearrange("p a c n -> p (a c n)"), PS[:, 7, 0:NC * C])\
                        .then_inc(h_sb, 1)
                gelu(5)
                if attn:
                    wait(act, shift_t, at(1))
                    wait(act, shift_rows[0], at(0), 16)
                    wait(act, shift_rows[1], at(0), 16)
                    nc.scalar.copy(shiftT[:, :], PSb[0:2 * H, 7, 0:N]).then_inc(shift_c, 1)
                if front:
                    wait(act, q_t, at(2))
                    wait(act, v_ps, at(1))
                    nc.scalar.copy(iT_q[:, :, :].rearrange("p k n -> p (k n)"), PSb[0:96, 7, 0:2 * N]).then_inc(q_tc, 1)
                exp(0)
                exp(1)
                if front:
                    for c in range(NC):
                        wait(act, qk_ps[c], at(2))
                        if c == 0:
                            wait(act, dup_done, at(1))
                            wait(act, q_steps[6], at(2))
                        nc.scalar.activation(part1[:, :, c, :], PS[:, QK_BANK[c], 0:2 * C].rearrange("p (s n) -> p s n", s=2),
                                             ACT.Copy, scale=sc_q[:, 6, c:c + 1]).then_inc(p1_done[c], 1)
                exp(2)
                if back:
                    wait(act, p_t, at(0))
                    wait(act, p_ps, at(-1))
                    nc.scalar.copy(iT_p[:, :, :].rearrange("p k n -> p (k n)"), PSb[0:96, 4, 0:2 * N]).then_inc(p_tc, 1)
                exp(3)
                out_t(0)
                exp(4)
                out_t(1)
                exp(5)
                out_t(2)
                if back:
                    wait(act, n_t, at(0))
                    wait(act, f1[NF - 1], at(-2))
                    wait(act, cls_done, at(-2))
                    nc.scalar.copy(xnT[1 - par][:, :, :].rearrange("p k n -> p (k n)"), PS[0:96, 4, :]).then_inc(n_tc, 1)
                if front:
                    wait(act, v_ps, at(2))
                    wait(act, pv[G - 1], at(1))
                    for c in range(NC):
                        last = nc.scalar.activation(vals[:, c, :, 0:D],
                                                    PS[:, 4, C * c:C * (c + 1)].rearrange("p (h d) -> p h d", d=D),
                                                    ACT.Copy, scale=sc_q[:, 6, c:c + 1])
                    last.then_inc(v_sb, 1)
                    for w in BY_ACT:
                        wait(act, stk_t[w], at(2))
                        nc.scalar.copy(qk[1 - par][0:96, :, 2 * w:2 * w + 2, :].rearrange("p s h n -> p s (h n)"),
                                       PSb[0:96, STACK_BANK[w], :].rearrange("p (s n) -> p s n", s=2)).then_inc(stk_c[w], 1)

            for k in range(11):
                act.wait_ge(s_fps, k + 1)
                nrow = GP * P0 if k == 0 else 96
                nc.scalar.copy(fused[0:nrow, k, :], PS[0:nrow, k % 8, 0:C]).then_inc(s_fsb, 1)
            for k in range(8):
                act.wait_ge(s_fps, W_STEPS + k + 1)
                dst = (x2T if k < 4 else x1T)[:, :, 4 * (k % 4):4 * (k % 4) + 4, :]
                src = PS[0:96, k, :].rearrange("p (b j n) -> p j b n", b=4, j=8 if k < 4 else 2)
                nc.scalar.copy(dst, src).then_inc(s_fsb, 1)
            act.wait_ge(s_fw, 48)
            steps(act, body)

            act.wait_ge(s_const, 4)
            for a in range(NEXP):
                act.wait_ge(e_b, a + 1)
                if a < 3:
                    view = hexp[:, 3:5, :, :].rearrange("p c f (l s b) -> p c s f l b", l=3, s=2)
                    for s in range(2):
                        last = nc.scalar.activation(view[:, s, s, :, a, :], hpre[:, a % 2, :, s, :], ACT.Gelu)
                else:
                    view = hexp[:, 0:3, :, :].rearrange("p c f (l s b) -> p c l s f b", l=3, s=2)
                    for l in range(3):
                        last = nc.scalar.activation(view[:, l, l, a - 3, :, :], hpre[:, a % 2, :, l, :], ACT.Gelu)
                last.then_inc(e_g, 1)
            act.wait_ge(e_gate, 4)
            nc.scalar.activation(gate[:, 3:5], gate[:, 3:5], ACT.Exp).then_inc(e_gate, 1)

        @block.vector
        def _(dve):
            V = nc.vector
            V.memset(ones[:, :], 1.0).then_inc(s_bw, 1)
            V.memset(neg_half[:, :], -0.5)
            for q in qk:
                V.memset(q[96:98, 1, :, :], 1.0)
            V.memset(vals[:, :, :, D:32], 0.0).then_inc(s_vc, 1)
            dve.wait_ge(s_vc, 1)
            V.memset(vals[:, :, :, D:D + 1], 1.0).then_inc(s_bw, 1)
            dve.wait_ge(s_tw, 96)
            dve.wait_ge(s_bw, 2)
            V.tensor_copy(b012_wide[:, :, :], b012_sb[:, :].unsqueeze(2).broadcast_to([64, 3, 128])).then_inc(s_bw, 1)
            dve.wait_ge(s_g12, 160)
            V.tensor_copy(pat2.rearrange("p b (t n) -> p b t n", t=2), gath2.rearrange("p t (b n) -> p b t n", b=B))\
             .then_inc(s_pat, 1)
            V.tensor_copy(pat1.rearrange("p b (t n) -> p b t n", t=8), gath1.rearrange("p t (b n) -> p b t n", b=B))\
             .then_inc(s_pat, 1)
            dve.wait_ge(s_aw, 80)
            for k, (a, b) in enumerate(((0, 3 * C), (3 * C, 4 * C))):
                last = V.tensor_reduce(wabs[:, k:k + 1], w_raw[:, :, a:b], AX.XY, ALU.add, apply_absolute_value=True)
            last.then_inc(s_wsum, 1)
            dve.wait_ge(s_wsum, 2)
            V.tensor_scalar(wscale[:, 0:1], PS[:, 7, 0:1], 1.0 / (3 * C * C), EPS, ALU.mult, ALU.max)
            V.tensor_scalar(wscale[:, 1:2], PS[:, 7, 1:2], 1.0 / (C * C), EPS, ALU.mult, ALU.max).then_inc(s_wt, 1)
            dve.wait_ge(s_wt, 1)
            V.reciprocal(wscale[:, 2:4], wscale[:, 0:2]).then_inc(s_wt, 1)
            V.tensor_scalar(wsq[:, :], wscale[:, 0:2], 1.0 / QMAX, None, ALU.mult).then_inc(s_wt, 1)
            dve.wait_ge(s_wt, 3)
            for k, (a, b) in enumerate(((0, 3 * C), (3 * C, 4 * C))):
                V.tensor_scalar(w_rnd[:, :, a:b], w_raw[:, :, a:b], wscale[0:96, 2 + k:3 + k], MAGIC, ALU.mult, ALU.add)\
                 .then_inc(s_wt, 1)
            dve.wait_ge(s_wt, 5)
            V.tensor_scalar(w_raw[:, :, :], w_rnd[:, :, :], -MAGIC, 1.0, ALU.add, ALU.min).then_inc(s_wt, 1)
            dve.wait_ge(s_wt, 6)
            V.tensor_scalar(wq[:, :, :], w_raw[:, :, 0:3 * C], -1.0, None, ALU.max).then_inc(s_wt, 1)
            V.tensor_scalar(wp[:, :, :], w_raw[:, :, 3 * C:4 * C], -1.0, None, ALU.max).then_inc(s_wt, 1)
            dve.wait_ge(s_fps, W_STEPS)
            V.tensor_copy(zbias[:, :], PS[:, 3, 0:C]).then_inc(s_vc, 1)
            dve.wait_ge(s_pool, 3)
            for lev, n_in in enumerate((T1, T2)):
                last = V.tensor_scalar(pos[:, lev, :], pos[:, lev, :], n_in / N, 0.5 * n_in / N - 0.5, ALU.mult, ALU.add)
            last.then_inc(s_vc, 1)
            dve.wait_ge(s_vc, 3)
            for lev, n_in in enumerate((T1, T2)):
                last = V.tensor_scalar(pos[:, lev, :], pos[:, lev, :], 0.0, float(n_in - 1), ALU.max, ALU.min)
            last.then_inc(s_vc, 1)
            dve.wait_ge(s_vc, 4)
            for lev, (a, b) in enumerate(((0, T1), (T1, ZR))):
                for c in range(NC):
                    last = V.tensor_scalar(hat[:, c, a:b], hat[:, c, a:b], pos[:, lev, c:c + 1], None, ALU.subtract)
            last.then_inc(s_bw, 1)
            dve.wait_ge(s_bw, 4)
            V.scalar_tensor_tensor(hat[:, :, :], hat[:, :, :], -1.0, hat[:, :, :], ALU.mult, ALU.max).then_inc(s_vc, 1)
            dve.wait_ge(s_vc, 5)
            V.tensor_scalar(hat[:, :, :], hat[:, :, :], -1.0, 1.0, ALU.mult, ALU.add).then_inc(s_bw, 1)
            dve.wait_ge(s_bw, 5)
            V.tensor_scalar(tok_in[:, :, 0:ZR], hat[:, :, :], 0.0, None, ALU.max).then_inc(s_vc, 1)
            for k in range(10):
                dve.wait_ge(s_fps, T_STEPS + k + 1)
                if k < 8:
                    V.tensor_tensor(z1[:, k, :], PS[:, k, 0:C], zbias[:, :], ALU.add).then_inc(s_zc, 1)
                else:
                    V.tensor_copy(z2[:, k - 8, :], PS[:, k - 8, 0:C]).then_inc(s_zc, 1)

            def quantise(k, stp, sc, u, r, w):
                V.tensor_tensor(sc[:, 3, :], sc[:, 2, :], sc[:, 1, :], ALU.mult).then_inc(stp[3], 1)
                wait(dve, stp[3], k)
                V.tensor_scalar(sc[:, 3, :], sc[:, 3, :], EPS, None, ALU.max).then_inc(stp[4], 1)
                wait(dve, stp[4], k)
                V.reciprocal(sc[:, 4, :], sc[:, 3, :]).then_inc(stp[5], 1)
                wait(dve, stp[5], k)
                V.tensor_scalar(sc[:, 6, :], sc[:, 3, :], w, None, ALU.mult)
                V.scalar_tensor_tensor(sc[:, 5, :], sc[:, 4, :], QMAX, sc[:, 1, :], ALU.mult, ALU.mult).then_inc(stp[6], 1)
                wait(dve, stp[6], k)
                for c in range(NC):
                    last = V.tensor_scalar(r[:, c, :], u[:, c, :], sc[:, 5, c:c + 1], MAGIC, ALU.mult, ALU.add)
                last.then_inc(stp[7], 1)

            def body(at, t, par):
                attn, front, back, ffn = has(t)

                def row_max(u):
                    if attn:
                        wait(dve, scores[u], at(1))
                        if u == 0:
                            wait(dve, shift_done, at(0))
                        V.tensor_reduce(negmax[:, 2 * u:2 * u + 2, :],
                                        PS[:, 2 * (u % 2):2 * (u % 2) + 2, :].rearrange("p a (c n) -> p a c n", c=NC),
                                        AX.X, ALU.max, negate=True).then_inc(maxed[u], 1)

                for u in range(U):
                    row_max(u)
                if attn:
                    wait(dve, maxed[U - 1], at(1))
                    wait(dve, shift_t, at(0))
                    hi = shift[:, :, 0, :].rearrange("p c h -> p h c")
                    lo = shift[:, :, 1, :].rearrange("p c h -> p h c")
                    V.tensor_copy(hi, negmax[:, :, :]).then_inc(shift_hi, 1)
                    wait(dve, shift_hi, at(1))
                    V.tensor_tensor(lo, negmax[:, :, :], hi, ALU.subtract).then_inc(shift_done, 1)
                if front:
                    hn = h_all[:, bass.ds(at(1), 1), :, :].rearrange("p a c n -> p (a c) n")
                    wait_alone(dve, h_sb, at(2))
                    for c in range(NC):
                        last = V.bn_stats(st_q[:, c, :], hn[:, c, :])
                    last.then_inc(q_steps[8], 1)
                if back:
                    wait(dve, o_t, at(0))
                    ov = PS[:, 4:6, 0:128 * G].rearrange("p c (h e) -> p c h e", e=32)
                    V.reciprocal(recip[:, :, :], ov[:, :, :, D]).then_inc(o_rec, 1)
                if front:
                    wait_alone(dve, q_steps[8], at(2))
                    for c in range(NC):
                        last = V.bn_aggr(mv_q[:, c, :], st_q[:, c, :])
                    last.then_inc(q_steps[0], 1)
                if back:
                    wait(dve, o_rec, at(0))
                    V.tensor_tensor(o[:, :, :, :], ov[:, :, :, 0:D],
                                    recip[:, :, :].unsqueeze(3).broadcast_to([128, NC, H, D]), ALU.mult).then_inc(o_sbd, 1)
                if front:
                    wait(dve, q_steps[0], at(2))
                    wait(dve, v_sb, at(1))
                    V.tensor_scalar(sc_q[:, 0, :], mv_q[:, :, 1], 1.0 + EPS, EPS * EPS, ALU.mult, ALU.add)\
                        .then_inc(q_steps[1], 1)
                    for c in range(NC):
                        last = V.scalar_tensor_tensor(u_q[:, c, :], hn[:, c, :], mv_q[:, c, 0:1], gq_sb[:, :],
                                                      ALU.subtract, ALU.mult)
                    last.then_inc(q_steps[2], 1)
                if back:
                    of = o[:, :, :, :].rearrange("p c h d -> p c (h d)")
                    wait_alone(dve, o_sbd, at(0))
                    for c in range(NC):
                        last = V.bn_stats(st_p[:, c, :], of[:, c, :])
                    last.then_inc(p_steps[8], 1)
                if front:
                    wait(dve, q_steps[2], at(2))
                    V.tensor_reduce(sc_q[:, 2, :], u_q[:, :, :], AX.X, ALU.max, apply_absolute_value=True).then_inc(q_steps[9], 1)
                if back:
                    wait_alone(dve, p_steps[8], at(0))
                    for c in range(NC):
                        last = V.bn_aggr(mv_p[:, c, :], st_p[:, c, :])
                    last.then_inc(p_steps[9], 1)
                if front:
                    wait(dve, q_steps[9], at(2))
                    wait(dve, q_pow, at(2))
                    wait(dve, q_int, at(1))
                    quantise(at(2), q_steps, sc_q, u_q, r_q, wsq[:, 0:1])
                if back:
                    wait(dve, p_steps[9], at(0))
                    V.tensor_tensor(sc_p[:, 7, :], mv_p[:, :, 0], mv_p[:, :, 0], ALU.mult).then_inc(p_steps[0], 1)
                    wait(dve, p_steps[0], at(0))
                    V.scalar_tensor_tensor(sc_p[:, 0, :], sc_p[:, 7, :], EPS, mv_p[:, :, 1], ALU.add, ALU.add)\
                        .then_inc(p_steps[1], 1)
                    V.tensor_tensor(u_p[:, :, :], of, gp_sb[:, :].unsqueeze(1).broadcast_to([128, NC, C]), ALU.mult)\
                        .then_inc(p_steps[2], 1)
                    wait(dve, p_steps[2], at(0))
                    V.tensor_reduce(sc_p[:, 2, :], u_p[:, :, :], AX.X, ALU.max, apply_absolute_value=True).then_inc(n_steps[0], 1)
                    wait(dve, n_steps[0], at(0))
                    wait(dve, p_pow, at(0))
                    wait(dve, p_int, at(-1))
                    quantise(at(0), p_steps, sc_p, u_p, r_p, wsq[:, 1:2])
                if ffn:
                    for c in range(NC):
                        if c == 0:
                            wait(dve, f2, at(-1))
                            wait(dve, hb_done, at(-1))
                        wait(dve, stored[c], at(-2), 16)
                        V.tensor_tensor(o_sb[:, c, :], PS[:, 6, C * c:C * (c + 1)], hb[par][:, c, :], ALU.add)\
                         .then_inc(out_done[c], 1)
                if front:
                    for c in range(NC):
                        wait(dve, p1_done[c], at(2))
                        if c == 0:
                            wait(dve, p3_done[0], at(1))
                        V.scalar_tensor_tensor(rest[:, :, c, :], PS[:, QK_BANK[c], 0:2 * C].rearrange("p (s n) -> p s n", s=2),
                                               sc_q[:, 6, c:c + 1], part1[:, :, c, :], ALU.mult, ALU.subtract)\
                            .then_inc(rest_done[c], 1)
                    wait(dve, stk_t[U - 1], at(1))

                    def dup(side, part, first, last_, step):
                        src = part[:, side, :, :].rearrange("p c (h d) -> p (c h) d", d=D)
                        dst = stack[:, side, :, :, :].rearrange("p c h (s d) -> p (c h) s d", d=D)[:, :, first:last_:step, :]
                        n = len(range(first, last_, step))
                        return V.tensor_copy(dst, src.unsqueeze(2).broadcast_to([128, NC * H, n, D]))

                    dup(0, part1, 0, 3, 1)
                    dup(1, part1, 0, 1, 1)
                    dup(1, part1, 3, 6, 2)
                    wait(dve, p2_done[0], at(2))
                    wait(dve, p2_done[1], at(2))
                    third_part(V, 1).then_inc(p3_done[1], 1)
                    dup(0, part2, 3, 5, 1)
                    dup(1, part2, 1, 5, 3).then_inc(dup_done, 1)
                if back:
                    wait(dve, p_ps, at(0))
                    hr = h_all[:, bass.ds(at(-1), 1), :, :].rearrange("p a c n -> p (a c) n")
                    for c in range(NC):
                        last = V.scalar_tensor_tensor(hr[:, c, :], PS[:, 4, C * c:C * (c + 1)], sc_p[:, 6, c:c + 1],
                                                      hr[:, c, :], ALU.mult, ALU.add)
                    last.then_inc(n_steps[1], 1)
                    wait_alone(dve, n_steps[1], at(0))
                    for c in range(NC):
                        last = V.bn_stats(st_n[:, c, :], hr[:, c, :])
                    last.then_inc(n_steps[3], 1)
                    wait_alone(dve, n_steps[3], at(0))
                    for c in range(NC):
                        last = V.bn_aggr(mv_n[:, c, :], st_n[:, c, :])
                    last.then_inc(n_steps[4], 1)
                    wait(dve, n_steps[4], at(0))
                    V.tensor_scalar(sc_n[:, 0, :], mv_n[:, :, 1], EPS, None, ALU.add).then_inc(n_steps[2], 1)
                    wait(dve, n_pow, at(0))
                    wait(dve, n_t, at(-1))
                    for c in range(NC):
                        last = V.tensor_scalar(xn[:, c, :], hr[:, c, :], mv_n[:, c, 0:1], sc_n[:, 1, c:c + 1],
                                               ALU.subtract, ALU.mult)
                    last.then_inc(xn_done, 1)
                if front:
                    for w in range(U):
                        if w not in BY_ACT:
                            wait(dve, stk_t[w], at(2))
                            V.tensor_copy(qk[1 - par][0:96, :, 2 * w:2 * w + 2, :].rearrange("p s h n -> p s (h n)"),
                                          PSb[0:96, STACK_BANK[w], :].rearrange("p (s n) -> p s n", s=2)).then_inc(stk_c[w], 1)

            steps(dve, body)

            dve.wait_ge(e_h, 1)
            dve.wait_ge(s_const, 3)
            V.tensor_tensor(logit[:, :, :], PS[0:NCLS * B, 7, 0:2 * NCLS].rearrange("p (i e) -> p e i", e=2), own[:, :, :],
                            ALU.mult).then_inc(e_gate, 1)
            dve.wait_ge(e_gate, 1)
            V.tensor_reduce(gate[:, 0:2], logit[:, :, :], AX.X, ALU.add).then_inc(e_gate, 1)
            dve.wait_ge(e_gate, 2)
            V.tensor_reduce(gate[:, 2:3], gate[:, 0:2], AX.X, ALU.max).then_inc(e_gate, 1)
            dve.wait_ge(e_gate, 3)
            V.tensor_scalar(gate[:, 3:5], gate[:, 0:2], gate[:, 2:3], None, ALU.subtract).then_inc(e_gate, 1)

            def expert_bias(a):
                dve.wait_ge(e_h, a + 2)
                if a >= 2:
                    dve.wait_ge(e_g, a - 1)
                pair = 2 * (a % 3)
                for half in range(2):
                    src = PS[:, pair + half, 0:3 * NCLS * B]
                    if a < 3:
                        src = src.rearrange("p (f l s b) -> p f l s b", f=3, l=3, s=2)[:, :, a, :, :]
                        n = 2
                    else:
                        src = src.rearrange("p (f l s b) -> p f l s b", f=3, l=3, s=2)[:, :, :, a - 3, :]
                        n = 3
                    bias = ab1_sb[:, a, 3 * half:3 * half + 3].unsqueeze(2).unsqueeze(3).broadcast_to([128, 3, n, B])
                    last = V.tensor_tensor(hpre[:, a % 2, 3 * half:3 * half + 3, 0:n, :], src, bias, ALU.add)
                last.then_inc(e_b, 1)

            dve.wait_ge(pv[G - 1], B)
            for a in range(NEXP):
                expert_bias(a)
            dve.wait_ge(e_gate, 5)
            V.tensor_reduce(gate[:, 5:6], gate[:, 3:5], AX.X, ALU.add).then_inc(e_gate, 1)
            dve.wait_ge(e_gate, 6)
            V.reciprocal(gate[:, 6:7], gate[:, 5:6]).then_inc(e_gate, 1)
            dve.wait_ge(e_gate, 7)
            V.tensor_scalar(gate[:, 7:9], gate[:, 3:5], gate[:, 6:7], None, ALU.mult).then_inc(e_gate, 1)
            dve.wait_ge(e_gate, 8)
            V.tensor_reduce(gate[:, 9:10], gate[:, 7:9], AX.X, ALU.min).then_inc(e_gate, 1)
            dve.wait_ge(e_gate, 9)
            V.scalar_tensor_tensor(gate[:, 10:12], gate[:, 7:9], gate[:, 9:10], gate[:, 7:9], ALU.is_gt, ALU.mult).then_inc(e_gate, 1)
            dve.wait_ge(e_gate, 10)
            V.tensor_reduce(gate[:, 12:13], gate[:, 10:12], AX.X, ALU.add).then_inc(e_gate, 1)
            dve.wait_ge(e_gate, 11)
            V.tensor_scalar(gate[:, 12:13], gate[:, 12:13], 1e-6, None, ALU.max).then_inc(e_gate, 1)
            dve.wait_ge(e_gate, 12)
            V.reciprocal(gate[:, 13:14], gate[:, 12:13]).then_inc(e_gate, 1)
            dve.wait_ge(e_gate, 13)
            V.tensor_scalar(gate[:, 14:16], gate[:, 10:12], gate[:, 13:14], None, ALU.mult).then_inc(e_gate, 1)
            dve.wait_ge(e_gate, 14)
            dve.wait_ge(e_hcls, 16 * NCLS)
            dve.wait_ge(e_h, NEXP + 2)
            V.scalar_tensor_tensor(ocls[:, :], PS[0:NCLS * B, 6, 0:C], gate[:, 14:15], hcls[:, :], ALU.mult, ALU.add)\
             .then_inc(e_fin, 1)
            dve.wait_ge(e_fin, 1)
            dve.wait_ge(e_h, NEXP + 3)
            V.scalar_tensor_tensor(ocls[:, :], PS[0:NCLS * B, 7, 0:C], gate[:, 15:16], ocls[:, :], ALU.mult, ALU.add)\
             .then_inc(e_fin, 1)

        @block.tensor
        def _(pe):
            T = nc.tensor

            def mm(o_, l, r, first=True, final=True):
                return T.matmul(o_, l, r, start=first, stop=final)

            pe.wait_ge(s_tw, 96)
            for k in range(11):
                if k >= 8:
                    pe.wait_ge(s_fsb, k - 7)
                if k == 0:
                    mm(PS[0:GP * P0, 0, 0:C], w0_sb[:, :], wf_sb[:, 0, :]).then_inc(s_fps, 1)
                elif k < 3:
                    mm(PS[0:96, k, 0:C], w1_sb[:, 96 * (k - 1):96 * k], wf_sb[:, 1, :]).then_inc(s_fps, 1)
                else:
                    mm(PS[0:96, k % 8, 0:C], w2_sb[:, 96 * (k - 3):96 * (k - 2)], wf_sb[:, 2, :]).then_inc(s_fps, 1)
            pe.wait_ge(s_bw, 3)
            pe.wait_ge(s_fsb, 4)
            for lev in range(3):
                mm(PS[:, 3, 0:C], b012_wide[:, lev, :], wf_sb[:, lev, :], lev == 0, False)
            mm(PS[:, 3, 0:C], ones[0:1, :], bf_sb[:, :], False, True).then_inc(s_fps, 1)
            pe.wait_ge(s_wsum, 1)
            pe.wait_ge(s_fsb, 8)
            mm(PS[:, 7, 0:2], ones[0:96, :], wabs[:, :]).then_inc(s_wsum, 1)
            pe.wait_ge(s_id, 2)
            pe.wait_ge(s_fsb, 11)
            pe.wait_ge(s_vc, 2)
            for k in range(8):
                src = pat2 if k < 4 else pat1
                if k % 4 == 0:
                    pe.wait_ge(s_pat, 1 + k // 4)
                if k == 7:
                    pe.wait_ge(s_wt, 1)
                for e in range(4):
                    b = 4 * (k % 4) + e
                    last = T.transpose(PS[0:96, k, 128 * e:128 * (e + 1)], src[:, b, :], ident[:, :])
                last.then_inc(s_fps, 1)
            for k in range(10):
                if k == 0:
                    pe.wait_ge(s_fsb, 19)
                if k >= 8:
                    pe.wait_ge(s_zc, k - 7)
                if k < 8:
                    for jh in range(2):
                        last = mm(PS[:, k, 0:C], x1T[:, jh, 2 * k:2 * k + 2, :].rearrange("p b n -> p (b n)"), fused[:, 1 + jh, :],
                                  jh == 0, jh == 1)
                else:
                    e = k - 8
                    for j8 in range(8):
                        last = mm(PS[:, e, 0:C], x2T[:, j8, 8 * e:8 * e + 8, :].rearrange("p b n -> p (b n)"), fused[:, 3 + j8, :],
                                  j8 == 0, j8 == 7)
                last.then_inc(s_fps, 1)
            pe.wait_ge(s_zc, 10)
            pe.wait_ge(s_zall, 16 * (B + 10))
            pe.wait_ge(s_wt, 8)
            pe.wait_ge(s_fw, 48)

            def body(at, t, par):
                attn, front, back, ffn = has(t)

                def score(u):
                    if attn:
                        wait(pe, stk_c[u], at(1))
                        if u < 2:
                            for w in (1 + 2 * u, 2 + 2 * u):
                                wait(pe, stk_c[w], at(1))
                        else:
                            wait(pe, maxed[u - 2], at(1))
                        for hh in range(2):
                            for c in range(NC):
                                last = mm(PS[:, 2 * (u % 2) + hh, N * c:N * (c + 1)],
                                          qk[par][0:96, 0, 2 * u + hh, 128 * c:128 * (c + 1)],
                                          qk[par][0:96, 1, 2 * u + hh, :])
                        last.then_inc(scores[u], 1)

                def score_t(u):
                    if attn:
                        if u < 2:
                            wait(pe, maxed[4 + u], at(1))
                        else:
                            wait(pe, expd[u - 2], at(1))
                        if u == 0:
                            for r in range(2):
                                wait(pe, shift_rows[r], at(1), 16)
                        for hh in range(2):
                            for c in range(NC):
                                last = mm(PS[:, 2 * (u % 2) + hh, N * c:N * (c + 1)],
                                          qk[par][:, 1, 2 * u + hh, 128 * c:128 * (c + 1)],
                                          qk[par][:, 0, 2 * u + hh, :])
                        last.then_inc(scoresT[u], 1)

                def weighted(g):
                    if attn:
                        wait(pe, expd[2 * g], at(1))
                        wait(pe, expd[2 * g + 1], at(1))
                        if g == 0:
                            wait(pe, v_sb, at(1))
                            if ffn:
                                wait(pe, out_done[0], at(-1))
                                wait(pe, out_done[1], at(-1))
                            else:
                                wait(pe, oT_done[G - 1], at(0))
                        else:
                            wait(pe, oT_done[g - 1], at(1))
                        for c in range(NC):
                            for j in range(4):
                                last = mm(PS[32 * j:32 * (j + 1), 6, 0:N], vals[:, c, 4 * g + j, :],
                                          probs[:, (2 * g + j // 2) % 4, j % 2, c, :], c == 0, c == NC - 1)
                        last.then_inc(pv[g], 1)

                def hidden(f):
                    if ffn:
                        if f == 0:
                            wait(pe, n_tc, at(-1))
                            wait(pe, v_sb, at(1))
                        elif f == 1:
                            wait(pe, stk_c[0], at(1))
                        else:
                            wait(pe, gelud[f - 2], at(-1))
                        for k in range(KC):
                            last = mm(PS[:, 4 + f % 2, 0:N], mw1_sb[:, k, 128 * f:128 * (f + 1)], xnT[par][:, k, :],
                                      k == 0, k == KC - 1)
                        last.then_inc(f1[f], 1)

                def transpose_ints(bank, ints, done):
                    for k in range(KC):
                        for c in range(NC):
                            last = T.transpose(PSb[0:96, bank, N * k + 128 * c:N * k + 128 * (c + 1)],
                                               ints[:, c, 96 * k:96 * (k + 1)], identb[:, :])
                    last.then_inc(done, 1)

                score(0)
                hidden(0)
                score(1)
                hidden(1)
                if front:
                    wait(pe, tok_ready, at(2))
                    wait(pe, stk_c[5], at(1))
                    for c in range(NC):
                        last = T.transpose(PS[:, 7, 128 * c:128 * (c + 1)], tok_in[:, c, :], ident[:, :])
                    last.then_inc(tok_t, 1)
                score(2)
                hidden(2)
                score(3)
                hidden(3)
                if front:
                    wait(pe, tok_c, at(2))
                    for c in range(NC):
                        last = mm(PS[:, 7, C * c:C * (c + 1)], tok_inT[:, 128 * c:128 * (c + 1)],
                                  zall[:, bass.ds(at(1), 1), :].rearrange("p a n -> p (a n)"))
                    last.then_inc(h_ps, 1)
                score(4)
                hidden(4)
                score(5)
                hidden(5)
                if back:
                    for g in range(G):
                        wait(pe, oT_done[g], at(0))
                    if ffn:
                        wait(pe, gelud[4], at(-1))
                        wait(pe, gelud[5], at(-1))
                    else:
                        wait(pe, v_sb, at(1))
                        wait(pe, stk_c[0], at(1))
                    for c in range(NC):
                        for g in range(G):
                            last = T.transpose(PS[:, 4 + c, 128 * g:128 * (g + 1)], oT[:, g, 128 * c:128 * (c + 1)], ident[:, :])
                    last.then_inc(o_t, 1)
                if attn:
                    wait(pe, shift_done, at(1))
                    if front:
                        wait(pe, h_sb, at(2))
                    else:
                        wait(pe, stk_c[5], at(1))
                    for c in range(NC):
                        last = T.transpose(PSb[0:2 * H, 7, 128 * c:128 * (c + 1)],
                                           shift[:, c, :, :].rearrange("p r h -> p (r h)"), identb[:, :])
                    last.then_inc(shift_t, 1)
                if ffn:
                    wait(pe, oT_done[G - 1], at(0))
                    for f in range(NF):
                        wait(pe, gelud[f], at(-1))
                    for c in range(NC):
                        for f in range(NF):
                            last = mm(PS[:, 6, C * c:C * (c + 1)], hid[:, f, 128 * c:128 * (c + 1)], mw2_sb[:, f, :],
                                      f == 0, f == NF - 1)
                    last.then_inc(f2, 1)
                if front:
                    wait(pe, q_int, at(2))
                    if attn:
                        wait(pe, shift_c, at(1))
                    else:
                        wait(pe, h_sb, at(2))
                    transpose_ints(7, i_q, q_t)
                score_t(0)
                score_t(1)
                if front:
                    wait(pe, q_tc, at(2))
                    if back:
                        wait(pe, o_sbd, at(0))
                    elif attn:
                        wait(pe, stk_c[0], at(1))
                    for c in range(NC):
                        for k in range(KC):
                            last = mm(PS[:, QK_BANK[c], 0:2 * C], iT_q[:, k, 128 * c:128 * (c + 1)], wq[:, k, 0:2 * C],
                                      k == 0, k == KC - 1)
                        last.then_inc(qk_ps[c], 1)
                score_t(2)
                if back:
                    wait(pe, p_int, at(0))
                    wait(pe, o_sbd, at(0))
                    transpose_ints(4, i_p, p_t)
                score_t(3)
                weighted(0)
                if back:
                    wait(pe, p_tc, at(0))
                    for c in range(NC):
                        for k in range(KC):
                            last = mm(PS[:, 4, C * c:C * (c + 1)], iT_p[:, k, 128 * c:128 * (c + 1)], wp[:, k, :],
                                      k == 0, k == KC - 1)
                    last.then_inc(p_ps, 1)
                score_t(4)
                weighted(1)
                score_t(5)
                weighted(2)
                if back:
                    wait(pe, xn_done, at(0))
                    for k in range(KC):
                        for c in range(NC):
                            last = T.transpose(PS[0:96, 4, N * k + 128 * c:N * k + 128 * (c + 1)],
                                               xn[:, c, 96 * k:96 * (k + 1)], ident[:, :])
                    last.then_inc(n_t, 1)
                if front:
                    if back:
                        wait(pe, n_tc, at(0))
                    elif attn:
                        wait(pe, v_sb, at(1))
                    for c in range(NC):
                        for k in range(KC):
                            last = mm(PS[:, 4, C * c:C * (c + 1)], iT_q[:, k, 128 * c:128 * (c + 1)], wq[:, k, 2 * C:3 * C],
                                      k == 0, k == KC - 1)
                    last.then_inc(v_ps, 1)
                    wait(pe, p3_done[0], at(2))
                    wait(pe, p3_done[1], at(2))
                    wait(pe, dup_done, at(2))
                    for w in range(U):
                        if w in (0, 5):
                            wait(pe, rest_done[w // 5], at(2))
                        elif attn:
                            wait(pe, expd[4 + (w - 1) // 2], at(1))
                        for side in range(2):
                            for hh in range(2):
                                for c in range(NC):
                                    col = (4 * side + 2 * hh + c) * 128
                                    last = T.transpose(PSb[0:96, STACK_BANK[w], col:col + 128], stack[:, side, c, 2 * w + hh, :],
                                                       identb[:, :])
                        last.then_inc(stk_t[w], 1)

            steps(pe, body)

            pe.wait_ge(s_ew, 80)
            pe.wait_ge(cls_done, B)
            pe.wait_ge(n_tc, B)
            tok = clsT[:, :, :, :].rearrange("p k i b -> p k (i b)")
            for k in range(KC):
                last = mm(PS[0:NCLS * B, 7, 0:2 * NCLS], tok[:, k, :], gw_sb[:, k, :], k == 0, k == KC - 1)
            last.then_inc(e_h, 1)

            def second(e, bank, experts):
                for c in experts:
                    for f in range(NF):
                        mm(PS[0:NCLS * B, bank, 0:C], hexp[:, c, f, :], aw2_sb[:, c, f, :], c == experts[0] and f == 0, False)
                mm(PS[0:NCLS * B, bank, 0:C], sel[:, e, :, :].rearrange("p i b -> p (i b)"), ab2_sb[:, :], False, True)\
                    .then_inc(e_h, 1)

            for a in range(NEXP):
                if a >= 3:
                    pe.wait_ge(e_b, a - 2)
                if a == 2:
                    pe.wait_ge(gelud[NF - 1], B)
                for f in range(NF):
                    for k in range(KC):
                        last = mm(PS[:, 2 * (a % 3) + f // 3, NCLS * B * (f % 3):NCLS * B * (f % 3 + 1)],
                                  aw1_sb[:, a, k, 128 * f:128 * (f + 1)], tok[:, k, :], k == 0, k == KC - 1)
                last.then_inc(e_h, 1)
            pe.wait_ge(s_const, 3)
            pe.wait_ge(out_done[1], B)
            pe.wait_ge(e_g, 3)
            second(0, 6, (3, 4))
            pe.wait_ge(e_g, 5)
            pe.wait_ge(e_gate, 1)
            second(1, 7, (0, 1, 2))


def kernel(**inputs):
    import numpy as np
    import concourse.bacc as bacc
    from concourse.bass_utils import run_bass_kernel_spmd

    a = {k: np.asarray(v) for k, v in inputs.items()}

    def patches(p):
        n = 64 // p
        return a["x"].reshape(B, 3, n, p, n, p).transpose(2, 4, 0, 3, 5, 1).reshape(n * n, B * p * p * 3)

    def chunks(w, rows):
        w = w.reshape(w.shape[:-2] + (w.shape[-2] // rows, rows, w.shape[-1]))
        return np.moveaxis(w, -2, 0)

    ins = {
        "x0": patches(1), "x1": patches(2), "x2": patches(4),
        "idx0": a["L0_tok_idx0"].reshape(NC, 128, GP).transpose(1, 0, 2).reshape(128, NC * GP),
        "idx1": a["L0_tok_idx1"].reshape(T1, 2, 8).transpose(1, 0, 2).reshape(128, 8),
        "idx2": a["L0_tok_idx2"].reshape(T2, 8, 2).transpose(1, 0, 2).reshape(128, 2),
        "w0": a["L0_tok_W0"], "w1": a["L0_tok_W1"], "w2": a["L0_tok_W2"],
        "b012": np.stack([a["L0_tok_b0"], a["L0_tok_b1"], a["L0_tok_b2"]], axis=1),
        "wf": chunks(a["L0_tok_Wf"].T, 64), "bf": a["L0_tok_bf"].reshape(1, C),
        "wqkv": chunks(a["L0_attn_w_qkv"].T, 96), "gqkv": a["L0_attn_g_qkv"].reshape(1, C),
        "wproj": chunks(a["L0_attn_w_proj"].T, 96), "gproj": a["L0_attn_g_proj"].reshape(1, C),
        "mw1": chunks(a["L0_ffn_moe0_W1"], 96), "mb1": a["L0_ffn_moe0_b1"].reshape(NF, 128).T,
        "mw2": chunks(a["L0_ffn_moe0_W2"], 128), "mb2": a["L0_ffn_moe0_b2"].reshape(1, C),
        "aw1": chunks(a["L0_ffn_A1_W"], 96), "ab1": a["L0_ffn_A1_b"].reshape(NEXP, NF, 128).transpose(2, 0, 1),
        "aw2": chunks(a["L0_ffn_A2_W"], 128), "ab2": a["L0_ffn_A2_b"],
        "gw": chunks(a["L0_ffn_G_W"].transpose(1, 0, 2).reshape(C, 2 * NCLS), 96),
    }
    nc = bacc.Bacc("TRN2", target_bir_lowering=False, num_devices=1)
    arrays, args = {}, []
    for name, v in ins.items():
        v = np.ascontiguousarray(v)
        arrays[f"in_{name}"] = v
        args.append(nc.dram_tensor(f"in_{name}", v.shape, mybir.dt.from_np(v.dtype), kind="ExternalInput").ap())
    args.append(nc.dram_tensor("out_0", (B, N, C), F32, kind="ExternalOutput").ap())
    vit_tower(nc, *args)
    r = run_bass_kernel_spmd(nc, [arrays], core_ids=[0])
    return r.results[0]["out_0"]
```

```python
import concourse.bass as bass
from concourse import mybir
from contextlib import ExitStack

F32 = mybir.dt.float32
BF16 = mybir.dt.bfloat16
I32 = mybir.dt.int32
ALU = mybir.AluOpType
ACT = mybir.ActivationFunctionType
AX = mybir.AxisListType

B = 16
N = 256
C = 192
H, D = 12, 16
NC = N // 128
KC = C // 96
G = H // 4
U = H // 2
HID = 768
NF = HID // 128
NCLS, NEXP = 6, 5
GP = 16
T1, T2 = 64, 16
P0, P1, P2 = 3, 12, 48
HOT = 3
X1 = (64 // 2) ** 2 // 128
ZR = T1 + T2
PARTS = 6
EPS = 1e-5
MAGIC = 1.5 * 2.0 ** 23
QMAX = 127.0


def vit_tower(nc, x0, x1, x2, idx0, idx1, idx1_row, idx2, w0, w1, w2, b012, wf, bf, wqkv, gqkv, wproj, gproj,
              mw1, mb1, mw2, mb2, aw1, ab1, aw2, ab2, gw, out):
    ctx = ExitStack()
    with ctx:
        def sb(name, shape, dt=F32):
            return ctx.enter_context(nc.sbuf_tensor(name, shape, dt))

        def sem(name):
            return ctx.enter_context(nc.semaphore(name))

        def sems(name, n):
            return [sem(f"{name}{i}") for i in range(n)]

        ident = sb("ident", [128, 128])
        identb = sb("identb", [128, 128], BF16)
        ones = sb("ones", [128, 128])
        neg_half = sb("neg_half", [128, 2])
        idx0_sb = sb("idx0_sb", [128, NC * GP], I32)
        idx1_sb = sb("idx1_sb", [128, 8], I32)
        idx2_sb = sb("idx2_sb", [128, 2], I32)
        gath0 = sb("gath0", [128, NC, GP, B * P0])
        b012_sb = sb("b012_sb", [64, 3])
        bf_sb = sb("bf_sb", [1, C])
        zall = sb("zall", [128, B, C])
        tok_in = sb("tok_in", [128, NC, 128])
        pos = sb("pos", [128, 2, NC])
        patch_no = sb("patch_no", [128, X1])
        tok_inT = sb("tok_inT", [128, N])
        h_all = sb("h_all", [128, B, NC, C])
        flat0 = h_all[:, :, :, :].rearrange("p b c n -> p (b c n)")
        fused = flat0[0:96, 0:11 * C].rearrange("p (k n) -> p k n", n=C)
        pat2, pat1 = (flat0[:, n:n + B * 96].rearrange("p (b n) -> p b n", b=B) for n in (11 * C, 11 * C + B * 96))
        wq = sb("wq", [96, KC, 3 * C], BF16)
        wp = sb("wp", [96, KC, C], BF16)
        wabs = sb("wabs", [96, 2])
        wscale = sb("wscale", [128, 4])
        wsq = sb("wsq", [128, 2])
        gq_sb = sb("gq_sb", [128, C])
        gp_sb = sb("gp_sb", [128, C])
        mb2_sb = sb("mb2_sb", [128, C])
        mw1_sb = sb("mw1_sb", [96, KC, HID])
        mb1_sb = sb("mb1_sb", [128, NF])
        spare = sb("spare", [1, 1])
        mw2_sb = sb("mw2_sb", [128, NF, C])

        u_q = sb("u_q", [128, NC, C])
        r_q = sb("r_q", [128, NC, C])
        i_q = sb("i_q", [128, NC, C], BF16)
        iT_q = sb("iT_q", [96, KC, N], BF16)
        st_q = sb("st_q", [128, NC, 6])
        mv_q = sb("mv_q", [128, NC, 2])
        sc_q = sb("sc_q", [128, 8, NC])
        part1 = sb("part1", [128, 2, NC, H * D], BF16)
        part2 = sb("part2", [128, 2, NC, H * D], BF16)
        rest = sb("rest", [128, 2, NC, H * D])
        stack = sb("stack", [128, 2, NC, H, PARTS * D], BF16)
        qk = [sb(f"qk{i}", [98, 2, H, N], BF16) for i in range(2)]
        vals = sb("vals", [128, NC, H, 32])
        negmax = sb("negmax", [128, H, NC])
        shift = sb("shift", [128, NC, 2, H], BF16)
        shiftT = sb("shiftT", [2 * H, N], BF16)
        probs = sb("probs", [128, 4, 2, NC, N])
        oT = sb("oT", [128, G, N])
        recip = sb("recip", [128, NC, H])
        o = sb("o", [128, NC, H, D])
        u_p = sb("u_p", [128, NC, C])
        r_p = sb("r_p", [128, NC, C])
        i_p = sb("i_p", [128, NC, C], BF16)
        iT_p = sb("iT_p", [96, KC, N], BF16)
        st_p = sb("st_p", [128, NC, 6])
        mv_p = sb("mv_p", [128, NC, 2])
        sc_p = sb("sc_p", [128, 8, NC])
        st_n = sb("st_n", [128, NC, 6])
        mv_n = sb("mv_n", [128, NC, 2])
        sc_n = sb("sc_n", [128, 2, NC])
        xn = sb("xn", [128, NC, C])
        xnT = [sb(f"xnT{i}", [96, KC, N]) for i in range(2)]
        hb = [sb(f"hb{i}", [128, NC, C]) for i in range(2)]
        hid = sb("hid", [128, NF, N])
        o_sb = sb("o_sb", [128, NC, C])

        clsT = sb("clsT", [96, KC, NCLS, B])
        aw1_sb = sb("aw1_sb", [96, NEXP, KC, HID])
        ab1_sb = sb("ab1_sb", [128, NEXP, NF])
        aw2_sb = sb("aw2_sb", [128, NEXP, NF, C])
        ab2_sb = sb("ab2_sb", [NEXP, C])
        flat1 = aw1_sb[:, :, :, :].rearrange("p e k n -> p (e k n)")
        flat2 = aw2_sb[:, :, :, :].rearrange("p e f n -> p (e f n)")
        n_x, n_w = B * 128, KC * 4 * C
        x1T = flat1[:, 0:n_x].rearrange("p (j b n) -> p j b n", j=2, b=B)
        x2T = flat1[:, n_x:2 * n_x].rearrange("p (j b n) -> p j b n", j=8, b=B)
        w_raw, w_rnd = (flat1[:, 2 * n_x + n_w * i:2 * n_x + n_w * (i + 1)].rearrange("p (k n) -> p k n", k=KC)
                        for i in range(2))
        n_g, n_z = B * P2 * 2, B // 2 * C
        gath1 = flat2[:, 0:n_g].rearrange("p (t n) -> p t n", t=8)
        gath2 = flat2[:, n_g:2 * n_g].rearrange("p (t n) -> p t n", t=2)
        z1 = flat2[:, 2 * n_g:2 * n_g + n_z].rearrange("p (a n) -> p a n", n=C)
        z2 = flat2[:, 2 * n_g + n_z:2 * n_g + n_z + B // 8 * C].rearrange("p (a n) -> p a n", n=C)
        gw_sb = sb("gw_sb", [96, KC, 2 * NCLS])
        sel = sb("sel", [NEXP, 2, NCLS, B])
        own = sb("own", [NCLS * B, 2, NCLS])
        flat3 = probs[:, :, :, :, :].rearrange("p s a c n -> p (s a c n)")
        w0_sb, w1_sb, w2_sb = flat3[0:64, 0:48], flat3[0:64, 48:240], flat3[0:64, 240:1008]
        wf_sb = flat3[0:64, 1008:1008 + 3 * C].rearrange("p (k n) -> p k n", k=3)
        b012_wide = flat3[0:64, 1600:1600 + 3 * 128].rearrange("p (k n) -> p k n", k=3)
        hat = flat3[:, 2000:2000 + NC * ZR].rearrange("p (c t) -> p c t", c=NC)
        zbias = flat3[:, 2200:2200 + C]
        x1_sb = hid[:, :, :].rearrange("p f n -> p (f n)").rearrange("p (k n) -> p k n", k=X1)
        hot_flat = stack[:, :, :, :, :].rearrange("p s c h n -> p (s c h n)").bitcast(F32)
        hot = [hot_flat[:, X1 * 128 * i:X1 * 128 * (i + 1)].rearrange("p (k n) -> p k n", k=X1) for i in range(2)]
        row_i = flat3[:, 2400:2400 + HOT * 128].bitcast(I32)
        row_f = flat3[:, 2400 + HOT * 128:2400 + 2 * HOT * 128]
        n_e, n_p = NEXP * NF * NCLS * B, 2 * NF * 3 * B
        hexp = flat3[:, 0:n_e].rearrange("p (c f t) -> p c f t", c=NEXP, f=NF)
        hcls = flat3[0:NCLS * B, n_e + n_p:n_e + n_p + C]
        ocls = flat3[0:NCLS * B, n_e + n_p + C:n_e + n_p + 2 * C]
        hpre = flat3[:, n_e:n_e + n_p].rearrange("p (a f s b) -> p a f s b", a=2, f=NF, s=3)
        logit = sb("logit", [NCLS * B, 2, NCLS])
        gate = sb("gate", [NCLS * B, 16])

        PS = ctx.enter_context(nc.psum_tensor("PS", [128, 8, 512], F32))
        PSb = PS[:, :, :].bitcast(BF16)

        s_idx = sem("s_idx")
        s_pat = sem("s_pat")
        s_tw = sem("s_tw")
        s_aw = sem("s_aw")
        s_fw = sem("s_fw")
        s_ew = sem("s_ew")
        s_g0, s_g12 = sem("s_g0"), sem("s_g12")
        s_zero = sem("s_zero")
        s_id = sem("s_id")
        s_pool = sem("s_pool")
        s_vc = sem("s_vc")
        s_wsum = sem("s_wsum")
        s_bw = sem("s_bw")
        s_row, s_hot = sem("s_row"), sem("s_hot")
        s_fps = sem("s_fps")
        s_fsb, s_zc = sem("s_fsb"), sem("s_zc")
        s_zall = sem("s_zall")
        s_wt = sem("s_wt")
        s_const = sem("s_const")
        W_STEPS, T_STEPS, Z_STEPS = HOT + 12, HOT + 20, HOT + 30
        s_carrier = sem("s_carrier")
        scores, maxed = sems("scores", U), sems("maxed", U)
        shift_hi, shift_done, shift_t, shift_c = sem("shift_hi"), sem("shift_done"), sem("shift_t"), sem("shift_c")
        shift_rows = sem("shift_rows")
        scoresT, expd = sems("scoresT", U), sems("expd", U)
        pv, oT_done = sems("pv", G), sems("oT_done", G)
        f1, gelud, f2, out_done, stored = sems("f1", NF), sems("gelud", NF), sem("f2"), sems("out_done", NC), sems("stored", NC)
        tok_ready, tok_t, tok_c, h_ps, h_sb = sem("tok_ready"), sem("tok_t"), sem("tok_c"), sem("h_ps"), sem("h_sb")
        q_steps = sems("q_step", 10)
        q_pow, q_int, q_t, q_tc = sem("q_pow"), sem("q_int"), sem("q_t"), sem("q_tc")
        qk_ps, v_ps, v_sb = sems("qk_ps", NC), sem("v_ps"), sem("v_sb")
        p1_done, rest_done, p2_done, p3_done = (sems(n, 2) for n in ("p1_done", "rest_done", "p2_done", "p3_done"))
        dup_done = sem("dup_done")
        stk_t, stk_c = sems("stk_t", U), sems("stk_c", U)
        o_t, o_rec, o_sbd = sem("o_t"), sem("o_rec"), sem("o_sbd")
        p_steps = sems("p_step", 10)
        p_pow, p_int, p_t, p_tc, p_ps = sem("p_pow"), sem("p_int"), sem("p_t"), sem("p_tc"), sem("p_ps")
        n_steps, xn_done = sems("n_step", 5), sem("xn_done")
        n_pow, n_t, n_tc, hb_done, cls_done = sem("n_pow"), sem("n_t"), sem("n_tc"), sem("hb_done"), sem("cls_done")
        e_hcls, e_gate = sem("e_hcls"), sem("e_gate")
        e_h, e_b, e_g, e_fin, e_out = sem("e_h"), sem("e_b"), sem("e_g"), sem("e_fin"), sem("e_out")

        block = ctx.enter_context(nc.Block())

        class At:

            def __init__(self, eng, t, loop=None):
                self.t, self.eng, self.loop = t, eng, loop
                self.seen = {}

            def __call__(self, off):
                if self.loop is None:
                    return min(self.t + off, B)
                k = self.t + off
                if k not in self.seen:
                    self.seen[k] = self.eng.snap(self.loop + k)
                return self.seen[k]

        def wait(eng, s, count, by=1):
            if isinstance(count, int):
                if count > 0:
                    eng.wait_ge(s, by * count)
            else:
                eng.wait_ge(s, count * by if by != 1 else count)

        def wait_alone(eng, s, count, by=1):
            wait(eng, s, count, by)
            eng.sem_inc(s_carrier)

        LOOP, LAST = 4, B + 1

        def steps(eng, body):
            for t in range(-1, LOOP):
                body(At(eng, t), t, t % 2)
            with eng.Fori(LOOP, B - 2, 2) as i:
                seen = {}
                for p in range(2):
                    at = At(eng, p, i)
                    at.seen = seen
                    body(at, LOOP, p)
            for t in range(B - 2, LAST + 1):
                body(At(eng, t), t, t % 2)

        def has(t):
            return 0 <= t < B, t + 1 < B, 1 <= t <= B, t >= 2

        def third_part(eng, side):
            slot = (5, 2)[side]
            return eng.tensor_tensor(stack[:, side, :, :, D * slot:D * (slot + 1)],
                                     rest[:, side, :, :].rearrange("p c (h d) -> p c h d", d=D),
                                     part2[:, side, :, :].rearrange("p c (h d) -> p c h d", d=D), ALU.subtract)

        STACK_BANK = (5, 0, 1, 2, 3, 6)
        BY_ACT = (1, 4)
        QK_BANK = (5, 7)
        PV_BANK = (6, 6, 4)

        @block.sync
        def _(sp):
            sp.dma_start(idx2_sb[:, :], idx2).then_inc(s_idx, 16)
            sp.dma_start(idx1_sb[:, :], idx1).then_inc(s_idx, 16)
            sp.dma_start(idx0_sb[:, :], idx0).then_inc(s_idx, 16)
            sp.dma_start(row_i, idx1_row.broadcast_to([128, HOT * 128])).then_inc(s_row, 16)
            sp.dma_start(x1_sb, x1.rearrange("(k p) n -> p k n", p=128)).then_inc(s_row, 16)
            for dst, src in ((w0_sb, w0), (w1_sb, w1), (w2_sb, w2), (wf_sb, wf),
                             (b012_sb[:, :], b012), (bf_sb[:, :], bf)):
                sp.dma_start(dst, src).then_inc(s_tw, 16)
            sp.dma_start(w_raw[:, :, 0:3 * C], wqkv).then_inc(s_aw, 16)
            sp.dma_start(w_raw[:, :, 3 * C:4 * C], wproj).then_inc(s_aw, 16)
            sp.dma_start(gq_sb[:, :], gqkv.broadcast_to([128, C])).then_inc(s_aw, 16)
            sp.dma_start(gp_sb[:, :], gproj.broadcast_to([128, C])).then_inc(s_aw, 16)
            sp.dma_start(mb2_sb[:, :], mb2.broadcast_to([128, C])).then_inc(s_aw, 16)
            sp.wait_ge(s_fsb, HOT + 1)
            for b in range(B):
                sp.dma_start(zall[ZR:128, b, :], fused[0:48, 0, :]).then_inc(s_zall, 16)
            sp.dma_start(mw1_sb[:, :, :], mw1).then_inc(s_fw, 16)
            sp.dma_start(mb1_sb[:, :], mb1).then_inc(s_fw, 16)
            sp.dma_start(mw2_sb[:, :, :], mw2).then_inc(s_fw, 16)
            sp.wait_ge(s_zc, 2)
            zoct = zall[T1:ZR, :, :].rearrange("p (a e) n -> p a e n", e=8)
            for e in range(8):
                sp.dma_start(zoct[:, :, e, :], z2[T2 * e:T2 * (e + 1), :, :]).then_inc(s_zall, 16)
            sp.wait_ge(s_wt, 8)
            sp.wait_ge(s_fps, Z_STEPS)
            sp.wait_ge(s_zall, 16 * (B + 10))
            sp.wait_ge(tok_ready, 1)
            sp.dma_start(aw1_sb[:, :, :, :], aw1).then_inc(s_ew, 16)
            sp.dma_start(aw2_sb[:, :, :, :], aw2).then_inc(s_ew, 16)
            sp.dma_start(ab1_sb[:, :, :], ab1).then_inc(s_ew, 16)
            sp.dma_start(ab2_sb[:, :], ab2).then_inc(s_ew, 16)
            sp.dma_start(gw_sb[:, :, :], gw).then_inc(s_ew, 16)

            def body(at, t, par):
                attn, front, back, ffn = has(t)
                if attn:
                    wait_alone(sp, scoresT[U - 1], at(-1))
                    wait(sp, shift_c, at(1))
                    sp.dma_start(qk[par][96:98, 0, :, :], shiftT[:, :]).then_inc(shift_rows, 16)
                if ffn:
                    img = at(-2)
                    wait_alone(sp, out_done[0], at(-1))
                    sp.dma_start(out[bass.ds(img, 1), NCLS:128, :].rearrange("a p n -> p a n"), o_sb[NCLS:128, 0:1, :])\
                      .then_inc(stored[0], 16)
                    wait_alone(sp, out_done[1], at(-1))
                    sp.dma_start(out[bass.ds(img, 1), 128:N, :].rearrange("a p n -> p a n"), o_sb[:, 1:2, :])\
                      .then_inc(stored[1], 16)

            steps(sp, body)
            sp.wait_ge(n_steps[1], B)
            sp.wait_ge(pv[G - 1], B)
            sp.dma_start(hcls[:, :], h_all[0:NCLS, :, 0, :]).then_inc(e_hcls, 16)
            sp.wait_ge(e_fin, 2)
            sp.dma_start(out.rearrange("b i n -> i b n")[0:NCLS, :, :], ocls[:, :]).then_inc(e_out, 16)
            sp.wait_ge(stored[0], 16 * B)
            sp.wait_ge(stored[1], 16 * B)
            sp.wait_ge(e_out, 16)

        @block.gpsimd
        def _(pool):
            pool.iota(patch_no[:, :], pattern=[[128, X1]], base=0, channel_multiplier=1,
                      allow_small_or_imprecise_dtypes=True).then_inc(s_pool, 1)
            pool.wait_ge(s_idx, 48)
            for t in range(2):
                pool.indirect_dma_start(gath2[:, t, :], None, x2, bass.IndirectOffsetOnAxis(idx2_sb[:, t:t + 1], 0))\
                    .then_inc(s_g12, 16)
            for t in range(8 - HOT):
                pool.indirect_dma_start(gath1[:, t, :], None, x1, bass.IndirectOffsetOnAxis(idx1_sb[:, t:t + 1], 0))\
                    .then_inc(s_g12, 16)
            pool.memset(ident[:, :], 0.0).then_inc(s_zero, 1)
            pool.memset(identb[:, :], 0.0).then_inc(s_zero, 1)
            pool.wait_ge(s_zero, 2)
            for m in (ident, identb):
                pool.affine_select(out=m[:, :], in_=m[:, :], compare_op=ALU.not_equal, fill=1.0, base=0,
                                   pattern=[[-1, 128]], channel_multiplier=1).then_inc(s_id, 1)
            pool.iota(hat[:, :, 0:T1], pattern=[[0, NC], [1, T1]], base=0, channel_multiplier=0,
                      allow_small_or_imprecise_dtypes=True).then_inc(s_pool, 1)
            pool.iota(hat[:, :, T1:ZR], pattern=[[0, NC], [1, T2]], base=0, channel_multiplier=0,
                      allow_small_or_imprecise_dtypes=True).then_inc(s_pool, 1)
            pool.iota(pos[:, :, :], pattern=[[0, 2], [128, NC]], base=0, channel_multiplier=1,
                      allow_small_or_imprecise_dtypes=True).then_inc(s_pool, 1)
            for j in range(NC * GP):
                pool.indirect_dma_start(gath0[:, j // GP, j % GP, :], None, x0,
                                        bass.IndirectOffsetOnAxis(idx0_sb[:, j:j + 1], 0)).then_inc(s_g0, 16)
            pool.wait_ge(s_g0, 16 * NC * GP)

            def body(at, t, par):
                attn, front, back, ffn = has(t)
                if front:
                    wait(pool, tok_t, at(1))
                    if t == -1:
                        pool.wait_ge(s_vc, 6)
                    src = gath0[:, :, :, bass.ds(at(1) * P0, P0)]
                    pool.tensor_copy(tok_in[:, :, ZR:128].rearrange("p c (j k) -> p c j k", k=P0), src)\
                        .then_inc(tok_ready, 1)
                if front:
                    wait(pool, q_steps[1], at(2))
                    pool.tensor_tensor(sc_q[:, 1, :], sc_q[:, 0, :], neg_half[:, :], ALU.pow).then_inc(q_pow, 1)
                if back:
                    wait(pool, o_sbd, at(0))
                    wait_alone(pool, p_steps[7], at(-1))
                    pool.tensor_tensor(u_p[:, :, :], o[:, :, :, :].rearrange("p c h d -> p c (h d)"),
                                       gp_sb[:, :].unsqueeze(1).broadcast_to([128, NC, C]), ALU.mult).then_inc(p_steps[2], 1)
                    wait(pool, p_steps[1], at(0))
                    pool.tensor_tensor(sc_p[:, 1, :], sc_p[:, 0, :], neg_half[:, :], ALU.pow).then_inc(p_pow, 1)
                if front:
                    wait(pool, q_steps[7], at(2))
                    wait_alone(pool, q_t, at(1))
                    pool.tensor_scalar(i_q[:, :, :], r_q[:, :, :], -MAGIC, 1.0, ALU.add, ALU.mult).then_inc(q_int, 1)
                if back:
                    wait(pool, p_steps[7], at(0))
                    wait_alone(pool, p_t, at(-1))
                    pool.tensor_scalar(i_p[:, :, :], r_p[:, :, :], -MAGIC, 1.0, ALU.add, ALU.mult).then_inc(p_int, 1)
                if front:
                    for c in range(NC):
                        wait(pool, rest_done[c], at(2))
                        if c == 0:
                            wait(pool, dup_done, at(1))
                        wait_alone(pool, stk_t[U - 1], at(1))
                        pool.tensor_scalar(part2[:, :, c, :], rest[:, :, c, :], 1.0, 0.0, ALU.mult, ALU.add)\
                            .then_inc(p2_done[c], 1)
                    wait(pool, p2_done[0], at(2))
                    wait(pool, p2_done[1], at(2))
                    third_part(pool, 0).then_inc(p3_done[0], 1)
                if back:
                    wait(pool, n_steps[2], at(0))
                    pool.tensor_tensor(sc_n[:, 1, :], sc_n[:, 0, :], neg_half[:, :], ALU.pow).then_inc(n_pow, 1)
                if back:
                    wait(pool, out_done[1], at(-2))
                    hrow = h_all[:, bass.ds(at(-1), 1), :, :].rearrange("p a c n -> p (a c) n")
                    pool.tensor_tensor(hb[1 - par][:, :, :], hrow,
                                       mb2_sb[:, :].unsqueeze(1).broadcast_to([128, NC, C]), ALU.add).then_inc(hb_done, 1)
                    wait(pool, n_tc, at(0))
                    pool.tensor_copy(clsT[:, :, :, bass.ds(at(-1), 1)].rearrange("p k i a -> p k (i a)"),
                                     xnT[1 - par][:, :, 0:NCLS]).then_inc(cls_done, 1)

            steps(pool, body)
            pool.memset(own[:, :, :], 1.0).then_inc(s_zero, 1)
            pool.wait_ge(s_zero, 3)
            pool.affine_select(out=own[:, :, :], in_=own[:, :, :], compare_op=ALU.is_ge, fill=0.0, base=0,
                               pattern=[[0, 2], [-B, NCLS]], channel_multiplier=1).then_inc(s_zero, 1)
            pool.wait_ge(s_zero, 4)
            pool.affine_select(out=own[:, :, :], in_=own[:, :, :], compare_op=ALU.is_ge, fill=0.0, base=B - 1,
                               pattern=[[0, 2], [B, NCLS]], channel_multiplier=-1).then_inc(s_const, 1)
            pool.memset(sel[:, :, :, :], 0.0).then_inc(s_zero, 1)
            pool.wait_ge(s_zero, 5)
            pool.affine_select(out=sel[:, 0, :, :].rearrange("p (l s) b -> p l s b", s=2),
                               in_=sel[:, 0, :, :].rearrange("p (l s) b -> p l s b", s=2),
                               compare_op=ALU.not_equal, fill=1.0, base=-3,
                               pattern=[[0, 3], [-1, 2], [0, B]], channel_multiplier=1).then_inc(s_const, 1)
            pool.affine_select(out=sel[:, 1, :, :].rearrange("p (l s) b -> p l s b", s=2),
                               in_=sel[:, 1, :, :].rearrange("p (l s) b -> p l s b", s=2),
                               compare_op=ALU.not_equal, fill=1.0, base=0,
                               pattern=[[-1, 3], [0, 2], [0, B]], channel_multiplier=1).then_inc(s_const, 1)
            pool.wait_ge(pv[G - 1], B)
            pool.memset(hexp[:, 3:5, :, :], 0.0).then_inc(s_const, 1)

        @block.scalar
        def _(act):
            def body(at, t, par):
                attn, front, back, ffn = has(t)

                def gelu(f):
                    if ffn:
                        wait(act, f1[f], at(-1))
                        if f == 0:
                            wait(act, f2, at(-2))
                        nc.scalar.activation(hid[:, f, NCLS:N], PS[:, 4 + f % 2, NCLS:N], ACT.Gelu, bias=mb1_sb[:, f:f + 1])\
                            .then_inc(gelud[f], 1)

                def exp(u):
                    if attn:
                        wait(act, scoresT[u], at(1))
                        if u == 0:
                            wait(act, pv[G - 1], at(0))
                        if u >= 4:
                            wait(act, pv[0], at(1))
                        nc.scalar.activation(probs[:, u % 4, :, :, :].rearrange("p a c n -> p (a c n)"),
                                             PS[:, 2 * (u % 2):2 * (u % 2) + 2, :].rearrange("p a n -> p (a n)"),
                                             ACT.Exp, scale=float(D) ** -0.5).then_inc(expd[u], 1)

                def out_t(g):
                    if attn:
                        wait(act, pv[g], at(1))
                        if g == 0:
                            wait(act, o_t, at(0))
                        nc.scalar.copy(oT[:, g, :], PS[:, PV_BANK[g], 0:N]).then_inc(oT_done[g], 1)

                def load_table(func):
                    nc.scalar.activation(spare[0:1, :], mb1_sb[0:1, 0:1], func, scale=0.0)

                if ffn:
                    load_table(ACT.Gelu)
                for f in range(3):
                    gelu(f)
                if front:
                    wait(act, tok_t, at(2))
                    wait(act, h_ps, at(1))
                    nc.scalar.copy(tok_inT[:, :], PS[:, 7, 0:N]).then_inc(tok_c, 1)
                gelu(3)
                gelu(4)
                if front:
                    wait_alone(act, h_ps, at(2))
                    nc.scalar.copy(h_all[:, bass.ds(at(1), 1), :, :].rearrange("p a c n -> p (a c n)"), PS[:, 7, 0:NC * C])\
                        .then_inc(h_sb, 1)
                gelu(5)
                if attn:
                    wait(act, shift_t, at(1))
                    wait(act, shift_rows, at(0), 16)
                    nc.scalar.copy(shiftT[:, :], PSb[0:2 * H, 7, 0:N]).then_inc(shift_c, 1)
                    load_table(ACT.Exp)
                exp(0)
                exp(1)
                exp(2)
                if front:
                    for c in range(NC):
                        wait(act, qk_ps[c], at(2))
                        if c == 0:
                            wait(act, dup_done, at(1))
                            wait(act, q_steps[6], at(2))
                        nc.scalar.activation(part1[:, :, c, :], PS[:, QK_BANK[c], 0:2 * C].rearrange("p (s n) -> p s n", s=2),
                                             ACT.Copy, scale=sc_q[:, 6, c:c + 1]).then_inc(p1_done[c], 1)
                exp(3)
                out_t(0)
                exp(4)
                exp(5)
                out_t(1)
                out_t(2)
                if front:
                    wait(act, v_ps, at(2))
                    wait(act, pv[G - 1], at(1))
                    for c in range(NC):
                        last = nc.scalar.activation(vals[:, c, :, 0:D],
                                                    PS[:, 7, C * c:C * (c + 1)].rearrange("p (h d) -> p h d", d=D),
                                                    ACT.Copy, scale=sc_q[:, 6, c:c + 1])
                    last.then_inc(v_sb, 1)
                    for w in BY_ACT:
                        wait(act, stk_t[w], at(2))
                        nc.scalar.copy(qk[1 - par][0:96, :, 2 * w:2 * w + 2, :].rearrange("p s h n -> p s (h n)"),
                                       PSb[0:96, STACK_BANK[w], :].rearrange("p (s n) -> p s n", s=2)).then_inc(stk_c[w], 1)
                if back:
                    wait(act, n_t, at(0))
                    wait(act, f1[NF - 1], at(-2))
                    wait(act, cls_done, at(-2))
                    nc.scalar.copy(xnT[1 - par][:, :, :].rearrange("p k n -> p (k n)"), PS[0:96, 4, :]).then_inc(n_tc, 1)

            for i in range(HOT):
                act.wait_ge(s_fps, i + 1)
                nc.scalar.copy(gath1[:, 8 - HOT + i, :], PS[:, i, 0:B * P1]).then_inc(s_fsb, 1)
            for k in range(11):
                act.wait_ge(s_fps, HOT + k + 1)
                nrow = GP * P0 if k == 0 else 96
                nc.scalar.copy(fused[0:nrow, k, :], PS[0:nrow, k % 8, 0:C]).then_inc(s_fsb, 1)
            for k in range(8):
                act.wait_ge(s_fps, W_STEPS + k + 1)
                dst = (x2T if k < 4 else x1T)[:, :, 4 * (k % 4):4 * (k % 4) + 4, :]
                src = PS[0:96, k, :].rearrange("p (b j n) -> p j b n", b=4, j=8 if k < 4 else 2)
                nc.scalar.copy(dst, src).then_inc(s_fsb, 1)
            act.wait_ge(s_zc, 10)
            zpair = zall[0:T1, :, :].rearrange("p (a e) n -> p a e n", e=2)
            for e in range(2):
                act.dma_start(zpair[:, :, e, :], z1[T1 * e:T1 * (e + 1), :, :]).then_inc(s_zall, 16)
            act.wait_ge(s_fw, 48)
            steps(act, body)

            act.wait_ge(s_const, 4)
            for a in range(NEXP):
                act.wait_ge(e_b, a + 1)
                if a < 3:
                    view = hexp[:, 3:5, :, :].rearrange("p c f (l s b) -> p c s f l b", l=3, s=2)
                    for s in range(2):
                        last = nc.scalar.activation(view[:, s, s, :, a, :], hpre[:, a % 2, :, s, :], ACT.Gelu)
                else:
                    view = hexp[:, 0:3, :, :].rearrange("p c f (l s b) -> p c l s f b", l=3, s=2)
                    for l in range(3):
                        last = nc.scalar.activation(view[:, l, l, a - 3, :, :], hpre[:, a % 2, :, l, :], ACT.Gelu)
                last.then_inc(e_g, 1)
            act.wait_ge(e_gate, 4)
            nc.scalar.activation(gate[:, 3:5], gate[:, 3:5], ACT.Exp).then_inc(e_gate, 1)

        @block.vector
        def _(dve):
            V = nc.vector
            V.memset(ones[:, :], 1.0).then_inc(s_bw, 1)
            for q in qk:
                V.memset(q[96:98, 1, :, :], 1.0)
            dve.wait_ge(s_row, 32)
            V.tensor_copy(row_f, row_i).then_inc(s_hot, 1)
            dve.wait_ge(s_hot, 1)
            dve.wait_ge(s_pool, 1)
            for i in range(HOT):
                if i >= 2:
                    dve.wait_ge(s_fps, i - 1)
                V.tensor_tensor(hot[i % 2][:, :, :], row_f[:, 128 * i:128 * (i + 1)].unsqueeze(1).broadcast_to([128, X1, 128]),
                                patch_no[:, :].unsqueeze(2).broadcast_to([128, X1, 128]), ALU.is_equal).then_inc(s_hot, 1)
            V.memset(neg_half[:, :], -0.5)
            V.memset(vals[:, :, :, D:32], 0.0).then_inc(s_vc, 1)
            dve.wait_ge(s_vc, 1)
            V.memset(vals[:, :, :, D:D + 1], 1.0).then_inc(s_bw, 1)
            dve.wait_ge(s_tw, 96)
            dve.wait_ge(s_bw, 2)
            V.tensor_copy(b012_wide[:, :, :], b012_sb[:, :].unsqueeze(2).broadcast_to([64, 3, 128])).then_inc(s_bw, 1)
            dve.wait_ge(s_g12, 16 * (10 - HOT))
            dve.wait_ge(s_fsb, HOT)
            V.tensor_copy(pat2.rearrange("p b (t n) -> p b t n", t=2), gath2.rearrange("p t (b n) -> p b t n", b=B))\
             .then_inc(s_pat, 1)
            V.tensor_copy(pat1.rearrange("p b (t n) -> p b t n", t=8), gath1.rearrange("p t (b n) -> p b t n", b=B))\
             .then_inc(s_pat, 1)
            dve.wait_ge(s_aw, 80)
            for k, (a, b) in enumerate(((0, 3 * C), (3 * C, 4 * C))):
                last = V.tensor_reduce(wabs[:, k:k + 1], w_raw[:, :, a:b], AX.XY, ALU.add, apply_absolute_value=True)
            last.then_inc(s_wsum, 1)
            dve.wait_ge(s_fps, W_STEPS)
            V.tensor_copy(zbias[:, :], PS[:, 3, 0:C]).then_inc(s_vc, 1)
            V.memset(hid[:, :, 0:NCLS], 0.0)
            dve.wait_ge(s_wsum, 2)
            V.tensor_scalar(wscale[:, 0:1], PS[:, 7, 0:1], 1.0 / (3 * C * C), EPS, ALU.mult, ALU.max)
            V.tensor_scalar(wscale[:, 1:2], PS[:, 7, 1:2], 1.0 / (C * C), EPS, ALU.mult, ALU.max).then_inc(s_wt, 1)
            dve.wait_ge(s_wt, 1)
            V.reciprocal(wscale[:, 2:4], wscale[:, 0:2]).then_inc(s_wt, 1)
            V.tensor_scalar(wsq[:, :], wscale[:, 0:2], 1.0 / QMAX, None, ALU.mult).then_inc(s_wt, 1)
            dve.wait_ge(s_wt, 3)
            for k, (a, b) in enumerate(((0, 3 * C), (3 * C, 4 * C))):
                V.tensor_scalar(w_rnd[:, :, a:b], w_raw[:, :, a:b], wscale[0:96, 2 + k:3 + k], MAGIC, ALU.mult, ALU.add)\
                 .then_inc(s_wt, 1)
            dve.wait_ge(s_wt, 5)
            V.tensor_scalar(w_raw[:, :, :], w_rnd[:, :, :], -MAGIC, 1.0, ALU.add, ALU.min).then_inc(s_wt, 1)
            dve.wait_ge(s_wt, 6)
            V.tensor_scalar(wq[:, :, :], w_raw[:, :, 0:3 * C], -1.0, None, ALU.max).then_inc(s_wt, 1)
            V.tensor_scalar(wp[:, :, :], w_raw[:, :, 3 * C:4 * C], -1.0, None, ALU.max).then_inc(s_wt, 1)
            dve.wait_ge(s_pool, 4)
            for lev, n_in in enumerate((T1, T2)):
                last = V.tensor_scalar(pos[:, lev, :], pos[:, lev, :], n_in / N, 0.5 * n_in / N - 0.5, ALU.mult, ALU.add)
            last.then_inc(s_vc, 1)
            dve.wait_ge(s_vc, 3)
            for lev, n_in in enumerate((T1, T2)):
                last = V.tensor_scalar(pos[:, lev, :], pos[:, lev, :], 0.0, float(n_in - 1), ALU.max, ALU.min)
            last.then_inc(s_vc, 1)
            dve.wait_ge(s_vc, 4)
            for lev, (a, b) in enumerate(((0, T1), (T1, ZR))):
                for c in range(NC):
                    last = V.tensor_scalar(hat[:, c, a:b], hat[:, c, a:b], pos[:, lev, c:c + 1], None, ALU.subtract)
            last.then_inc(s_bw, 1)
            dve.wait_ge(s_bw, 4)
            V.scalar_tensor_tensor(hat[:, :, :], hat[:, :, :], -1.0, hat[:, :, :], ALU.mult, ALU.max).then_inc(s_vc, 1)
            dve.wait_ge(s_vc, 5)
            V.tensor_scalar(hat[:, :, :], hat[:, :, :], -1.0, 1.0, ALU.mult, ALU.add).then_inc(s_bw, 1)
            dve.wait_ge(s_bw, 5)
            V.tensor_scalar(tok_in[:, :, 0:ZR], hat[:, :, :], 0.0, None, ALU.max).then_inc(s_vc, 1)
            for k in range(10):
                dve.wait_ge(s_fps, T_STEPS + k + 1)
                if k < 2:
                    V.tensor_copy(z2[:, k, :], PS[:, k, 0:C]).then_inc(s_zc, 1)
                else:
                    V.tensor_tensor(z1[:, k - 2, :], PS[:, k % 8, 0:C], zbias[:, :], ALU.add).then_inc(s_zc, 1)

            def floor(k, stp, sc):
                V.tensor_tensor(sc[:, 3, :], sc[:, 2, :], sc[:, 1, :], ALU.mult).then_inc(stp[3], 1)
                wait(dve, stp[3], k)
                V.tensor_scalar(sc[:, 3, :], sc[:, 3, :], EPS, None, ALU.max).then_inc(stp[4], 1)

            def invert(k, stp, sc):
                wait(dve, stp[4], k)
                V.reciprocal(sc[:, 4, :], sc[:, 3, :]).then_inc(stp[5], 1)

            def factors(k, stp, sc, w):
                wait(dve, stp[5], k)
                V.tensor_scalar(sc[:, 6, :], sc[:, 3, :], w, None, ALU.mult)
                V.scalar_tensor_tensor(sc[:, 5, :], sc[:, 4, :], QMAX, sc[:, 1, :], ALU.mult, ALU.mult).then_inc(stp[6], 1)

            def rounded(k, stp, sc, u, r):
                wait(dve, stp[6], k)
                for c in range(NC):
                    last = V.tensor_scalar(r[:, c, :], u[:, c, :], sc[:, 5, c:c + 1], MAGIC, ALU.mult, ALU.add)
                last.then_inc(stp[7], 1)

            def body(at, t, par):
                attn, front, back, ffn = has(t)

                def row_max(u):
                    if attn:
                        wait(dve, scores[u], at(1))
                        if u == 0:
                            wait(dve, shift_done, at(0))
                        V.tensor_reduce(negmax[:, 2 * u:2 * u + 2, :],
                                        PS[:, 2 * (u % 2):2 * (u % 2) + 2, :].rearrange("p a (c n) -> p a c n", c=NC),
                                        AX.X, ALU.max, negate=True).then_inc(maxed[u], 1)

                def ffn_rows():
                    if ffn:
                        wait(dve, f2, at(-1))
                        wait(dve, hb_done, at(-1))
                        for c in range(NC):
                            wait(dve, stored[c], at(-2), 16)
                            V.tensor_tensor(o_sb[:, c, :], PS[:, 6, C * c:C * (c + 1)], hb[par][:, c, :], ALU.add)\
                             .then_inc(out_done[c], 1)

                def copy_stack(w):
                    wait(dve, stk_t[w], at(2))
                    V.tensor_copy(qk[1 - par][0:96, :, 2 * w:2 * w + 2, :].rearrange("p s h n -> p s (h n)"),
                                  PSb[0:96, STACK_BANK[w], :].rearrange("p (s n) -> p s n", s=2)).then_inc(stk_c[w], 1)

                def less_first(c):
                    wait(dve, p1_done[c], at(2))
                    V.scalar_tensor_tensor(rest[:, :, c, :], PS[:, QK_BANK[c], 0:2 * C].rearrange("p (s n) -> p s n", s=2),
                                           sc_q[:, 6, c:c + 1], part1[:, :, c, :], ALU.mult, ALU.subtract)\
                        .then_inc(rest_done[c], 1)

                for u in range(U):
                    row_max(u)
                if attn:
                    wait(dve, maxed[U - 1], at(1))
                    wait(dve, shift_t, at(0))
                    hi = shift[:, :, 0, :].rearrange("p c h -> p h c")
                    lo = shift[:, :, 1, :].rearrange("p c h -> p h c")
                    V.tensor_copy(hi, negmax[:, :, :]).then_inc(shift_hi, 1)
                    wait(dve, shift_hi, at(1))
                    V.tensor_tensor(lo, negmax[:, :, :], hi, ALU.subtract).then_inc(shift_done, 1)
                if front:
                    hn = h_all[:, bass.ds(at(1), 1), :, :].rearrange("p a c n -> p (a c) n")
                    wait_alone(dve, h_sb, at(2))
                    for c in range(NC):
                        last = V.bn_stats(st_q[:, c, :], hn[:, c, :])
                    last.then_inc(q_steps[8], 1)
                if back:
                    wait(dve, o_t, at(0))
                    ov = PS[:, 0:2, 0:128 * G].rearrange("p c (h e) -> p c h e", e=32)
                    V.reciprocal(recip[:, :, :], ov[:, :, :, D]).then_inc(o_rec, 1)
                if front:
                    wait_alone(dve, q_steps[8], at(2))
                    for c in range(NC):
                        last = V.bn_aggr(mv_q[:, c, :], st_q[:, c, :])
                    last.then_inc(q_steps[0], 1)
                if back:
                    wait(dve, o_rec, at(0))
                    V.tensor_tensor(o[:, :, :, :], ov[:, :, :, 0:D],
                                    recip[:, :, :].unsqueeze(3).broadcast_to([128, NC, H, D]), ALU.mult).then_inc(o_sbd, 1)
                if front:
                    wait(dve, q_steps[0], at(2))
                    wait(dve, v_sb, at(1))
                    V.tensor_scalar(sc_q[:, 0, :], mv_q[:, :, 1], 1.0 + EPS, EPS * EPS, ALU.mult, ALU.add)\
                        .then_inc(q_steps[1], 1)
                    for c in range(NC):
                        last = V.scalar_tensor_tensor(u_q[:, c, :], hn[:, c, :], mv_q[:, c, 0:1], gq_sb[:, :],
                                                      ALU.subtract, ALU.mult)
                    last.then_inc(q_steps[2], 1)
                if back:
                    of = o[:, :, :, :].rearrange("p c h d -> p c (h d)")
                    wait_alone(dve, o_sbd, at(0))
                    for c in range(NC):
                        last = V.bn_stats(st_p[:, c, :], of[:, c, :])
                    last.then_inc(p_steps[8], 1)
                if front:
                    wait(dve, q_steps[2], at(2))
                    V.tensor_reduce(sc_q[:, 2, :], u_q[:, :, :], AX.X, ALU.max, apply_absolute_value=True).then_inc(q_steps[9], 1)
                if back:
                    wait_alone(dve, p_steps[8], at(0))
                    for c in range(NC):
                        last = V.bn_aggr(mv_p[:, c, :], st_p[:, c, :])
                    last.then_inc(p_steps[9], 1)
                if front:
                    wait(dve, q_steps[9], at(2))
                    wait(dve, q_pow, at(2))
                    wait(dve, q_int, at(1))
                    floor(at(2), q_steps, sc_q)
                if back:
                    wait(dve, p_steps[9], at(0))
                    V.tensor_tensor(sc_p[:, 7, :], mv_p[:, :, 0], mv_p[:, :, 0], ALU.mult).then_inc(p_steps[0], 1)
                if front:
                    invert(at(2), q_steps, sc_q)
                if back:
                    wait(dve, p_steps[0], at(0))
                    V.scalar_tensor_tensor(sc_p[:, 0, :], sc_p[:, 7, :], EPS, mv_p[:, :, 1], ALU.add, ALU.add)\
                        .then_inc(p_steps[1], 1)
                if front:
                    factors(at(2), q_steps, sc_q, wsq[:, 0:1])
                if front:
                    rounded(at(2), q_steps, sc_q, u_q, r_q)
                if back:
                    wait(dve, p_steps[2], at(0))
                    V.tensor_reduce(sc_p[:, 2, :], u_p[:, :, :], AX.X, ALU.max, apply_absolute_value=True).then_inc(n_steps[0], 1)
                    wait(dve, n_steps[0], at(0))
                    wait(dve, p_pow, at(0))
                    wait(dve, p_int, at(-1))
                    floor(at(0), p_steps, sc_p)
                    invert(at(0), p_steps, sc_p)
                if front:
                    wait(dve, q_t, at(2))
                    wait(dve, v_ps, at(1))
                    V.tensor_copy(iT_q[:, :, :].rearrange("p k n -> p (k n)"), PSb[0:96, 7, 0:2 * N]).then_inc(q_tc, 1)
                if attn:
                    ffn_rows()
                if back:
                    factors(at(0), p_steps, sc_p, wsq[:, 1:2])
                    rounded(at(0), p_steps, sc_p, u_p, r_p)
                if front:
                    wait(dve, p3_done[0], at(1))
                    less_first(0)
                    less_first(1)
                if back:
                    wait(dve, p_t, at(0))
                    wait(dve, p_ps, at(-1))
                    V.tensor_copy(iT_p[:, :, :].rearrange("p k n -> p (k n)"), PSb[0:96, 4, 0:2 * N]).then_inc(p_tc, 1)
                if front:
                    wait(dve, stk_t[U - 1], at(1))

                    def dup(side, part, first, last_, step):
                        src = part[:, side, :, :].rearrange("p c (h d) -> p (c h) d", d=D)
                        dst = stack[:, side, :, :, :].rearrange("p c h (s d) -> p (c h) s d", d=D)[:, :, first:last_:step, :]
                        n = len(range(first, last_, step))
                        return V.tensor_copy(dst, src.unsqueeze(2).broadcast_to([128, NC * H, n, D]))

                    dup(0, part1, 0, 3, 1)
                    dup(1, part1, 0, 1, 1)
                    dup(1, part1, 3, 6, 2)
                if back:
                    wait(dve, p_ps, at(0))
                    hr = h_all[:, bass.ds(at(-1), 1), :, :].rearrange("p a c n -> p (a c) n")
                    for c in range(NC):
                        last = V.scalar_tensor_tensor(hr[:, c, :], PS[:, 4, C * c:C * (c + 1)], sc_p[:, 6, c:c + 1],
                                                      hr[:, c, :], ALU.mult, ALU.add)
                    last.then_inc(n_steps[1], 1)
                if front:
                    wait(dve, p2_done[0], at(2))
                    wait(dve, p2_done[1], at(2))
                    third_part(V, 1).then_inc(p3_done[1], 1)
                if front:
                    dup(0, part2, 3, 5, 1)
                    dup(1, part2, 1, 5, 3).then_inc(dup_done, 1)
                if back:
                    wait_alone(dve, n_steps[1], at(0))
                    for c in range(NC):
                        last = V.bn_stats(st_n[:, c, :], hr[:, c, :])
                    last.then_inc(n_steps[3], 1)
                    wait_alone(dve, n_steps[3], at(0))
                    for c in range(NC):
                        last = V.bn_aggr(mv_n[:, c, :], st_n[:, c, :])
                    last.then_inc(n_steps[4], 1)
                    wait(dve, n_steps[4], at(0))
                    V.tensor_scalar(sc_n[:, 0, :], mv_n[:, :, 1], EPS, None, ALU.add).then_inc(n_steps[2], 1)
                if front:
                    copy_stack(0)
                if back:
                    wait(dve, n_pow, at(0))
                    wait(dve, n_t, at(-1))
                    for c in range(NC):
                        last = V.tensor_scalar(xn[:, c, :], hr[:, c, :], mv_n[:, c, 0:1], sc_n[:, 1, c:c + 1],
                                               ALU.subtract, ALU.mult)
                    last.then_inc(xn_done, 1)
                if front:
                    for w in range(1, U):
                        if w not in BY_ACT:
                            copy_stack(w)
                if not attn:
                    ffn_rows()

            steps(dve, body)

            dve.wait_ge(e_h, 1)
            dve.wait_ge(s_const, 3)
            V.tensor_tensor(logit[:, :, :], PS[0:NCLS * B, 7, 0:2 * NCLS].rearrange("p (i e) -> p e i", e=2), own[:, :, :],
                            ALU.mult).then_inc(e_gate, 1)
            dve.wait_ge(e_gate, 1)
            V.tensor_reduce(gate[:, 0:2], logit[:, :, :], AX.X, ALU.add).then_inc(e_gate, 1)
            dve.wait_ge(e_gate, 2)
            V.tensor_reduce(gate[:, 2:3], gate[:, 0:2], AX.X, ALU.max).then_inc(e_gate, 1)
            dve.wait_ge(e_gate, 3)
            V.tensor_scalar(gate[:, 3:5], gate[:, 0:2], gate[:, 2:3], None, ALU.subtract).then_inc(e_gate, 1)

            def expert_bias(a):
                dve.wait_ge(e_h, a + 2)
                if a >= 2:
                    dve.wait_ge(e_g, a - 1)
                pair = 2 * (a % 3)
                for half in range(2):
                    src = PS[:, pair + half, 0:3 * NCLS * B]
                    if a < 3:
                        src = src.rearrange("p (f l s b) -> p f l s b", f=3, l=3, s=2)[:, :, a, :, :]
                        n = 2
                    else:
                        src = src.rearrange("p (f l s b) -> p f l s b", f=3, l=3, s=2)[:, :, :, a - 3, :]
                        n = 3
                    bias = ab1_sb[:, a, 3 * half:3 * half + 3].unsqueeze(2).unsqueeze(3).broadcast_to([128, 3, n, B])
                    last = V.tensor_tensor(hpre[:, a % 2, 3 * half:3 * half + 3, 0:n, :], src, bias, ALU.add)
                last.then_inc(e_b, 1)

            dve.wait_ge(pv[G - 1], B)
            for a in range(NEXP):
                expert_bias(a)
            dve.wait_ge(e_gate, 5)
            V.tensor_reduce(gate[:, 5:6], gate[:, 3:5], AX.X, ALU.add).then_inc(e_gate, 1)
            dve.wait_ge(e_gate, 6)
            V.reciprocal(gate[:, 6:7], gate[:, 5:6]).then_inc(e_gate, 1)
            dve.wait_ge(e_gate, 7)
            V.tensor_scalar(gate[:, 7:9], gate[:, 3:5], gate[:, 6:7], None, ALU.mult).then_inc(e_gate, 1)
            dve.wait_ge(e_gate, 8)
            V.tensor_reduce(gate[:, 9:10], gate[:, 7:9], AX.X, ALU.min).then_inc(e_gate, 1)
            dve.wait_ge(e_gate, 9)
            V.scalar_tensor_tensor(gate[:, 10:12], gate[:, 7:9], gate[:, 9:10], gate[:, 7:9], ALU.is_gt, ALU.mult).then_inc(e_gate, 1)
            dve.wait_ge(e_gate, 10)
            V.tensor_reduce(gate[:, 12:13], gate[:, 10:12], AX.X, ALU.add).then_inc(e_gate, 1)
            dve.wait_ge(e_gate, 11)
            V.tensor_scalar(gate[:, 12:13], gate[:, 12:13], 1e-6, None, ALU.max).then_inc(e_gate, 1)
            dve.wait_ge(e_gate, 12)
            V.reciprocal(gate[:, 13:14], gate[:, 12:13]).then_inc(e_gate, 1)
            dve.wait_ge(e_gate, 13)
            V.tensor_scalar(gate[:, 14:16], gate[:, 10:12], gate[:, 13:14], None, ALU.mult).then_inc(e_gate, 1)
            dve.wait_ge(e_gate, 14)
            dve.wait_ge(e_hcls, 16)
            dve.wait_ge(e_h, NEXP + 2)
            V.scalar_tensor_tensor(ocls[:, :], PS[0:NCLS * B, 6, 0:C], gate[:, 14:15], hcls[:, :], ALU.mult, ALU.add)\
             .then_inc(e_fin, 1)
            dve.wait_ge(e_fin, 1)
            dve.wait_ge(e_h, NEXP + 3)
            V.scalar_tensor_tensor(ocls[:, :], PS[0:NCLS * B, 7, 0:C], gate[:, 15:16], ocls[:, :], ALU.mult, ALU.add)\
             .then_inc(e_fin, 1)

        @block.tensor
        def _(pe):
            T = nc.tensor

            def mm(o_, l, r, first=True, final=True):
                return T.matmul(o_, l, r, start=first, stop=final)

            for i in range(HOT):
                pe.wait_ge(s_hot, i + 2)
                if i == 0:
                    pe.wait_ge(s_row, 32)
                for k in range(X1):
                    last = mm(PS[:, i, 0:B * P1], hot[i % 2][:, k, :], x1_sb[:, k, :], k == 0, k == X1 - 1)
                last.then_inc(s_fps, 1)
            pe.wait_ge(s_tw, 96)
            for k in range(11):
                if k < HOT:
                    pe.wait_ge(s_fsb, k + 1)
                if k >= 8:
                    pe.wait_ge(s_fsb, HOT + k - 7)
                if k == 0:
                    mm(PS[0:GP * P0, 0, 0:C], w0_sb[:, :], wf_sb[:, 0, :]).then_inc(s_fps, 1)
                elif k < 3:
                    mm(PS[0:96, k, 0:C], w1_sb[:, 96 * (k - 1):96 * k], wf_sb[:, 1, :]).then_inc(s_fps, 1)
                else:
                    mm(PS[0:96, k % 8, 0:C], w2_sb[:, 96 * (k - 3):96 * (k - 2)], wf_sb[:, 2, :]).then_inc(s_fps, 1)
            pe.wait_ge(s_bw, 3)
            pe.wait_ge(s_fsb, HOT + 4)
            for lev in range(3):
                mm(PS[:, 3, 0:C], b012_wide[:, lev, :], wf_sb[:, lev, :], lev == 0, False)
            mm(PS[:, 3, 0:C], ones[0:1, :], bf_sb[:, :], False, True).then_inc(s_fps, 1)
            pe.wait_ge(s_wsum, 1)
            pe.wait_ge(s_fsb, HOT + 8)
            mm(PS[:, 7, 0:2], ones[0:96, :], wabs[:, :]).then_inc(s_wsum, 1)
            pe.wait_ge(s_id, 2)
            pe.wait_ge(s_fsb, HOT + 11)
            pe.wait_ge(s_vc, 2)
            for k in range(8):
                src = pat2 if k < 4 else pat1
                if k % 4 == 0:
                    pe.wait_ge(s_pat, 1 + k // 4)
                if k == 7:
                    pe.wait_ge(s_wt, 1)
                for e in range(4):
                    b = 4 * (k % 4) + e
                    last = T.transpose(PS[0:96, k, 128 * e:128 * (e + 1)], src[:, b, :], ident[:, :])
                last.then_inc(s_fps, 1)
            for k in range(10):
                if k == 0:
                    pe.wait_ge(s_fsb, HOT + 15)
                if k == 2:
                    pe.wait_ge(s_fsb, HOT + 19)
                if k >= 8:
                    pe.wait_ge(s_zc, k - 7)
                if k < 2:
                    for j8 in range(8):
                        last = mm(PS[:, k, 0:C], x2T[:, j8, 8 * k:8 * k + 8, :].rearrange("p b n -> p (b n)"), fused[:, 3 + j8, :],
                                  j8 == 0, j8 == 7)
                else:
                    b = 2 * (k - 2)
                    for jh in range(2):
                        last = mm(PS[:, k % 8, 0:C], x1T[:, jh, b:b + 2, :].rearrange("p b n -> p (b n)"), fused[:, 1 + jh, :],
                                  jh == 0, jh == 1)
                last.then_inc(s_fps, 1)
            pe.wait_ge(s_zc, 10)
            pe.wait_ge(s_zall, 16 * (B + 10))
            pe.wait_ge(s_wt, 8)
            pe.wait_ge(s_fw, 48)

            tok = clsT[:, :, :, :].rearrange("p k i b -> p k (i b)")

            def first_layer(a):
                if a >= 3:
                    pe.wait_ge(e_b, a - 2)
                if a == 2:
                    pe.wait_ge(gelud[NF - 1], B)
                for f in range(NF):
                    for k in range(KC):
                        last = mm(PS[:, 2 * (a % 3) + f // 3, NCLS * B * (f % 3):NCLS * B * (f % 3 + 1)],
                                  aw1_sb[:, a, k, 128 * f:128 * (f + 1)], tok[:, k, :], k == 0, k == KC - 1)
                last.then_inc(e_h, 1)

            def gates_and_first_expert():
                pe.wait_ge(s_ew, 80)
                pe.wait_ge(cls_done, B)
                pe.wait_ge(n_tc, B)
                for k in range(KC):
                    last = mm(PS[0:NCLS * B, 7, 0:2 * NCLS], tok[:, k, :], gw_sb[:, k, :], k == 0, k == KC - 1)
                last.then_inc(e_h, 1)
                first_layer(0)

            def body(at, t, par):
                attn, front, back, ffn = has(t)

                def score(u):
                    if attn:
                        wait(pe, stk_c[u], at(1))
                        if u < 2:
                            for w in (1 + 2 * u, 2 + 2 * u):
                                wait(pe, stk_c[w], at(1))
                        else:
                            wait(pe, maxed[u - 2], at(1))
                        for hh in range(2):
                            for c in range(NC):
                                last = mm(PS[:, 2 * (u % 2) + hh, N * c:N * (c + 1)],
                                          qk[par][0:96, 0, 2 * u + hh, 128 * c:128 * (c + 1)],
                                          qk[par][0:96, 1, 2 * u + hh, :])
                        last.then_inc(scores[u], 1)

                def score_t(u):
                    if attn:
                        if u < 2:
                            wait(pe, maxed[4 + u], at(1))
                            if u == 0 and back:
                                wait(pe, o_sbd, at(0))
                        else:
                            wait(pe, expd[u - 2], at(1))
                        if u == 0:
                            wait(pe, shift_rows, at(1), 16)
                        for hh in range(2):
                            for c in range(NC):
                                last = mm(PS[:, 2 * (u % 2) + hh, N * c:N * (c + 1)],
                                          qk[par][:, 1, 2 * u + hh, 128 * c:128 * (c + 1)],
                                          qk[par][:, 0, 2 * u + hh, :])
                        last.then_inc(scoresT[u], 1)

                def weighted(g):
                    if attn:
                        wait(pe, expd[2 * g], at(1))
                        wait(pe, expd[2 * g + 1], at(1))
                        if g == 0:
                            wait(pe, v_sb, at(1))
                            if ffn:
                                wait(pe, out_done[0], at(-1))
                                wait(pe, out_done[1], at(-1))
                            else:
                                wait(pe, oT_done[G - 1], at(0))
                                wait(pe, stk_c[5], at(1))
                        elif g == 1:
                            wait(pe, oT_done[0], at(1))
                        elif back:
                            wait(pe, n_steps[1], at(0))
                        for c in range(NC):
                            for j in range(4):
                                last = mm(PS[32 * j:32 * (j + 1), PV_BANK[g], 0:N], vals[:, c, 4 * g + j, :],
                                          probs[:, (2 * g + j // 2) % 4, j % 2, c, :], c == 0, c == NC - 1)
                        last.then_inc(pv[g], 1)

                def hidden(f):
                    if ffn:
                        if f == 0:
                            wait(pe, n_tc, at(-1))
                        elif f == 1:
                            wait(pe, stk_c[0], at(1))
                        else:
                            wait(pe, gelud[f - 2], at(-1))
                        for k in range(KC):
                            last = mm(PS[:, 4 + f % 2, NCLS:N], mw1_sb[:, k, 128 * f:128 * (f + 1)], xnT[par][:, k, NCLS:N],
                                      k == 0, k == KC - 1)
                        last.then_inc(f1[f], 1)

                def outputs_by_token():
                    if back:
                        for g in range(G):
                            wait(pe, oT_done[g], at(0))
                        if attn:
                            wait(pe, maxed[4], at(1))
                        else:
                            wait(pe, expd[4], at(0))
                        for c in range(NC):
                            for g in range(G):
                                last = T.transpose(PS[:, c, 128 * g:128 * (g + 1)], oT[:, g, 128 * c:128 * (c + 1)], ident[:, :])
                        last.then_inc(o_t, 1)

                def ffn_out(c, first, last_):
                    for f in range(first, last_):
                        last = mm(PS[:, 6, C * c:C * (c + 1)], hid[:, f, 128 * c:128 * (c + 1)], mw2_sb[:, f, :],
                                  f == 0, f == NF - 1)
                    return last

                def transpose_ints(bank, ints, done):
                    for k in range(KC):
                        for c in range(NC):
                            last = T.transpose(PSb[0:96, bank, N * k + 128 * c:N * k + 128 * (c + 1)],
                                               ints[:, c, 96 * k:96 * (k + 1)], identb[:, :])
                    last.then_inc(done, 1)

                def projection_in():
                    if back:
                        wait(pe, p_int, at(0))
                        if ffn:
                            wait(pe, gelud[4], at(-1))
                        transpose_ints(4, i_p, p_t)

                def projection():
                    if back:
                        wait(pe, p_tc, at(0))
                        for c in range(NC):
                            for k in range(KC):
                                last = mm(PS[:, 4, C * c:C * (c + 1)], iT_p[:, k, 128 * c:128 * (c + 1)], wp[:, k, :],
                                          k == 0, k == KC - 1)
                        last.then_inc(p_ps, 1)

                def transpose_shift():
                    if attn:
                        wait(pe, shift_done, at(1))
                        if front:
                            wait(pe, h_sb, at(2))
                        else:
                            wait(pe, v_sb, at(1))
                        for c in range(NC):
                            last = T.transpose(PSb[0:2 * H, 7, 128 * c:128 * (c + 1)],
                                               shift[:, c, :, :].rearrange("p r h -> p (r h)"), identb[:, :])
                        last.then_inc(shift_t, 1)

                if not attn:
                    outputs_by_token()
                score(0)
                score(1)
                hidden(0)
                hidden(1)
                if front:
                    wait(pe, tok_ready, at(2))
                    wait(pe, v_sb, at(1))
                    for c in range(NC):
                        last = T.transpose(PS[:, 7, 128 * c:128 * (c + 1)], tok_in[:, c, :], ident[:, :])
                    last.then_inc(tok_t, 1)
                score(2)
                hidden(2)
                score(3)
                hidden(3)
                score(4)
                hidden(4)
                score(5)
                if front:
                    wait(pe, tok_c, at(2))
                    for c in range(NC):
                        last = mm(PS[:, 7, C * c:C * (c + 1)], tok_inT[:, 128 * c:128 * (c + 1)],
                                  zall[:, bass.ds(at(1), 1), :].rearrange("p a n -> p (a n)"))
                    last.then_inc(h_ps, 1)
                hidden(5)
                if attn:
                    outputs_by_token()
                transpose_shift()

                if not attn:
                    projection_in()
                    projection()
                if t == LAST:
                    gates_and_first_expert()
                if ffn:
                    wait(pe, oT_done[1], at(0))
                    if attn:
                        wait(pe, stk_c[5], at(1))
                    else:
                        wait(pe, out_done[1], at(-2))
                    for f in range(NF):
                        wait(pe, gelud[f], at(-1))
                    ffn_out(0, 0, NF)
                    ffn_out(1, 0, 2)
                score_t(0)
                score_t(1)
                if ffn:
                    ffn_out(1, 2, 5)
                    score_t(2)
                if front:
                    wait(pe, q_int, at(2))
                    if attn:
                        wait(pe, shift_c, at(1))
                    else:
                        wait(pe, h_sb, at(2))
                    transpose_ints(7, i_q, q_t)
                if ffn:
                    ffn_out(1, 5, NF).then_inc(f2, 1)
                else:
                    score_t(2)
                score_t(3)
                if front:
                    wait(pe, q_tc, at(2))
                    if ffn:
                        wait(pe, gelud[5], at(-1))
                    elif attn:
                        wait(pe, stk_c[0], at(1))
                    for c in range(NC):
                        for k in range(KC):
                            last = mm(PS[:, QK_BANK[c], 0:2 * C], iT_q[:, k, 128 * c:128 * (c + 1)], wq[:, k, 0:2 * C],
                                      k == 0, k == KC - 1)
                        last.then_inc(qk_ps[c], 1)
                weighted(0)
                score_t(4)
                if attn:
                    projection_in()
                score_t(5)
                if attn:
                    projection()
                weighted(1)
                if front:
                    wait(pe, rest_done[1], at(2))
                    for c in range(NC):
                        for k in range(KC):
                            last = mm(PS[:, 7, C * c:C * (c + 1)], iT_q[:, k, 128 * c:128 * (c + 1)], wq[:, k, 2 * C:3 * C],
                                      k == 0, k == KC - 1)
                    last.then_inc(v_ps, 1)
                weighted(2)
                if front:
                    wait(pe, p3_done[0], at(2))
                    wait(pe, p3_done[1], at(2))
                    wait(pe, dup_done, at(2))
                    for w in range(U):
                        if w == 0:
                            wait(pe, rest_done[0], at(2))
                        elif attn:
                            wait(pe, expd[4 + (w - 1) // 2] if w < 5 else oT_done[1], at(1))
                        for side in range(2):
                            for hh in range(2):
                                for c in range(NC):
                                    col = (4 * side + 2 * hh + c) * 128
                                    last = T.transpose(PSb[0:96, STACK_BANK[w], col:col + 128], stack[:, side, c, 2 * w + hh, :],
                                                       identb[:, :])
                        last.then_inc(stk_t[w], 1)
                if back:
                    wait(pe, xn_done, at(0))
                    if attn:
                        wait(pe, oT_done[G - 1], at(1))
                    for k in range(KC):
                        for c in range(NC):
                            last = T.transpose(PS[0:96, 4, N * k + 128 * c:N * k + 128 * (c + 1)],
                                               xn[:, c, 96 * k:96 * (k + 1)], ident[:, :])
                    last.then_inc(n_t, 1)

            steps(pe, body)

            def bias_rows(e, first, final):
                return mm(PS[0:NCLS * B, 6 + e, 0:C], sel[:, e, :, :].rearrange("p i b -> p (i b)"), ab2_sb[:, :], first, final)

            for a in range(1, NEXP):
                first_layer(a)
            pe.wait_ge(s_const, 3)
            pe.wait_ge(out_done[1], B)
            pe.wait_ge(e_g, 3)
            bias_rows(0, True, False)
            for c in (3, 4):
                for f in range(NF):
                    last = mm(PS[0:NCLS * B, 6, 0:C], hexp[:, c, f, :], aw2_sb[:, c, f, :], False, c == 4 and f == NF - 1)
            last.then_inc(e_h, 1)
            pe.wait_ge(e_g, 5)
            pe.wait_ge(e_gate, 1)
            bias_rows(1, True, False)
            for f in range(NF):
                for c in range(3):
                    last = mm(PS[2 * B * c:2 * B * (c + 1), 7, 0:C], hexp[:, c, f, 2 * B * c:2 * B * (c + 1)], aw2_sb[:, c, f, :],
                              False, f == NF - 1)
            last.then_inc(e_h, 1)


def kernel(**inputs):
    import numpy as np
    import concourse.bacc as bacc
    from concourse.bass_utils import run_bass_kernel_spmd

    a = {k: np.asarray(v) for k, v in inputs.items()}

    def patches(p):
        n = 64 // p
        return a["x"].reshape(B, 3, n, p, n, p).transpose(2, 4, 0, 3, 5, 1).reshape(n * n, B * p * p * 3)

    def chunks(w, rows):
        w = w.reshape(w.shape[:-2] + (w.shape[-2] // rows, rows, w.shape[-1]))
        return np.moveaxis(w, -2, 0)

    ins = {
        "x0": patches(1), "x1": patches(2), "x2": patches(4),
        "idx0": a["L0_tok_idx0"].reshape(NC, 128, GP).transpose(1, 0, 2).reshape(128, NC * GP),
        "idx1": a["L0_tok_idx1"].reshape(T1, 2, 8).transpose(1, 0, 2).reshape(128, 8),
        "idx1_row": a["L0_tok_idx1"].reshape(T1, 2, 8)[:, :, 8 - HOT:].transpose(2, 1, 0).reshape(1, HOT * 128),
        "idx2": a["L0_tok_idx2"].reshape(T2, 8, 2).transpose(1, 0, 2).reshape(128, 2),
        "w0": a["L0_tok_W0"], "w1": a["L0_tok_W1"], "w2": a["L0_tok_W2"],
        "b012": np.stack([a["L0_tok_b0"], a["L0_tok_b1"], a["L0_tok_b2"]], axis=1),
        "wf": chunks(a["L0_tok_Wf"].T, 64), "bf": a["L0_tok_bf"].reshape(1, C),
        "wqkv": chunks(a["L0_attn_w_qkv"].T, 96), "gqkv": a["L0_attn_g_qkv"].reshape(1, C),
        "wproj": chunks(a["L0_attn_w_proj"].T, 96), "gproj": a["L0_attn_g_proj"].reshape(1, C),
        "mw1": chunks(a["L0_ffn_moe0_W1"], 96), "mb1": a["L0_ffn_moe0_b1"].reshape(NF, 128).T,
        "mw2": chunks(a["L0_ffn_moe0_W2"], 128), "mb2": a["L0_ffn_moe0_b2"].reshape(1, C),
        "aw1": chunks(a["L0_ffn_A1_W"], 96), "ab1": a["L0_ffn_A1_b"].reshape(NEXP, NF, 128).transpose(2, 0, 1),
        "aw2": chunks(a["L0_ffn_A2_W"], 128), "ab2": a["L0_ffn_A2_b"],
        "gw": chunks(a["L0_ffn_G_W"].transpose(1, 0, 2).reshape(C, 2 * NCLS), 96),
    }
    nc = bacc.Bacc("TRN2", target_bir_lowering=False, num_devices=1)
    arrays, args = {}, []
    for name, v in ins.items():
        v = np.ascontiguousarray(v)
        arrays[f"in_{name}"] = v
        args.append(nc.dram_tensor(f"in_{name}", v.shape, mybir.dt.from_np(v.dtype), kind="ExternalInput").ap())
    args.append(nc.dram_tensor("out_0", (B, N, C), F32, kind="ExternalOutput").ap())
    vit_tower(nc, *args)
    r = run_bass_kernel_spmd(nc, [arrays], core_ids=[0])
    return r.results[0]["out_0"]
```
